# Optimizing a Trainium2 kernel written in Bass

```python
import numpy as np
import jax
import jax.numpy as jnp

def _softmax(x, axis=-1):
    return jax.nn.softmax(x, axis=axis)
def _gelu(x):
    return jax.nn.gelu(x, approximate=True)
def _silu(x):
    return jax.nn.silu(x)
def _sigmoid(x):
    return jax.nn.sigmoid(x)
def _layernorm(x, axis=-1, eps=1e-5):
    m = jnp.mean(x, axis=axis, keepdims=True)
    v = jnp.var(x, axis=axis, keepdims=True)
    return (x - m) / jnp.sqrt(v + eps)
def _scatter_add(tgt, idx, src, axis=0):
    return tgt.at[idx].add(src)
def _segment_sum(src, seg, n):
    return jax.ops.segment_sum(src, seg, n)

kernel_name = 'mk_adj_ffn_d1_adj_256_29fe9d'

def setup_inputs(seed: int = 0):
    np.random.seed(seed)
    _w = jnp.asarray
    def _rec_inputs():
        import jax
        import jax.numpy as jnp
        _gk = jax.random.key(seed)
        x = -0.0005207 + 1.001 * jax.random.normal(jax.random.fold_in(_gk, 1), (8192, 256), jnp.float32)
        _a = jax.random.bernoulli(jax.random.fold_in(_gk, 2), 0.000488281, (8192, 8192))
        adj = _a.astype(jnp.int32)
        return x, adj
    x, adj = _rec_inputs()
    def _L0_gnn_setup():
        import jax, jax.numpy as jnp
        import numpy as np
        ALPHA = 0.2
        MASK_VAL = -9000000000000000.0
        key = jax.random.key(seed)
        k1, k2, k3, k4 = jax.random.split(key, 4)
        N, Fin, Fout = (8192, 256, 256)
        h = jax.random.normal(k1, (N, Fin), dtype=jnp.float32)
        adj = jax.random.randint(k2, (N, N), 0, 2, dtype=jnp.int32)
        W = jax.random.normal(k3, (Fin, Fout), dtype=jnp.float32) * 0.06
        a = jax.random.normal(k4, (2 * Fout, 1), dtype=jnp.float32) * 0.06
        return {'h': h, 'adj': adj, 'W': W, 'a': a}
    _L0_gnn_all = _L0_gnn_setup()
    _L0_gnn_in = {k: v for k, v in _L0_gnn_all.items() if k in ('W', 'a', )}
    del _L0_gnn_all

    def _L0_ffn_setup():
        import jax, jax.numpy as jnp
        import numpy as np
        B, K, D = (512, 16, 256)
        E = 32
        H = int(D * 0.25)
        key = jax.random.key(seed)
        ks = jax.random.split(key, 7)
        d_rs = D ** (-0.5)
        h_rs = H ** (-0.5)
        x = jax.random.normal(ks[0], (B, K, D), dtype=jnp.float32)
        router_w = jax.random.uniform(ks[1], (E, D), jnp.float32, -d_rs, d_rs)
        router_b = jax.random.uniform(ks[2], (E,), jnp.float32, -d_rs, d_rs)
        W1 = jax.random.uniform(ks[3], (E, D, H), jnp.float32, -h_rs, h_rs)
        b1 = jax.random.uniform(ks[4], (E, H), jnp.float32, -h_rs, h_rs)
        W2 = jax.random.uniform(ks[5], (E, H, D), jnp.float32, -d_rs, d_rs)
        b2 = jax.random.uniform(ks[6], (E, D), jnp.float32, -d_rs, d_rs)
        return {'x': x, 'router_w': router_w, 'router_b': router_b, 'W1': W1, 'b1': b1, 'W2': W2, 'b2': b2}
    _L0_ffn_all = _L0_ffn_setup()
    _L0_ffn_in = {k: v for k, v in _L0_ffn_all.items() if k in ('router_w', 'router_b', 'W1', 'b1', 'W2', 'b2', )}
    del _L0_ffn_all

    return {
        "x": x,
        "adj": adj,
        "L0_gnn_W": _L0_gnn_in["W"],
        "L0_gnn_a": _L0_gnn_in["a"],
        "L0_ffn_router_w": _L0_ffn_in["router_w"],
        "L0_ffn_router_b": _L0_ffn_in["router_b"],
        "L0_ffn_W1": _L0_ffn_in["W1"],
        "L0_ffn_b1": _L0_ffn_in["b1"],
        "L0_ffn_W2": _L0_ffn_in["W2"],
        "L0_ffn_b2": _L0_ffn_in["b2"],
    }

def reference(x, adj, L0_gnn_W, L0_gnn_a, L0_ffn_router_w, L0_ffn_router_b, L0_ffn_W1, L0_ffn_b1, L0_ffn_W2, L0_ffn_b2):
    import jax
    import jax.numpy as jnp
    def _L0_gnn_ref(h, adj, W, a):
        import jax, jax.numpy as jnp
        import numpy as np
        ALPHA = 0.2
        MASK_VAL = -9000000000000000.0
        Fout = W.shape[1]
        Wh = h @ W
        a1, a2 = (a[:Fout, 0], a[Fout:, 0])
        e = (Wh @ a1)[:, None] + (Wh @ a2)[None, :]
        e = jnp.where(e > 0, e, ALPHA * e)
        e = jnp.where(adj > 0, e, MASK_VAL)
        attention = jax.nn.softmax(e, axis=1)
        h_prime = attention @ Wh
        return jax.nn.elu(h_prime)

    def _L0_ffn_ref(x, router_w, router_b, W1, b1, W2, b2):
        import jax, jax.numpy as jnp
        import numpy as np
        B, K, D = (512, 16, 256)
        E = 32
        H = int(D * 0.25)
        xf = x.reshape(-1, D)
        logits = xf @ router_w.T + router_b
        idx = jnp.argmax(logits, axis=-1)
        w1t = jnp.take(W1, idx, axis=0)
        h = jnp.einsum('nd,ndh->nh', xf, w1t) + jnp.take(b1, idx, axis=0)
        h = jax.nn.relu(h)
        w2t = jnp.take(W2, idx, axis=0)
        out = jnp.einsum('nh,nhd->nd', h, w2t) + jnp.take(b2, idx, axis=0)
        out = jax.nn.relu(out)
        return out.reshape(x.shape)

    x = x + _L0_gnn_ref(_layernorm(x, axis=-1), adj, L0_gnn_W, L0_gnn_a)
    x = x + _L0_ffn_ref((_layernorm(x, axis=-1))[None], L0_ffn_router_w, L0_ffn_router_b, L0_ffn_W1, L0_ffn_b1, L0_ffn_W2, L0_ffn_b2)[0]
    return x


_drawn_inputs = setup_inputs


def setup_inputs(seed=0):
    import zlib

    import numpy as np

    out = dict(_drawn_inputs(seed))
    spreads = {}
    factors = {'L0_ffn_b1': 6.415}
    for name, (base, spread) in spreads.items():
        noise = np.random.default_rng([zlib.crc32(name.encode()), seed]).standard_normal(out[name].shape)
        drawn = base * np.exp(spread * noise) if base else spread * noise
        out[name] = jnp.asarray(drawn.astype(out[name].dtype))
    for name, factor in factors.items():
        out[name] = (out[name] * factor).astype(out[name].dtype)
    return out
```

```python
import concourse.bass as bass
from concourse import mybir
from contextlib import ExitStack

P = 128
D = 256
DH = D // P
E = 32
H = 64
ROW = 264
Q = 4
TOP = 8
K = 16
KEPT = 4
GROUP = 8
EPS = 1e-5
ALPHA = 0.2
MASK_VAL = -9000000000000000.0
NO_TOKEN = 1.0e6


def gat_moe(nc, x, adj, gW, ga, rw, rb, W1, b1, W2, b2, out, table, region):
    f32, i32, u32 = mybir.dt.float32, mybir.dt.int32, mybir.dt.uint32
    bf16, f8 = mybir.dt.bfloat16, mybir.dt.float8e4
    ALU, ACT, AX = mybir.AluOpType, mybir.ActivationFunctionType, mybir.AxisListType

    N = x.shape[0]
    NS = N // P
    LAG = NS // GROUP
    C = N // Q
    WORDS = C // KEPT
    CAND = Q * TOP * KEPT
    SPAN = N + 2 * P
    BLOCKS = NS + E - 1
    NULL_ROW = E // 2 * SPAN
    assert LAG % 2 == 0 and NS % (2 * GROUP) == 0 and BLOCKS <= P

    ctx = ExitStack()
    with ctx:
        def sb(name, shape, dt=f32):
            return ctx.enter_context(nc.sbuf_tensor(name, shape, dt))

        def ps(name, shape, dt=f32):
            return ctx.enter_context(nc.psum_tensor(name, shape, dt))

        def sem(name):
            return ctx.enter_context(nc.semaphore(name))

        ident = sb("ident", [P, P])
        ones_f = sb("ones_f", [P, P])
        ones_b = sb("ones_b", [P, P], bf16)
        before = sb("before", [P, P], bf16)
        byte_sign = sb("byte_sign", [P, Q * TOP, KEPT], i32)
        code_base = sb("code_base", [P, Q, TOP, KEPT])
        expert_no = sb("expert_no", [P, E])
        region_base = sb("region_base", [P, E])
        direction = sb("direction", [P, E])
        first_block = sb("first_block", [P, E])
        pad_shift = sb("pad_shift", [P, E])
        token_no = sb("token_no", [P, NS])
        minus_half = sb("minus_half", [P, GROUP])
        part_no = sb("part_no", [P, 1])
        pad_row = sb("pad_row", [P, ROW])
        zero_col = sb("zero_col", [P, 1])

        w_aug = sb("w_aug", [P, DH, D + 2])
        w_raw = sb("w_raw", [P, DH, D])
        w_t = sb("w_t", [P, DH, D])
        a_sb = sb("a_sb", [P, DH, 2])
        rw_sb = sb("rw_sb", [E, D])
        rw_t = sb("rw_t", [P, DH, E])
        rb_sb = sb("rb_sb", [1, E])
        w1_sb = sb("w1_sb", [P, E, DH, H])
        b1_sb = sb("b1_sb", [1, E, H])
        w2_sb = sb("w2_sb", [H + 1, E, D])

        w1_flat = w1_sb[:, :, :, :].rearrange("p e h n -> p (e h n)")
        xg = [w1_flat[:, i * GROUP * D:(i + 1) * GROUP * D].rearrange("p (r d) -> p r d", r=GROUP) for i in range(2)]
        st = sb("st", [P, GROUP, 6])
        mv = sb("mv", [P, GROUP, 2])
        ve = sb("ve", [P, GROUP])
        rs = sb("rs", [P, GROUP])
        xn = [sb(f"xn{i}", [P, D]) for i in range(2)]
        xT = [sb(f"xT{i}", [P, DH, P]) for i in range(2)]
        xsum = sb("xsum", [P, DH, NS])
        xmean = sb("xmean", [P, DH])
        whr = [sb(f"whr{i}", [P, ROW]) for i in range(2)]
        s1 = sb("s1", [P, NS])
        s2 = sb("s2", [P, NS])

        raw_all = sb("raw_all", [P, Q * C], i32)
        raw = [raw_all[:, q * C:(q + 1) * C] for q in range(Q)]
        sg = [[sb(f"sg{i}{q}", [P, C], f8) for q in range(Q)] for i in range(2)]
        top_word = sb("top_word", [P, Q, TOP])
        top_pos = sb("top_pos", [P, Q, TOP], u32)
        bits = sb("bits", [P, Q * TOP, KEPT], i32)
        code = sb("code", [P, CAND])
        key = sb("key", [P, CAND])
        key2 = sb("key2", [P, CAND])
        key16 = sb("key16", [P, K])
        keys = sb("keys", [P, NS, K])
        most_words = sb("most_words", [P, Q])

        idx = [sb(f"idx{i}", [P, K], u32) for i in range(2)]
        G = [sb(f"G{i}", [P, K, ROW]) for i in range(2)]
        sc = sb("sc", [P, K])
        lr = sb("lr", [P, K])
        pen = sb("pen", [P, K])
        ee = sb("ee", [P, K])
        mx = sb("mx", [P, 1])
        nmx = sb("nmx", [P, 1])
        pr = sb("pr", [P, K])
        den = sb("den", [P, 1])
        rden = [sb(f"rden{i}", [P, 1]) for i in range(2)]
        diag = sb("diag", [P, K, P])

        xr = [sb(f"xr{i}", [P, D]) for i in range(2)]
        hh = sb("hh", [P, D])
        um = sb("um", [P, D])
        ex = sb("ex", [P, D])
        el = sb("el", [P, D])
        st2 = sb("st2", [P, 6])
        ve2 = sb("ve2", [P, 1])
        x1 = [sb(f"x1{i}", [P, ROW]) for i in range(2)]
        xn2 = sb("xn2", [P, D])
        xT2 = sb("xT2", [P, DH, P])
        lg = sb("lg", [P, E])
        lmax = sb("lmax", [P, TOP])
        lidx = sb("lidx", [P, TOP], u32)
        ef = sb("ef", [P, 1])
        oh = sb("oh", [P, E], bf16)
        count = sb("count", [P, E])
        c2 = sb("c2", [P, E])
        c3 = sb("c3", [P, E])
        posf = sb("posf", [P, 1])
        posu = [sb(f"posu{i}", [P, 1], u32) for i in range(2)]

        nbi = sb("nbi", [P, E], i32)
        nbj = sb("nbj", [P, E], i32)
        nbf = sb("nbf", [P, E])
        cum = [sb(f"cum{i}", [P, E]) for i in range(2)]
        le = sb("le", [P, E])
        le2 = sb("le2", [P, E])
        plan = sb("plan", [P, 8])
        plan_i = sb("plan_i", [1, 3 * P], i32)

        scores = raw_all[:, :].bitcast(f32)
        adj_block = sb("adj_block", [P, P], i32)
        dsum = sb("dsum", [P, NS])
        dacc = sb("dacc", [P, D])
        flagc = sb("flagc", [P, 2])
        flag_i = sb("flag_i", [1, 2], i32)

        xb = [sb(f"xb{i}", [P, ROW]) for i in range(2)]
        xnb = sb("xnb", [P, D])
        xTb = [sb(f"xTb{i}", [P, DH, P]) for i in range(2)]
        hb = [sb(f"hb{i}", [P, H + 1]) for i in range(2)]
        hT = [sb(f"hT{i}", [H + 1, P]) for i in range(2)]
        yb = [sb(f"yb{i}", [P, D]) for i in range(2)]
        tok = [sb(f"tok{i}", [P, 1], u32) for i in range(2)]

        psP = ps("psP", [P, 512])
        psW = [ps(f"psW{i}", [P, 512]) for i in range(2)]
        psO = [ps(f"psO{i}", [P, 512]) for i in range(2)]
        psT = ps("psT", [P, 512])
        psL = ps("psL", [P, 512])
        psC = ps("psC", [P, 512])

        const_in = sem("const_in")
        ffn_in = sem("ffn_in")
        consts = sem("consts")
        v_const = sem("v_const")
        pe_w = sem("pe_w")
        v_w = sem("v_w")
        xg_in = [sem(f"xg_in{i}") for i in range(2)]
        v_st = sem("v_st")
        v_group = sem("v_group")
        pl_rs = sem("pl_rs")
        v_xn = sem("v_xn")
        pe_xT = sem("pe_xT")
        a_xT = sem("a_xT")
        pe_wh = sem("pe_wh")
        v_wh = sem("v_wh")
        tab_out = [sem(f"tab_out{i}") for i in range(2)]
        mean_out = sem("mean_out")

        raw_in = [sem(f"raw_in{q}") for q in range(Q)]
        a_sg = sem("a_sg")
        v_top = sem("v_top")
        v_find = sem("v_find")
        v_dec = sem("v_dec")
        v_idx = sem("v_idx")
        gat = [sem(f"gat{i}") for i in range(2)]
        v_sm = sem("v_sm")
        a_p = sem("a_p")
        v_diag = sem("v_diag")
        pe_o = sem("pe_o")
        a_h = sem("a_h")
        v_post = sem("v_post")
        a_ex = sem("a_ex")
        pl_rs2 = sem("pl_rs2")
        pe_t2 = sem("pe_t2")
        a_x2 = sem("a_x2")
        pe_lg = sem("pe_lg")
        pe_cum = sem("pe_cum")
        xr_in = [sem(f"xr_in{i}") for i in range(2)]
        sc_out = [sem(f"sc_out{i}") for i in range(2)]

        v_flag = sem("v_flag")
        pe_flag = sem("pe_flag")
        d_in = sem("d_in")
        d_wh = sem("d_wh")
        d_v = sem("d_v")
        d_pe = sem("d_pe")
        d_a = sem("d_a")

        v_plan = sem("v_plan")
        pe_plan = sem("pe_plan")
        pad_out = sem("pad_out")
        xb_in = [sem(f"xb_in{i}") for i in range(2)]
        v_xb = sem("v_xb")
        pe_xb = sem("pe_xb")
        a_xb = sem("a_xb")
        pe_h = sem("pe_h")
        v_h = sem("v_h")
        pe_hT = sem("pe_hT")
        a_hT = sem("a_hT")
        pe_y = sem("pe_y")
        v_y = sem("v_y")
        y_out = [sem(f"y_out{i}") for i in range(2)]

        VP = 17
        CR = 2 * VP
        VD = 8
        VS = 6
        NONE_WORD = -float(_word_of_signs(0xB8B8B8B8))

        def segments():
            yield "first", 0, 2
            if NS - LAG > 2:
                yield "steady", 2, NS - LAG
            if NS - 2 > NS - LAG:
                yield "drain", NS - LAG, NS - 2
            yield "last", NS - 2, NS

        def rounds(eng, step):
            for kind, lo, hi in segments():
                searching = kind in ("first", "steady") and NS > LAG
                if hi - lo == 2:
                    for par in range(2):
                        u = lo + par
                        step(u, par, u + LAG < NS and searching, u >= 2, u + 1 < NS)
                else:
                    with eng.Fori(lo // 2, hi // 2) as i:
                        for par in range(2):
                            step(i * 2 + par, par, searching, True, True)

        def dense_strips(eng, step):
            with eng.Fori(0, NS // 2) as i:
                for par in range(2):
                    step(i * 2 + par, par)

        DV_A = 7
        DV_STRIP = NS * DV_A + 2 + NS * 2 + 1
        PLAN_ROWS = 28
        PLAN_STEPS = PLAN_ROWS + 3
        BPAIRS = BLOCKS // 2

        def blocks_loop(eng, step):
            step(0, 0)
            step(1, 1)
            with eng.Fori(1, BPAIRS) as i:
                for par in range(2):
                    step(i * 2 + par, par)
            if BLOCKS % 2:
                step(BLOCKS - 1, 0)

        block = ctx.enter_context(nc.Block())

        @block.sync
        def _(sp):
            sp.dma_start(w_raw[:, :, :], gW.rearrange("(h p) n -> p h n", p=P)).then_inc(const_in, 16)
            with nc.allow_non_contiguous_dma(reason="two small vectors"):
                sp.dma_start(a_sb[:, :, 0:1], ga[D:2 * D, :].rearrange("(h p) o -> p h o", p=P)).then_inc(const_in, 16)
                sp.dma_start(a_sb[:, :, 1:2], ga[0:D, :].rearrange("(h p) o -> p h o", p=P)).then_inc(const_in, 16)
            sp.dma_start(rw_sb[:, :], rw[:, :]).then_inc(const_in, 16)
            sp.dma_start(rb_sb[:, :], rb.rearrange("(o n) -> o n", o=1)).then_inc(const_in, 16)

            def load_group(g, par, i):
                sp.wait_ge(v_group, 2 * g + 1)
                sp.nop(nofuse=True)
                sp.dma_start(xg[par][:, :, :],
                             x[bass.ds(g * GROUP * P, GROUP * P), :].rearrange("(r p) d -> p r d", p=P)
                             ).then_inc(xg_in[par], 16)

            def load_strip(t):
                for q in range(Q):
                    sp.wait_ge(a_sg, t * Q + q + 1)
                    sp.nop(nofuse=True)
                    sp.dma_start(raw[q], adj[bass.ds(t * P, P), q * C:(q + 1) * C]).then_inc(raw_in[q], 16)

            def load_x(v, par):
                sp.wait_ge(v_post, v * VP + 3)
                sp.nop(nofuse=True)
                sp.dma_start(xr[par][:, :], x[bass.ds(v * P, P), :]).then_inc(xr_in[par], 16)

            with sp.Fori(0, LAG // 2) as i:
                for par in range(2):
                    load_group(i * 2 + par, par, i)
                    load_strip(i * 2 + par)

            def step(u, par, searching, post, more):
                if searching:
                    load_strip(u + LAG)
                load_x(u, par)
            rounds(sp, step)

            sp.wait_ge(v_group, 2 * LAG + 3)
            sp.nop(nofuse=True)
            sp.dma_start(w1_sb[:, :, :, :].rearrange("p e h n -> p (e h) n"),
                         W1.rearrange("e (h p) n -> p (e h) n", p=P)).then_inc(ffn_in, 16)
            sp.dma_start(w2_sb[0:H, :, :], W2.rearrange("e k n -> k e n")).then_inc(ffn_in, 16)
            sp.dma_start(w2_sb[H:H + 1, :, :], b2.rearrange("(o e) n -> o e n", o=1)).then_inc(ffn_in, 16)
            sp.dma_start(b1_sb[:, :, :], b1.rearrange("(o e) n -> o e n", o=1)).then_inc(ffn_in, 16)

            sp.wait_ge(v_flag, 5)
            sp.nop(nofuse=True)
            flag = sp.value_load(flag_i[0:1, 0:1], min_val=0, max_val=4 * P)
            with sp.If(flag > 0):
                def dense(t, par):
                    with sp.Fori(0, NS) as b:
                        sp.wait_ge(d_v, t * DV_STRIP + b * DV_A + 1)
                        sp.nop(nofuse=True)
                        sp.dma_start(adj_block[:, :], adj[bass.ds(t * P, P), bass.ds(b * P, P)]).then_inc(d_in, 16)
                        sp.wait_ge(d_in, (t * NS + b) * 16 + 16)
                        sp.nop(nofuse=True)
                    with sp.Fori(0, NS) as b:
                        sp.wait_ge(d_v, t * DV_STRIP + NS * DV_A + 2 + b * 2 + 1)
                        sp.nop(nofuse=True)
                        sp.dma_start(G[0][:, 0, :], table[bass.ds(b * P, P), :]).then_inc(d_wh, 16)
                        sp.wait_ge(d_wh, (t * NS + b) * 16 + 16)
                        sp.nop(nofuse=True)
                    sp.wait_ge(v_post, (t + NS) * VP + 3)
                    sp.nop(nofuse=True)
                    sp.dma_start(xr[par][:, :], x[bass.ds(t * P, P), :]).then_inc(xr_in[par], 16)
                dense_strips(sp, dense)
                sp.wait_ge(sc_out[0], 16 + 16 * NS)
                sp.nop(nofuse=True)
                sp.wait_ge(sc_out[1], 16 + 16 * NS)
                sp.nop(nofuse=True)

            sp.wait_ge(v_plan, PLAN_STEPS)
            sp.nop(nofuse=True)
            with sp.Fori(0, E) as e:
                row = sp.value_load(plan_i[0:1, bass.ds(e + 2 * P, 1)], min_val=0, max_val=NULL_ROW)
                sp.dma_start(region[bass.ds(row, P), :], pad_row[:, :]).then_inc(pad_out, 16)
            sp.wait_ge(pad_out, 16 * E)
            sp.nop(nofuse=True)
            sp.wait_ge(sc_out[0], 16 + 8 * NS)
            sp.nop(nofuse=True)
            sp.wait_ge(sc_out[1], 16 + 8 * NS)
            sp.nop(nofuse=True)

            def load_block(b, par):
                row = sp.value_load(plan_i[0:1, bass.ds(b, 1)], min_val=0, max_val=NULL_ROW)
                sp.wait_ge(v_y, 2 * b + 2)
                sp.nop(nofuse=True)
                sp.dma_start(xb[par][:, :], region[bass.ds(row, P), :]).then_inc(xb_in[par], 16)
            blocks_loop(sp, load_block)

        @block.gpsimd
        def _(pool):
            pool.memset(ones_f[:, :], 1.0).then_inc(consts, 1)
            pool.memset(ones_b[:, :], 1.0).then_inc(consts, 1)
            pool.memset(ident[:, :], 0.0).then_inc(consts, 1)
            pool.memset(minus_half[:, :], -0.5).then_inc(consts, 1)
            pool.wait_ge(consts, 4)
            pool.nop(nofuse=True)
            pool.affine_select(out=ident[:, :], in_=ident[:, :], compare_op=ALU.not_equal, fill=1.0, base=0,
                               pattern=[[-1, P]], channel_multiplier=1).then_inc(consts, 1)
            pool.affine_select(out=before[:, :], in_=ones_b[:, :], compare_op=ALU.is_gt, fill=0.0, base=0,
                               pattern=[[1, P]], channel_multiplier=-1).then_inc(consts, 1)
            pool.iota(code_base[:, :, :, :], [[-C, Q], [0, TOP], [-1, KEPT]], base=N, channel_multiplier=0,
                      allow_small_or_imprecise_dtypes=True).then_inc(consts, 1)
            pool.iota(expert_no[:, :], [[1, E]], base=0, channel_multiplier=0,
                      allow_small_or_imprecise_dtypes=True).then_inc(consts, 1)
            for tile, at, step_odd in ((region_base, 0, SPAN - 1), (direction, 1, -2),
                                       (first_block, 0, SPAN - P), (pad_shift, 0, 1 - P)):
                by_pair = SPAN if tile in (region_base, first_block) else 0
                pool.iota(tile[:, :], [[by_pair, E // 2], [step_odd, 2]], base=at, channel_multiplier=0,
                          allow_small_or_imprecise_dtypes=True).then_inc(consts, 1)
            pool.iota(token_no[:, :], [[P, NS]], base=0, channel_multiplier=1,
                      allow_small_or_imprecise_dtypes=True).then_inc(consts, 1)
            pool.iota(part_no[:, :], [[0, 1]], base=0, channel_multiplier=1,
                      allow_small_or_imprecise_dtypes=True).then_inc(consts, 1)
            pool.wait_ge(v_const, 7)
            pool.nop(nofuse=True)
            for par in range(2):
                half_block = NULL_ROW + par * (P // 2)
                pool.dma_start(region[half_block:half_block + P // 2, :], pad_row[0:P // 2, :]).then_inc(sc_out[par], 16)
                pool.dma_start(table[N:N + 1, par * (ROW // 2):(par + 1) * (ROW // 2)],
                               pad_row[0:1, 0:ROW // 2]).then_inc(tab_out[par], 16)
            last_row = pool.to_reg(N - 1)
            mean_row = pool.to_reg(N)
            last_region_row = pool.to_reg(NULL_ROW - 1)

            def group(g, par):
                pool.wait_ge(v_group, 2 * g + 1 + 3)
                pool.nop(nofuse=True)
                pool.tensor_tensor(rs[:, :], ve[:, :], minus_half[:, :], ALU.pow).then_inc(pl_rs, 1)
                for r in range(GROUP):
                    pool.wait_ge(v_wh, 2 * (g * GROUP + r) + 6)
                    pool.nop(nofuse=True)
                    pool.dma_start(table[bass.ds((g * GROUP + r) * P, P), :], whr[r % 2][:, :]
                                   ).then_inc(tab_out[r % 2], 16)
            with pool.Fori(0, LAG // 2) as i:
                for par in range(2):
                    group(i * 2 + par, par)
            pool.wait_ge(v_wh, 2 * NS + 4 + 1)
            pool.nop(nofuse=True)
            pool.dma_start(table[N:N + 1, :], whr[0][0:1, :]).then_inc(mean_out, 16)
            pool.wait_ge(tab_out[0], 16 + 8 * NS)
            pool.nop(nofuse=True)
            pool.wait_ge(tab_out[1], 16 + 8 * NS)
            pool.nop(nofuse=True)
            pool.wait_ge(mean_out, 16)
            pool.nop(nofuse=True)

            def gather(u, par, k0, k1):
                for k in range(k0, k1):
                    pool.indirect_dma_start(
                        out=G[par][:, k, :], out_offset=None, in_=table[:, :],
                        in_offset=bass.IndirectOffsetOnAxis(ap=idx[par][:, k:k + 1], axis=0),
                        bounds_check=mean_row if k == 0 else last_row, oob_is_err=False).then_inc(gat[par], 16)

            def gather_waits(u, par):
                pool.wait_ge(v_idx, u + 1)
                pool.nop(nofuse=True)
                pool.wait_ge(pe_o, u + 1)
                pool.nop(nofuse=True)

            def inverse_std(w, par):
                pool.wait_ge(v_post, w * VP + CR + 6)
                pool.nop(nofuse=True)
                pool.tensor_tensor(x1[par][:, D + 1:D + 2], ve2[:, :], minus_half[:, 0:1], ALU.pow).then_inc(pl_rs2, 1)

            def scatter(w, par):
                pool.wait_ge(v_post, w * VP + CR + VP)
                pool.nop(nofuse=True)
                pool.indirect_dma_start(
                    out=region[:, :], out_offset=bass.IndirectOffsetOnAxis(ap=posu[par][:, 0:1], axis=0),
                    in_=x1[par][:, :], in_offset=None, bounds_check=last_region_row, oob_is_err=False
                ).then_inc(sc_out[par], 16)

            gather_waits(0, 0)
            gather(0, 0, 0, K)

            def step(u, par, searching, post, more):
                if more:
                    gather_waits(u + 1, 1 - par)
                    gather(u + 1, 1 - par, 0, 4)
                if post:
                    inverse_std(u - 2, par)
                if more:
                    gather(u + 1, 1 - par, 4, 12)
                if post:
                    scatter(u - 2, par)
                if more:
                    gather(u + 1, 1 - par, 12, K)
            rounds(pool, step)
            for par in range(2):
                inverse_std(NS - 2 + par, par)
                scatter(NS - 2 + par, par)

            pool.wait_ge(v_flag, 5)
            pool.nop(nofuse=True)
            flag = pool.value_load(flag_i[0:1, 0:1], min_val=0, max_val=4 * P)
            with pool.If(flag > 0):
                def dense(t, par):
                    inverse_std(t + NS, par)
                    scatter(t + NS, par)
                dense_strips(pool, dense)

            def store_block(b, par):
                pool.wait_ge(v_y, 2 * b + 2 + 4)
                pool.nop(nofuse=True)
                pool.indirect_dma_start(
                    out=out[:, :], out_offset=bass.IndirectOffsetOnAxis(ap=tok[par][:, 0:1], axis=0),
                    in_=yb[par][:, :], in_offset=None, bounds_check=last_row, oob_is_err=False
                ).then_inc(y_out[par], 16)
            blocks_loop(pool, store_block)
            pool.wait_ge(y_out[0], 16 * ((BLOCKS + 1) // 2))
            pool.nop(nofuse=True)
            pool.wait_ge(y_out[1], 16 * (BLOCKS // 2))
            pool.nop(nofuse=True)

        @block.scalar
        def _(act):
            act.sem_inc(a_xT, 2)
            act.sem_inc(a_sg, Q)
            act.sem_inc(a_h, 2)
            act.sem_inc(a_x2, 1)
            act.sem_inc(a_xb, 1)
            act.wait_ge(v_const, 7)

            def transposes(s, r):
                act.wait_ge(pe_xT, s + 1 + 2)
                act.wait_ge(pe_wh, s + 1)
                act.nop(nofuse=True)
                for h in range(DH):
                    act.activation(xT[r % 2][:, h, :], psP[:, h * P:(h + 1) * P], ACT.Copy,
                                   accum_out=xsum[:, h, bass.ds(s, 1)]).then_inc(a_xT, 1)

            def signs(t, par, q):
                act.wait_ge(raw_in[q], t * 16 + 16)
                act.wait_ge(v_find, t * Q + q + 1)
                act.nop(nofuse=True)
                act.activation(sg[par][q][:, :], raw[q], ACT.Sign, bias=minus_half[:, 0:1],
                               saturate=False).then_inc(a_sg, 1)

            with act.Fori(0, LAG // 2) as i:
                for par in range(2):
                    for r in range(GROUP):
                        transposes((i * 2 + par) * GROUP + r, r)
                        if r % 2:
                            signs(i * 2 + par, par, r // 2)

            def attention_sum(w, par):
                act.wait_ge(pe_o, w + 3)
                act.wait_ge(v_post, w * VP + CR)
                act.activation(hh[:, :], psO[par][:, 0:D], ACT.Copy, scale=rden[par][:, 0:1]).then_inc(a_h, 1)

            def elu_exp(w):
                act.wait_ge(v_post, w * VP + CR + 1)
                act.activation(ex[:, :], um[:, :], ACT.Exp).then_inc(a_ex, 1)

            def transposes2(w):
                act.wait_ge(pe_t2, w + 1)
                act.wait_ge(pe_lg, w + 1)
                act.activation(xT2[:, :, :].rearrange("p h n -> p (h n)"), psT[:, 0:D], ACT.Copy).then_inc(a_x2, 1)

            def softmax_exp(u):
                act.wait_ge(v_sm, u * VS + VS)
                act.activation(pr[:, :], ee[:, :], ACT.Exp, bias=nmx[:, 0:1], accum_out=den[:, 0:1]).then_inc(a_p, 1)

            def step(u, par, searching, post, more):
                if searching:
                    signs(u + LAG, par, 0)
                if post:
                    attention_sum(u - 2, par)
                if searching:
                    signs(u + LAG, par, 1)
                if post:
                    elu_exp(u - 2)
                if searching:
                    signs(u + LAG, par, 2)
                    signs(u + LAG, par, 3)
                if post:
                    transposes2(u - 2)
                softmax_exp(u)
            rounds(act, step)
            for par in range(2):
                attention_sum(NS - 2 + par, par)
                elu_exp(NS - 2 + par)
                transposes2(NS - 2 + par)

            act.wait_ge(v_flag, 5)
            flag = act.value_load(flag_i[0:1, 0:1], min_val=0, max_val=4 * P)
            with act.If(flag > 0):
                def dense(t, par):
                    with act.Fori(0, NS) as b:
                        act.wait_ge(d_v, t * DV_STRIP + NS * DV_A + 2 + b * 2 + 1)
                        act.activation(diag[:, 1, :], scores[:, bass.ds(b * P, P)], ACT.Exp, bias=nmx[:, 0:1],
                                       accum_out=dsum[:, bass.ds(b, 1)]).then_inc(d_a, 1)
                    act.wait_ge(d_v, (t + 1) * DV_STRIP + 1)
                    act.wait_ge(v_post, (t + NS) * VP + CR)
                    act.activation(hh[:, :], dacc[:, :], ACT.Copy, scale=rden[0][:, 0:1]).then_inc(a_h, 1)
                    elu_exp(t + NS)
                    transposes2(t + NS)
                dense_strips(act, dense)

            def block_step(b, par):
                act.wait_ge(pe_xb, b + 1)
                act.activation(xTb[par][:, :, :].rearrange("p h n -> p (h n)"), psP[:, 0:D], ACT.Copy).then_inc(a_xb, 1)
                act.wait_ge(pe_hT, b + 1)
                act.activation(hT[par][:, :], psT[0:H + 1, 0:P], ACT.Copy).then_inc(a_hT, 1)
            blocks_loop(act, block_step)


        @block.vector
        def _(v):
            v.sem_inc(v_wh, 4)
            v.sem_inc(v_group, 3)
            v.sem_inc(v_find, 2 * Q)
            v.sem_inc(v_post, CR)
            v.sem_inc(v_y, 4)
            for r in range(KEPT):
                v.memset(byte_sign[:, :, r], _int32(0x80 << (8 * r))).then_inc(v_const, 1)
            v.memset(most_words[:, :], NONE_WORD).then_inc(v_const, 1)
            v.memset(pad_row[:, 0:D + 2], 0.0)
            v.memset(pad_row[:, D + 2:ROW], NO_TOKEN)
            v.memset(pen[:, :], 0.0)
            for par in range(2):
                v.memset(G[par][:, :, :], 0.0)
                v.memset(whr[par][:, :], 0.0)
                v.memset(x1[par][:, :], 0.0)
                v.memset(hb[par][:, :], 1.0)
            v.memset(zero_col[:, :], 0.0).then_inc(v_const, 1)
            v.wait_ge(consts, 14)
            v.tensor_copy(count[:, :], region_base[:, :]).then_inc(v_const, 1)

            for h in range(DH):
                v.wait_ge(pe_w, h + 1)
                v.tensor_copy(w_t[:, h, :], psT[:, 0:D]).then_inc(v_w, 1)
            for h in range(DH):
                v.tensor_copy(w_aug[:, h, 0:D], w_raw[:, h, :]).then_inc(v_w, 1)
            for h in range(DH):
                v.wait_ge(pe_w, DH + 1)
                v.tensor_copy(w_aug[:, h, D:D + 2], psL[:, 2 * h:2 * h + 2]).then_inc(v_w, 1)
            v.wait_ge(pe_w, DH + 2)
            v.tensor_copy(rw_t[:, :, :], psC[:, 0:DH * E].rearrange("p (h e) -> p h e", h=DH)).then_inc(v_w, 1)

            def search(t, par, q):
                v.wait_ge(a_sg, t * Q + q + 1 + Q)
                v.nop(nofuse=True)
                words = sg[par][q][:, :].bitcast(f32)
                v.max(top_word[:, q, :], words).then_inc(v_top, 1)
                v.wait_ge(v_top, t * Q + q + 1)
                v.nop(nofuse=True)
                v.max_index(top_pos[:, q, :], top_word[:, q, :], words).then_inc(v_find, 1)

            def decode(t):
                at = t * VD
                v.wait_ge(v_find, t * Q + Q + 2 * Q)
                v.tensor_tensor(bits[:, :, :],
                                top_word[:, :, :].rearrange("p q n -> p (q n)").bitcast(i32).unsqueeze(2).to_broadcast([P, Q * TOP, KEPT]),
                                byte_sign[:, :, :], ALU.bitwise_and).then_inc(v_dec, 1)
                v.scalar_tensor_tensor(out=code[:, :].rearrange("p (n r) -> p n r", r=KEPT),
                                       in0=top_pos[:, :, :].rearrange("p q n -> p (q n)").unsqueeze(2).to_broadcast([P, Q * TOP, KEPT]),
                                       scalar=-float(KEPT),
                                       in1=code_base[:, :, :, :].rearrange("p q n r -> p (q n) r"),
                                       op0=ALU.mult, op1=ALU.add).then_inc(v_dec, 1)
                v.tensor_tensor(most_words[:, :], most_words[:, :], top_word[:, :, TOP - 1], ALU.max).then_inc(v_dec, 1)
                v.wait_ge(v_dec, at + 3)
                v.scalar_tensor_tensor(out=key[:, :], in0=bits[:, :, :].rearrange("p n r -> p (n r)"), scalar=0.0,
                                       in1=code[:, :], op0=ALU.is_equal, op1=ALU.mult).then_inc(v_dec, 1)
                v.wait_ge(v_dec, at + 4)
                v.nop(nofuse=True)
                v.max(key16[:, 0:TOP], key[:, :]).then_inc(v_dec, 1)
                v.wait_ge(v_dec, at + 5)
                v.nop(nofuse=True)
                v.match_replace(key2[:, :], key16[:, 0:TOP], key[:, :], 0.0).then_inc(v_dec, 1)
                v.wait_ge(v_dec, at + 6)
                v.nop(nofuse=True)
                v.max(key16[:, TOP:K], key2[:, :]).then_inc(v_dec, 1)
                v.wait_ge(v_dec, at + 7)
                v.tensor_copy(keys[:, bass.ds(t, 1), :], key16[:, :].unsqueeze(1)).then_inc(v_dec, 1)

            def group_stats(g, par, i):
                v.wait_ge(xg_in[par], i * 16 + 16)
                v.nop(nofuse=True)
                for r in range(GROUP):
                    v.bn_stats(st[:, r, :], xg[par][:, r, :]).then_inc(v_st, 1)
                v.wait_ge(v_st, g * 2 * GROUP + GROUP)
                v.nop(nofuse=True)
                for r in range(GROUP):
                    v.bn_aggr(mv[:, r, :], st[:, r, :]).then_inc(v_st, 1)
                v.wait_ge(v_st, g * 2 * GROUP + 2 * GROUP)
                v.tensor_scalar(ve[:, :], mv[:, :, 1], EPS, None, ALU.add).then_inc(v_group, 1)
                v.wait_ge(pl_rs, g + 1)

            def normalise(g, par, r):
                s = g * GROUP + r
                v.wait_ge(pe_xT, s + 1)
                v.tensor_scalar(xn[r % 2][:, :], xg[par][:, r, :], mv[:, r, 0:1], rs[:, r:r + 1],
                                ALU.subtract, ALU.mult).then_inc(v_xn, 1)

            def table_rows(g, r):
                s = g * GROUP + r
                v.wait_ge(pe_wh, s + 1 + 2)
                v.wait_ge(tab_out[r % 2], (g * (GROUP // 2) + r // 2) * 16 + 16)
                v.tensor_copy(s2[:, bass.ds(s, 1)], psW[r % 2][:, D:D + 1])
                v.tensor_copy(whr[r % 2][:, 0:D + 1], psW[r % 2][:, 0:D + 1]).then_inc(v_wh, 1)
                v.tensor_copy(s1[:, bass.ds(s, 1)], psW[r % 2][:, D + 1:D + 2]).then_inc(v_wh, 1)

            with v.Fori(0, LAG // 2) as i:
                for par in range(2):
                    g = i * 2 + par
                    group_stats(g, par, i)
                    for r in range(GROUP):
                        normalise(g, par, r)
                        if r:
                            table_rows(g, r - 1)
                        if r % 2:
                            search(g, par, r // 2)
                    v.wait_ge(v_xn, g * GROUP + GROUP)
                    v.nop(nofuse=True)
                    v.engine_nop().then_inc(v_group, 1)
                    table_rows(g, GROUP - 1)
                    decode(g)
            v.wait_ge(a_xT, 2 * NS + 2)
            v.tensor_reduce(xmean[:, :], xsum[:, :, :], AX.X, ALU.add).then_inc(v_w, 1)
            v.wait_ge(v_w, 3 * DH + 2)
            v.tensor_scalar(xmean[:, :], xmean[:, :], 1.0 / N, None, ALU.mult).then_inc(v_w, 1)
            v.wait_ge(pe_w, DH + 3)
            v.wait_ge(tab_out[0], 16 + 8 * NS)
            v.tensor_copy(whr[0][0:1, 0:D + 1], psW[0][0:1, 0:D + 1]).then_inc(v_wh, 1)

            def indices(u, par):
                v.wait_ge(v_dec, u * VD + VD)
                v.tensor_scalar(idx[par][:, :], keys[:, bass.ds(u, 1), :].rearrange("p o k -> p (o k)"), -1.0, float(N),
                                ALU.mult, ALU.add).then_inc(v_idx, 1)

            def softmax(u, par, i16):
                at = u * VS
                v.wait_ge(gat[par], i16)
                v.tensor_scalar(sc[:, :], G[par][:, :, D], s1[:, bass.ds(u, 1)], None, ALU.add).then_inc(v_sm, 1)
                v.tensor_scalar(pen[:, 1:K], keys[:, bass.ds(u, 1), 1:K].rearrange("p o k -> p (o k)"), 0.0, MASK_VAL,
                                ALU.is_equal, ALU.mult).then_inc(v_sm, 1)
                v.wait_ge(v_sm, at + 2)
                v.scalar_tensor_tensor(out=lr[:, :], in0=sc[:, :], scalar=ALPHA, in1=sc[:, :],
                                       op0=ALU.mult, op1=ALU.max).then_inc(v_sm, 1)
                v.wait_ge(v_sm, at + 3)
                v.tensor_tensor(ee[:, :], lr[:, :], pen[:, :], ALU.add).then_inc(v_sm, 1)
                v.wait_ge(v_sm, at + 4)
                v.tensor_reduce(mx[:, :], ee[:, :], AX.X, ALU.max).then_inc(v_sm, 1)
                v.wait_ge(v_sm, at + 5)
                v.tensor_scalar(nmx[:, :], mx[:, :], -1.0, None, ALU.mult).then_inc(v_sm, 1)
                v.wait_ge(a_p, u + 1)
                v.reciprocal(rden[par][:, :], den[:, :])
                v.wait_ge(pe_o, u + 2)
                v.tensor_tensor(diag[:, :, :], ident[:, :].unsqueeze(1).to_broadcast([P, K, P]),
                                pr[:, :].unsqueeze(2).to_broadcast([P, K, P]), ALU.mult).then_inc(v_diag, 1)

            def post_min(w):
                v.wait_ge(a_h, w + 3)
                v.tensor_scalar(um[:, :], hh[:, :], 0.0, None, ALU.min).then_inc(v_post, 1)

            def post_x1(w, par, i16, strip):
                at = w * VP + CR
                v.wait_ge(a_ex, w + 1)
                v.scalar_tensor_tensor(out=el[:, :], in0=ex[:, :], scalar=-1.0, in1=hh[:, :],
                                       op0=ALU.add, op1=ALU.max).then_inc(v_post, 1)
                v.wait_ge(v_post, at + 2)
                v.wait_ge(xr_in[par], i16)
                v.wait_ge(sc_out[par], i16)
                v.tensor_tensor(x1[par][:, 0:D], el[:, :], xr[par][:, :], ALU.add).then_inc(v_post, 1)
                v.wait_ge(v_post, at + 3)
                v.bn_stats(st2[:, :], x1[par][:, 0:D]).then_inc(v_post, 1)
                v.wait_ge(v_post, at + 4)
                v.nop(nofuse=True)
                v.bn_aggr(x1[par][:, D:D + 2], st2[:, :]).then_inc(v_post, 1)
                v.wait_ge(v_post, at + 5)
                v.tensor_scalar(ve2[:, :], x1[par][:, D + 1:D + 2], EPS, None, ALU.add).then_inc(v_post, 1)
                v.tensor_copy(x1[par][:, D + 2:D + 3], token_no[:, bass.ds(strip, 1)]).then_inc(v_post, 1)

            def post_norm(w, par):
                v.wait_ge(pl_rs2, w + 1)
                v.tensor_scalar(xn2[:, :], x1[par][:, 0:D], x1[par][:, D:D + 1], x1[par][:, D + 1:D + 2],
                                ALU.subtract, ALU.mult).then_inc(v_post, 1)

            def post_expert(w):
                at = w * VP + CR
                v.wait_ge(pe_lg, w + 2)
                v.tensor_copy(lg[:, :], psL[:, 0:E]).then_inc(v_post, 1)
                v.wait_ge(v_post, at + 9)
                v.nop(nofuse=True)
                v.max(lmax[:, :], lg[:, :]).then_inc(v_post, 1)
                v.wait_ge(v_post, at + 10)
                v.nop(nofuse=True)
                v.max_index(lidx[:, :], lmax[:, :], lg[:, :]).then_inc(v_post, 1)
                v.wait_ge(v_post, at + 11)
                v.tensor_copy(ef[:, :], lidx[:, 0:1]).then_inc(v_post, 1)
                v.wait_ge(v_post, at + 12)
                v.scalar_tensor_tensor(out=oh[:, :], in0=expert_no[:, :], scalar=ef[:, 0:1], in1=direction[:, :],
                                       op0=ALU.is_equal, op1=ALU.mult).then_inc(v_post, 1)

            def post_position(w, par):
                at = w * VP + CR
                v.wait_ge(pe_cum, w + 1)
                v.tensor_tensor(c2[:, :], psC[:, 0:E], count[:, :], ALU.add).then_inc(v_post, 1)
                v.tensor_tensor(count[:, :], psC[:, E:2 * E], count[:, :], ALU.add).then_inc(v_post, 1)
                v.wait_ge(v_post, at + 15)
                v.tensor_tensor_reduce(out=c3[:, :], in0=c2[:, :], in1=oh[:, :], scale=1.0, scalar=0.0,
                                       op0=ALU.mult, op1=ALU.add, accum_out=posf[:, :]).then_inc(v_post, 1)
                v.wait_ge(v_post, at + 16)
                v.scalar_tensor_tensor(out=posu[par][:, :], in0=posf[:, :], scalar=-1.0, in1=posf[:, :],
                                       op0=ALU.mult, op1=ALU.max).then_inc(v_post, 1)

            indices(0, 0)

            def half_up(u, par):
                return (u - par) * 8 + 16

            def step(u, par, searching, post, more):
                w = u - 2
                if more:
                    indices(u + 1, 1 - par)
                if searching:
                    search(u + LAG, par, 0)
                if post:
                    post_min(w)
                if searching:
                    search(u + LAG, par, 1)
                if post:
                    post_x1(w, par, half_up(w, par), w)
                if searching:
                    search(u + LAG, par, 2)
                if post:
                    post_norm(w, par)
                if searching:
                    search(u + LAG, par, 3)
                if post:
                    post_expert(w)
                if searching:
                    decode(u + LAG)
                if post:
                    post_position(w, par)
                softmax(u, par, half_up(u, par) * K)
            rounds(v, step)
            for par in range(2):
                w = NS - 2 + par
                post_min(w)
                post_x1(w, par, half_up(w, par), w)
                post_norm(w, par)
                post_expert(w)
                post_position(w, par)

            v.tensor_reduce(mx[:, :], keys[:, :, K - 1], AX.X, ALU.max).then_inc(v_flag, 1)
            v.tensor_reduce(nmx[:, :], most_words[:, :], AX.X, ALU.max).then_inc(v_flag, 1)
            v.wait_ge(v_flag, 2)
            v.tensor_scalar(flagc[:, 0:1], mx[:, :], 0.0, None, ALU.is_gt).then_inc(v_flag, 1)
            v.tensor_scalar(flagc[:, 1:2], nmx[:, :], NONE_WORD, None, ALU.is_gt).then_inc(v_flag, 1)
            v.wait_ge(pe_flag, 1)
            v.tensor_copy(flag_i[0:1, 0:1], psL[0:1, 0:1]).then_inc(v_flag, 1)
            v.wait_ge(v_flag, 5)
            flag = v.value_load(flag_i[0:1, 0:1], min_val=0, max_val=4 * P)
            with v.If(flag > 0):
                v.wait_ge(v_post, NS * VP + CR)
                v.tensor_copy(count[:, :], region_base[:, :])
                v.engine_nop().then_inc(d_v, 1)

                def dense(t, par):
                    A = t * DV_STRIP + 1
                    with v.Fori(0, NS) as b:
                        at = A + b * DV_A
                        v.tensor_scalar(diag[:, 0, :], ident[:, :], s2[:, bass.ds(b, 1)], None, ALU.mult).then_inc(d_v, 1)
                        v.wait_ge(d_in, (t * NS + b) * 16 + 16)
                        v.tensor_scalar(diag[:, 2, :], adj_block[:, :], 0.0, None, ALU.is_gt).then_inc(d_v, 1)
                        v.wait_ge(d_v, at + 2)
                        v.wait_ge(d_pe, t * 3 * NS + b + 1)
                        v.tensor_scalar(diag[:, 3, :], psC[:, 0:P], s1[:, bass.ds(t, 1)], None, ALU.add).then_inc(d_v, 1)
                        v.tensor_scalar(diag[:, 4, :], diag[:, 2, :], -1.0, -MASK_VAL, ALU.add, ALU.mult).then_inc(d_v, 1)
                        v.wait_ge(d_v, at + 4)
                        v.scalar_tensor_tensor(out=diag[:, 5, :], in0=diag[:, 3, :], scalar=ALPHA, in1=diag[:, 3, :],
                                               op0=ALU.mult, op1=ALU.max).then_inc(d_v, 1)
                        v.wait_ge(d_v, at + 5)
                        v.tensor_tensor(diag[:, 6, :], diag[:, 5, :], diag[:, 2, :], ALU.mult).then_inc(d_v, 1)
                        v.wait_ge(d_v, at + 6)
                        v.tensor_tensor(scores[:, bass.ds(b * P, P)], diag[:, 6, :], diag[:, 4, :], ALU.add).then_inc(d_v, 1)
                        v.wait_ge(d_v, at + 7)
                    at = A + NS * DV_A
                    v.tensor_reduce(mx[:, :], scores[:, :], AX.X, ALU.max).then_inc(d_v, 1)
                    v.wait_ge(d_v, at + 1)
                    v.tensor_scalar(nmx[:, :], mx[:, :], -1.0, None, ALU.mult)
                    v.memset(dacc[:, :], 0.0).then_inc(d_v, 1)
                    with v.Fori(0, NS) as b:
                        v.wait_ge(d_pe, t * 3 * NS + NS + b * 2 + 1)
                        v.tensor_copy(diag[:, 7, :], psT[:, 0:P]).then_inc(d_v, 1)
                        v.wait_ge(d_pe, t * 3 * NS + NS + b * 2 + 2)
                        v.tensor_tensor(dacc[:, :], dacc[:, :], psO[0][:, 0:D], ALU.add).then_inc(d_v, 1)
                    v.wait_ge(d_v, at + 2 + 2 * NS)
                    v.tensor_reduce(den[:, :], dsum[:, :], AX.X, ALU.add)
                    v.drain()
                    v.reciprocal(rden[0][:, :], den[:, :]).then_inc(d_v, 1)
                    post_min(t + NS)
                    post_x1(t + NS, par, half_up(t, par) + 8 * NS, t)
                    post_norm(t + NS, par)
                    post_expert(t + NS)
                    post_position(t + NS, par)
                dense_strips(v, dense)

            n = 0

            def planned(ins):
                nonlocal n
                n += 1
                ins.then_inc(v_plan, 1)
                return n

            v.wait_ge(v_plan, planned(v.tensor_tensor(nbf[:, :], count[:, :], region_base[:, :], ALU.subtract)))
            v.wait_ge(v_plan, planned(v.tensor_tensor(nbf[:, :], nbf[:, :], direction[:, :], ALU.mult)))
            v.wait_ge(v_plan, planned(v.tensor_scalar(nbi[:, :], nbf[:, :], float(P - 1), None, ALU.add)))
            v.wait_ge(v_plan, planned(v.tensor_scalar(nbj[:, :], nbi[:, :], 7, None, ALU.arith_shift_right)))
            v.wait_ge(v_plan, planned(v.tensor_copy(nbf[:, :], nbj[:, :])))
            v.wait_ge(v_plan, planned(v.tensor_copy(cum[0][:, :], nbj[:, :])))
            src = 0
            for shift in (1, 2, 4, 8, 16):
                v.wait_ge(v_plan, planned(v.tensor_copy(cum[1 - src][:, 0:shift], cum[src][:, 0:shift])))
                v.wait_ge(v_plan, planned(v.tensor_tensor(cum[1 - src][:, shift:E], cum[src][:, shift:E], cum[src][:, 0:E - shift],
                                        ALU.add)))
                src = 1 - src
            v.wait_ge(v_plan, planned(v.tensor_scalar(le[:, :], cum[src][:, :], part_no[:, 0:1], None, ALU.is_le)))
            v.wait_ge(v_plan, planned(v.tensor_reduce(plan[:, 0:1], le[:, :], AX.X, ALU.add)))

            def pick(col, row, of):
                v.wait_ge(v_plan, planned(v.tensor_tensor_reduce(out=le2[:, :], in0=row[:, :], in1=of[:, :], scale=1.0, scalar=0.0,
                                               op0=ALU.mult, op1=ALU.add, accum_out=plan[:, col:col + 1])))
            pick(1, le, nbf)
            v.wait_ge(v_plan, planned(v.tensor_scalar(plan[:, 2:3], plan[:, 1:2], part_no[:, 0:1], -float(P), ALU.subtract, ALU.mult)))
            v.wait_ge(v_plan, planned(v.tensor_scalar(le[:, :], expert_no[:, :], plan[:, 0:1], None, ALU.is_equal)))
            pick(3, le, direction)
            pick(4, le, first_block)
            v.wait_ge(v_plan, planned(v.tensor_scalar(plan[:, 5:6], plan[:, 0:1], float(E), float(NULL_ROW), ALU.is_ge, ALU.mult)))
            v.wait_ge(v_plan, planned(v.tensor_tensor(plan[:, 2:3], plan[:, 2:3], plan[:, 3:4], ALU.mult)))
            v.wait_ge(v_plan, planned(v.tensor_tensor(plan[:, 4:5], plan[:, 4:5], plan[:, 5:6], ALU.add)))
            v.wait_ge(v_plan, planned(v.tensor_tensor(plan[:, 6:7], plan[:, 2:3], plan[:, 4:5], ALU.add)))
            v.wait_ge(v_plan, planned(v.tensor_tensor(cum[0][:, :], count[:, :], pad_shift[:, :], ALU.add)))
            assert n == PLAN_ROWS
            v.wait_ge(pe_plan, 1)
            v.wait_ge(v_plan, planned(v.tensor_copy(plan_i[:, 0:P], psC[0:1, 0:P])))
            v.wait_ge(v_plan, planned(v.tensor_scalar(plan_i[:, P:2 * P], psC[0:1, P:2 * P], float(E - 1), None, ALU.min)))
            v.wait_ge(v_plan, planned(v.tensor_copy(plan_i[:, 2 * P:2 * P + E], cum[0][0:1, :])))
            assert n == PLAN_STEPS

            def block_step(b, par):
                v.wait_ge(xb_in[par], (b - par) * 8 + 16)
                v.tensor_scalar(xnb[:, :], xb[par][:, 0:D], xb[par][:, D:D + 1], xb[par][:, D + 1:D + 2],
                                ALU.subtract, ALU.mult).then_inc(v_xb, 1)
                v.wait_ge(pe_h, b + 1)
                v.tensor_scalar(hb[par][:, 0:H], psL[:, 0:H], 0.0, None, ALU.max).then_inc(v_h, 1)
                v.wait_ge(pe_y, b + 1)
                if not isinstance(b, int) or b > 1:
                    v.wait_ge(y_out[par], (b - par) * 8)
                v.scalar_tensor_tensor(out=yb[par][:, :], in0=psO[par][:, 0:D], scalar=0.0, in1=xb[par][:, 0:D],
                                       op0=ALU.max, op1=ALU.add).then_inc(v_y, 1)
                v.tensor_copy(tok[par][:, :], xb[par][:, D + 2:D + 3]).then_inc(v_y, 1)
            blocks_loop(v, block_step)

        @block.tensor
        def _(pe):
            pe.sem_inc(pe_xT, 2)
            pe.sem_inc(pe_wh, 2)
            pe.sem_inc(pe_o, 2)
            pe.sem_inc(pe_lg, 1)
            pe.wait_ge(const_in, 16 * 5)
            pe.wait_ge(consts, 14)
            pe.nop(nofuse=True)
            for fh in range(DH):
                if fh:
                    pe.wait_ge(v_w, fh)
                    pe.nop(nofuse=True)
                for kh in range(DH):
                    mm = pe.transpose(psT[:, kh * P:(kh + 1) * P], w_raw[:, kh, fh * P:(fh + 1) * P], ident[:, :])
                mm.then_inc(pe_w, 1)
            pe.wait_ge(v_w, DH)
            pe.nop(nofuse=True)
            for kh in range(DH):
                for fh in range(DH):
                    mm = pe.matmul(psL[:, 2 * kh:2 * kh + 2], w_t[:, fh, kh * P:(kh + 1) * P], a_sb[:, fh, :],
                                   start=(fh == 0), stop=(fh == DH - 1))
            mm.then_inc(pe_w, 1)
            for h in range(DH):
                mm = pe.transpose(psC[:, h * E:(h + 1) * E], rw_sb[:, h * P:(h + 1) * P], ident[0:E, 0:E])
            mm.then_inc(pe_w, 1)
            pe.wait_ge(v_w, 3 * DH)

            def transposes(s, r):
                pe.wait_ge(v_xn, s + 1)
                pe.wait_ge(a_xT, 2 * s + 2)
                pe.nop(nofuse=True)
                for h in range(DH):
                    mm = pe.transpose(psP[:, h * P:(h + 1) * P], xn[r % 2][:, h * P:(h + 1) * P], ident[:, :])
                mm.then_inc(pe_xT, 1)

            def table_rows(s, r):
                pe.wait_ge(a_xT, 2 * s + 4)
                pe.wait_ge(v_wh, 2 * s + 2)
                pe.nop(nofuse=True)
                for h in range(DH):
                    mm = pe.matmul(psW[r % 2][:, 0:D + 2], xT[r % 2][:, h, :], w_aug[:, h, :],
                                   start=(h == 0), stop=(h == DH - 1))
                mm.then_inc(pe_wh, 1)

            with pe.Fori(0, LAG // 2) as i:
                for par in range(2):
                    s = (i * 2 + par) * GROUP
                    for r in range(GROUP):
                        transposes(s + r, r)
                        if r:
                            table_rows(s + r - 1, r - 1)
                    table_rows(s + GROUP - 1, GROUP - 1)
            pe.wait_ge(v_w, 3 * DH + 3)
            pe.wait_ge(v_wh, 2 * NS + 4)
            pe.nop(nofuse=True)
            for h in range(DH):
                mm = pe.matmul(psW[0][0:1, 0:D + 2], xmean[:, h:h + 1], w_aug[:, h, :],
                               start=(h == 0), stop=(h == DH - 1))
            mm.then_inc(pe_w, 1)

            def weighted_sum(u, par):
                pe.wait_ge(v_diag, u + 1)
                pe.wait_ge(a_h, u + 1)
                pe.wait_ge(gat[par], ((u - par) * 8 + 16) * K)
                pe.nop(nofuse=True)
                for k in range(K):
                    mm = pe.matmul(psO[par][:, 0:D], diag[:, k, :], G[par][:, k, 0:D],
                                   start=(k == 0), stop=(k == K - 1))
                mm.then_inc(pe_o, 1)

            def post_transposes(w):
                pe.wait_ge(v_post, w * VP + CR + 8)
                pe.wait_ge(a_x2, w + 1)
                pe.nop(nofuse=True)
                for h in range(DH):
                    mm = pe.transpose(psT[:, h * P:(h + 1) * P], xn2[:, h * P:(h + 1) * P], ident[:, :])
                mm.then_inc(pe_t2, 1)

            def logits(w):
                pe.wait_ge(a_x2, w + 2)
                pe.nop(nofuse=True)
                for h in range(DH):
                    pe.matmul(psL[:, 0:E], xT2[:, h, :], rw_t[:, h, :], start=(h == 0), stop=False)
                pe.matmul(psL[:, 0:E], ones_f[0:1, :], rb_sb[:, :], start=False, stop=True).then_inc(pe_lg, 1)

            def ranks(w):
                pe.wait_ge(v_post, w * VP + CR + 13)
                pe.matmul(psC[:, 0:E], before[:, :], oh[:, :], start=True, stop=True)
                pe.matmul(psC[:, E:2 * E], ones_b[:, :], oh[:, :], start=True, stop=True).then_inc(pe_cum, 1)

            pe.wait_ge(v_w, 3 * DH + 1)

            def step(u, par, searching, post, more):
                if post:
                    post_transposes(u - 2)
                    logits(u - 2)
                    ranks(u - 2)
                weighted_sum(u, par)
            rounds(pe, step)
            for par in range(2):
                post_transposes(NS - 2 + par)
                logits(NS - 2 + par)
                ranks(NS - 2 + par)

            pe.wait_ge(v_flag, 4)
            pe.matmul(psL[0:1, 0:1], flagc[:, 0:1], ones_f[:, 0:1], start=True, stop=False)
            pe.matmul(psL[0:1, 0:1], flagc[:, 1:2], ones_f[:, 0:1], start=False, stop=True).then_inc(pe_flag, 1)
            pe.wait_ge(v_flag, 5)
            flag = pe.value_load(flag_i[0:1, 0:1], min_val=0, max_val=4 * P)
            with pe.If(flag > 0):
                def dense(t, par):
                    with pe.Fori(0, NS) as b:
                        pe.wait_ge(d_v, t * DV_STRIP + 1 + b * DV_A + 1)
                        pe.matmul(psC[:, 0:P], ones_f[:, :], diag[:, 0, :], start=True, stop=True).then_inc(d_pe, 1)
                    with pe.Fori(0, NS) as b:
                        pe.wait_ge(d_a, t * NS + b + 1)
                        pe.transpose(psT[:, 0:P], diag[:, 1, :], ident[:, :]).then_inc(d_pe, 1)
                        pe.wait_ge(d_v, t * DV_STRIP + 1 + NS * DV_A + 2 + 2 * b + 1)
                        pe.wait_ge(d_wh, (t * NS + b) * 16 + 16)
                        pe.matmul(psO[0][:, 0:D], diag[:, 7, :], G[0][:, 0, 0:D], start=True, stop=True).then_inc(d_pe, 1)
                    post_transposes(t + NS)
                    logits(t + NS)
                    ranks(t + NS)
                dense_strips(pe, dense)

            pe.wait_ge(v_plan, PLAN_ROWS)
            pe.nop(nofuse=True)
            for j, col in ((0, 6), (1, 0)):
                mm = pe.matmul(psC[0:1, j * P:(j + 1) * P], plan[:, col:col + 1], ident[:, :], start=True, stop=True)
            mm.then_inc(pe_plan, 1)
            pe.wait_ge(ffn_in, 16 * 4)
            pe.wait_ge(v_plan, PLAN_STEPS)

            def block_step(b, par):
                e = pe.value_load(plan_i[0:1, bass.ds(b + P, 1)], min_val=0, max_val=E - 1)
                pe.wait_ge(v_xb, b + 1)
                pe.wait_ge(a_xb, b + 1)
                pe.nop(nofuse=True)
                for h in range(DH):
                    mm = pe.transpose(psP[:, h * P:(h + 1) * P], xnb[:, h * P:(h + 1) * P], ident[:, :])
                mm.then_inc(pe_xb, 1)
                pe.wait_ge(a_xb, b + 2)
                pe.nop(nofuse=True)
                for h in range(DH):
                    pe.matmul(psL[:, 0:H], xTb[par][:, h, :], w1_sb[:, bass.ds(e, 1), h, :].rearrange("p o n -> p (o n)"),
                              start=(h == 0), stop=False)
                pe.matmul(psL[:, 0:H], ones_f[0:1, :], b1_sb[:, bass.ds(e, 1), :].rearrange("p o n -> p (o n)"),
                          start=False, stop=True).then_inc(pe_h, 1)
                pe.wait_ge(v_h, b + 1)
                pe.transpose(psT[0:H + 1, 0:P], hb[par][:, :], ident[:, :]).then_inc(pe_hT, 1)
                pe.wait_ge(a_hT, b + 1)
                pe.wait_ge(v_y, 2 * b + 1)
                pe.matmul(psO[par][:, 0:D], hT[par][:, :], w2_sb[:, bass.ds(e, 1), :].rearrange("p o n -> p (o n)"),
                          start=True, stop=True).then_inc(pe_y, 1)
            blocks_loop(pe, block_step)


def _int32(bits):
    return bits - (1 << 32) if bits >> 31 else bits


def _word_of_signs(bits):
    import numpy as np
    return abs(float(np.array([bits], np.uint32).view(np.float32)[0]))


_INS = ["x", "adj", "L0_gnn_W", "L0_gnn_a", "L0_ffn_router_w", "L0_ffn_router_b",
        "L0_ffn_W1", "L0_ffn_b1", "L0_ffn_W2", "L0_ffn_b2"]


def kernel(**inputs):
    import numpy as np
    import concourse.bacc as bacc
    from concourse.bass_utils import run_bass_kernel_spmd as run

    nc = bacc.Bacc("TRN2", target_bir_lowering=False, num_devices=1)
    arrays, args = {}, []
    for name in _INS:
        a = np.ascontiguousarray(inputs[name])
        arrays[f"in_{name}"] = a
        args.append(nc.dram_tensor(f"in_{name}", a.shape, mybir.dt.from_np(a.dtype), kind="ExternalInput").ap())
    N = arrays["in_x"].shape[0]
    args.append(nc.dram_tensor("out_x", (N, D), mybir.dt.float32, kind="ExternalOutput").ap())
    args.append(nc.dram_tensor("wh_table", (N + 1, ROW), mybir.dt.float32, kind="Internal").ap())
    args.append(nc.dram_tensor("regions", (E // 2 * (N + 2 * P) + P, ROW), mybir.dt.float32, kind="Internal").ap())
    gat_moe(nc, *args)
    return run(nc, [arrays], core_ids=[0]).results[0]["out_x"]
```

```python
import concourse.bass as bass
from concourse import mybir
from contextlib import ExitStack

P = 128
D = 256
DH = D // P
E = 32
H = 64
ROW = 264
Q = 4
TOP = 8
K = 16
K_ALL = 10
K_MID = 12
RING = 6
KEPT = 4
GROUP = 8
EPS = 1e-5
ALPHA = 0.2
MASK_VAL = -9000000000000000.0
NO_TOKEN = 1.0e6


def gat_moe(nc, x, adj, gW, ga, rw, rb, W1, b1, W2, b2, out, table, region):
    f32, i32, u32 = mybir.dt.float32, mybir.dt.int32, mybir.dt.uint32
    bf16, f8 = mybir.dt.bfloat16, mybir.dt.float8e4
    ALU, ACT, AX = mybir.AluOpType, mybir.ActivationFunctionType, mybir.AxisListType

    N = x.shape[0]
    NS = N // P
    LAG = NS // GROUP
    C = N // Q
    WORDS = C // KEPT
    CAND = Q * TOP * KEPT
    SPAN = N + 2 * P
    BLOCKS = NS + E - 1
    NULL_ROW = E // 2 * SPAN
    assert LAG % 2 == 0 and NS % (2 * GROUP) == 0 and NS >= LAG + 4 and 3 * RING <= BLOCKS <= P

    ctx = ExitStack()
    with ctx:
        def sb(name, shape, dt=f32):
            return ctx.enter_context(nc.sbuf_tensor(name, shape, dt))

        def ps(name, shape, dt=f32):
            return ctx.enter_context(nc.psum_tensor(name, shape, dt))

        def sem(name):
            return ctx.enter_context(nc.semaphore(name))

        ident = sb("ident", [P, P])
        ones_f = sb("ones_f", [P, P])
        ones_b = sb("ones_b", [P, P], bf16)
        before = sb("before", [P, P], bf16)
        byte_sign = sb("byte_sign", [P, Q * TOP, KEPT], i32)
        code_base = sb("code_base", [P, Q, TOP, KEPT])
        expert_no = sb("expert_no", [P, E])
        region_base = sb("region_base", [P, E])
        direction = sb("direction", [P, E])
        first_block = sb("first_block", [P, E])
        pad_shift = sb("pad_shift", [P, E])
        token_no = sb("token_no", [P, NS])
        minus_half = sb("minus_half", [P, GROUP])
        part_no = sb("part_no", [P, 1])
        pad_row = sb("pad_row", [P, ROW])
        zero_col = sb("zero_col", [P, 1])

        w_aug = sb("w_aug", [P, DH, D + 2])
        w_raw = sb("w_raw", [P, DH, D])
        w_t = sb("w_t", [P, DH, D])
        a_sb = sb("a_sb", [P, DH, 2])
        rw_sb = sb("rw_sb", [E, D])
        rw_t = sb("rw_t", [P, DH, E])
        rb_sb = sb("rb_sb", [1, E])
        w1_sb = sb("w1_sb", [P, E, DH, H])
        b1_t = sb("b1_t", [H, E])
        w2_sb = sb("w2_sb", [H + 1, E, D])

        w1_flat = w1_sb[:, :, :, :].rearrange("p e h n -> p (e h n)")
        xg = [w1_flat[:, i * GROUP * D:(i + 1) * GROUP * D].rearrange("p (r d) -> p r d", r=GROUP) for i in range(2)]
        st = sb("st", [P, GROUP, 6])
        mv = sb("mv", [P, GROUP, 2])
        ve = sb("ve", [P, GROUP])
        rs = sb("rs", [P, GROUP])
        xn = [sb(f"xn{i}", [P, D]) for i in range(2)]
        xT = [sb(f"xT{i}", [P, DH, P]) for i in range(2)]
        xsum = sb("xsum", [P, DH, NS])
        xmean = sb("xmean", [P, DH])
        mean_sb = sb("mean_sb", [1, ROW])
        s1 = sb("s1", [P, NS])
        s2 = sb("s2", [P, NS])

        raw_all = sb("raw_all", [P, Q * C], i32)
        raw = [raw_all[:, q * C:(q + 1) * C] for q in range(Q)]
        sg = [[sb(f"sg{i}{q}", [P, C], f8) for q in range(Q)] for i in range(2)]
        top_word = sb("top_word", [P, Q, TOP])
        top_pos = sb("top_pos", [P, Q, TOP], u32)
        bits = sb("bits", [P, Q * TOP, KEPT], i32)
        code = sb("code", [P, CAND])
        key = sb("key", [P, CAND])
        key2 = sb("key2", [P, CAND])
        key16 = sb("key16", [P, K])
        keys = sb("keys", [P, NS, K])
        many = sb("many", [P, 2, 2], bf16)
        more = sb("more", [1, 2, 2])
        more_sum = [sb(f"more_sum{i}", [1, 2]) for i in range(2)]
        gate = sb("gate", [1, NS, 4], i32)
        most_words = sb("most_words", [P, Q])

        idx = [sb(f"idx{i}", [P, K], u32) for i in range(2)]
        G = [sb(f"G{i}", [P, K, ROW]) for i in range(2)]
        sc = sb("sc", [P, K])
        pen = sb("pen", [P, K])
        ee = sb("ee", [P, K])
        mx = sb("mx", [P, 1])
        nmx = sb("nmx", [P, 1])
        pr = sb("pr", [P, K])
        den = sb("den", [P, 1])
        rden = [sb(f"rden{i}", [P, 1]) for i in range(2)]
        diag = sb("diag", [P, K, P])

        table_rows_sb = [G[0][:, i * GROUP:(i + 1) * GROUP, :] for i in range(2)]

        xr = [sb(f"xr{i}", [P, D]) for i in range(2)]
        hh = sb("hh", [P, D])
        um = sb("um", [P, D])
        ex = sb("ex", [P, D])
        el = sb("el", [P, D])
        st2 = sb("st2", [P, 6])
        ve2 = sb("ve2", [P, 1])
        x1 = [sb(f"x1{i}", [P, ROW]) for i in range(2)]
        xn2 = sb("xn2", [P, D])
        xT2 = sb("xT2", [P, DH, P])
        lg = sb("lg", [P, E])
        lmax = sb("lmax", [P, TOP])
        lidx = sb("lidx", [P, TOP], u32)
        ef = sb("ef", [P, 1])
        oh = sb("oh", [P, E], bf16)
        count = sb("count", [P, E])
        c2 = sb("c2", [P, E])
        c3 = sb("c3", [P, E])
        posf = sb("posf", [P, 1])
        posu = [sb(f"posu{i}", [P, 1], u32) for i in range(2)]

        nbi = sb("nbi", [P, E], i32)
        nbj = sb("nbj", [P, E], i32)
        nbf = sb("nbf", [P, E])
        cum = [sb(f"cum{i}", [P, E]) for i in range(2)]
        le = sb("le", [P, E])
        le2 = sb("le2", [P, E])
        plan = sb("plan", [P, 8])
        plan_i = sb("plan_i", [1, 2 * P], i32)
        pad_i = sb("pad_i", [1, E], i32)

        scores = raw_all[:, :].bitcast(f32)
        adj_block = sb("adj_block", [P, P], i32)
        dsum = sb("dsum", [P, NS])
        dacc = sb("dacc", [P, D])
        flagc = sb("flagc", [P, 2])
        flag_i = sb("flag_i", [1, 2], i32)

        xb = [sb(f"xb{i}", [P, ROW]) for i in range(RING)]
        xnb = [sb(f"xnb{i}", [P, D]) for i in range(2)]
        xTb = [sb(f"xTb{i}", [P, DH, P]) for i in range(2)]
        w1_b = [sb(f"w1_b{i}", [P, DH, H]) for i in range(2)]
        b1_b = [sb(f"b1_b{i}", [H, 1]) for i in range(2)]
        w2_b = [sb(f"w2_b{i}", [H + 1, D]) for i in range(2)]
        hT = [sb(f"hT{i}", [H + 1, P]) for i in range(2)]
        yb = [sb(f"yb{i}", [P, D]) for i in range(2)]
        tok = [sb(f"tok{i}", [P, 1], u32) for i in range(2)]

        psP = ps("psP", [P, 512])
        psW = [ps(f"psW{i}", [P, 512]) for i in range(2)]
        psO = [ps(f"psO{i}", [P, 512]) for i in range(2)]
        psT = ps("psT", [P, 512])
        psL = ps("psL", [P, 512])
        psC = ps("psC", [P, 512])
        psXn = [psP, psO[0]]
        psX = [psP, psW[0]]
        psH = [psL, psW[1]]

        const_in = sem("const_in")
        ffn_in = sem("ffn_in")
        consts = sem("consts")
        v_const = sem("v_const")
        pe_w = sem("pe_w")
        v_w = sem("v_w")
        xg_in = [sem(f"xg_in{i}") for i in range(2)]
        v_st = sem("v_st")
        v_var = sem("v_var")
        pl_rs = sem("pl_rs")
        v_xn = sem("v_xn")
        pe_xT = sem("pe_xT")
        a_xT = sem("a_xT")
        pe_wh = sem("pe_wh")
        v_wh = sem("v_wh")
        v_s = sem("v_s")
        tab_out = [sem(f"tab_out{i}") for i in range(2)]
        mean_out = sem("mean_out")

        raw_in = [sem(f"raw_in{q}") for q in range(Q)]
        a_sg = sem("a_sg")
        v_top = sem("v_top")
        v_find = sem("v_find")
        v_dec = sem("v_dec")
        v_idx = sem("v_idx")
        v_gs = sem("v_gs")
        pe_gate = sem("pe_gate")
        gates = sem("gates")
        gat = [sem(f"gat{i}") for i in range(2)]
        gat_more = [sem(f"gat_more{i}") for i in range(2)]
        v_sm = sem("v_sm")
        a_p = sem("a_p")
        v_diag = sem("v_diag")
        pe_o = sem("pe_o")
        a_h = sem("a_h")
        v_post = sem("v_post")
        a_ex = sem("a_ex")
        pl_rs2 = sem("pl_rs2")
        pe_t2 = sem("pe_t2")
        a_x2 = sem("a_x2")
        pe_lg = sem("pe_lg")
        pe_cum = sem("pe_cum")
        xr_in = [sem(f"xr_in{i}") for i in range(2)]
        sc_out = [sem(f"sc_out{i}") for i in range(2)]

        v_flag = sem("v_flag")
        pe_flag = sem("pe_flag")
        d_in = sem("d_in")
        d_wh = sem("d_wh")
        d_v = sem("d_v")
        d_pe = sem("d_pe")
        d_a = sem("d_a")

        v_plan = sem("v_plan")
        pe_plan = sem("pe_plan")
        pad_out = sem("pad_out")
        pad_out_pool = sem("pad_out_pool")
        xb_in = [sem(f"xb_in{i}") for i in range(RING)]
        v_xb = sem("v_xb")
        pe_xb = sem("pe_xb")
        a_xb = sem("a_xb")
        v_w2 = sem("v_w2")
        a_w1 = sem("a_w1")
        pe_h = sem("pe_h")
        a_hT = sem("a_hT")
        pe_y = sem("pe_y")
        v_y = sem("v_y")
        y_out = [sem(f"y_out{i}") for i in range(2)]

        VP = 17
        CR = 2 * VP
        VD = 8
        VS = 4
        NONE_WORD = -float(_word_of_signs(0xB8B8B8B8))

        def segments():
            yield "first", 0, 2
            if NS - LAG - 2 > 2:
                yield "steady", 2, NS - LAG - 2
            yield "turn", NS - LAG - 2, NS - LAG
            if NS - 2 > NS - LAG:
                yield "drain", NS - LAG, NS - 2
            yield "last", NS - 2, NS

        def rounds(eng, step):
            for kind, lo, hi in segments():
                searching = kind in ("first", "steady", "turn")
                if kind in ("first", "turn", "last"):
                    for par in range(2):
                        u = lo + par
                        step(u, par, searching, u + LAG + 1 < NS, u >= 2, u + 1 < NS)
                else:
                    with eng.Fori(lo // 2, hi // 2) as i:
                        for par in range(2):
                            step(i * 2 + par, par, searching, searching, True, True)

        def dense_strips(eng, step):
            with eng.Fori(0, NS // 2) as i:
                for par in range(2):
                    step(i * 2 + par, par)

        DV_A = 7
        DV_STRIP = NS * DV_A + 2 + NS * 2 + 1
        PLAN_PADS = 2
        PLAN_ROWS = PLAN_PADS + 27
        PLAN_STEPS = PLAN_ROWS + 2
        TAIL = 3

        def blocks_loop(eng, stages):
            def step(i, r, turn):
                for stage, lag in stages:
                    if not isinstance(i, int) or 0 <= i - lag < BLOCKS:
                        stage(i - lag, (r - lag) % RING, turn if lag <= r else turn - 1)
            turns = BLOCKS // RING
            for r in range(RING):
                step(r, r, 0)
            with eng.Fori(1, turns) as turn:
                for r in range(RING):
                    step(turn * RING + r, r, turn)
            for i in range(turns * RING, BLOCKS + TAIL):
                step(i, i % RING, i // RING)

        block = ctx.enter_context(nc.Block())

        def pad_experts(eng, first, end, done):
            eng.wait_ge(v_plan, PLAN_PADS)
            eng.nop(nofuse=True)
            with eng.Fori(first, end) as e:
                row = eng.value_load(pad_i[0:1, bass.ds(e, 1)], min_val=0, max_val=NULL_ROW)
                eng.dma_start(region[bass.ds(row, P), :], pad_row[:, :]).then_inc(done, 16)

        @block.sync
        def _(sp):
            sp.dma_start(w_raw[:, :, :], gW.rearrange("(h p) n -> p h n", p=P)).then_inc(const_in, 16)
            with nc.allow_non_contiguous_dma(reason="two small vectors"):
                sp.dma_start(a_sb[:, :, 0:1], ga[D:2 * D, :].rearrange("(h p) o -> p h o", p=P)).then_inc(const_in, 16)
                sp.dma_start(a_sb[:, :, 1:2], ga[0:D, :].rearrange("(h p) o -> p h o", p=P)).then_inc(const_in, 16)
            sp.dma_start(rw_sb[:, :], rw[:, :]).then_inc(const_in, 16)
            sp.dma_start(rb_sb[:, :], rb.rearrange("(o n) -> o n", o=1)).then_inc(const_in, 16)

            def load_group(g, par, i):
                sp.wait_ge(v_xn, g * GROUP + GROUP)
                sp.nop(nofuse=True)
                sp.dma_start(xg[par][:, :, :],
                             x[bass.ds(g * GROUP * P, GROUP * P), :].rearrange("(r p) d -> p r d", p=P)
                             ).then_inc(xg_in[par], 16)

            def load_strip(t):
                for q in range(Q):
                    sp.wait_ge(a_sg, t * Q + q + 1)
                    sp.nop(nofuse=True)
                    sp.dma_start(raw[q], adj[bass.ds(t * P, P), q * C:(q + 1) * C]).then_inc(raw_in[q], 16)

            def load_x(v, par):
                sp.wait_ge(v_post, v * VP + 3)
                sp.nop(nofuse=True)
                sp.dma_start(xr[par][:, :], x[bass.ds(v * P, P), :]).then_inc(xr_in[par], 16)

            with sp.Fori(0, LAG // 2) as i:
                for par in range(2):
                    load_group(i * 2 + par, par, i)
                    load_strip(i * 2 + par)

            sp.dma_start(w2_sb[0:H, :, :], W2.rearrange("e k n -> k e n")).then_inc(ffn_in, 16)
            sp.dma_start(w2_sb[H:H + 1, :, :], b2.rearrange("(o e) n -> o e n", o=1)).then_inc(ffn_in, 16)
            with nc.allow_non_contiguous_dma(reason="a small matrix, transposed"):
                sp.dma_start(b1_t[:, :], b1.rearrange("e n -> n e")).then_inc(ffn_in, 16)
            sp.wait_ge(v_xn, NS + 2 * GROUP)
            sp.nop(nofuse=True)
            sp.dma_start(w1_sb[:, :, :, :].rearrange("p e h n -> p (e h) n"),
                         W1.rearrange("e (h p) n -> p (e h) n", p=P)).then_inc(ffn_in, 16)

            def step(u, par, searching, ahead, post, more):
                if searching:
                    load_strip(u + LAG)
                if post or u:
                    load_x(u - 1, 1 - par)
            rounds(sp, step)
            load_x(NS - 1, 1)

            sp.wait_ge(v_flag, 5)
            sp.nop(nofuse=True)
            flag = sp.value_load(flag_i[0:1, 0:1], min_val=0, max_val=4 * P)
            with sp.If(flag > 0):
                def dense(t, par):
                    with sp.Fori(0, NS) as b:
                        sp.wait_ge(d_v, t * DV_STRIP + b * DV_A + 1)
                        sp.nop(nofuse=True)
                        sp.dma_start(adj_block[:, :], adj[bass.ds(t * P, P), bass.ds(b * P, P)]).then_inc(d_in, 16)
                        sp.wait_ge(d_in, (t * NS + b) * 16 + 16)
                        sp.nop(nofuse=True)
                    with sp.Fori(0, NS) as b:
                        sp.wait_ge(d_v, t * DV_STRIP + NS * DV_A + 2 + b * 2 + 1)
                        sp.nop(nofuse=True)
                        sp.dma_start(G[0][:, 0, :], table[bass.ds(b * P, P), :]).then_inc(d_wh, 16)
                        sp.wait_ge(d_wh, (t * NS + b) * 16 + 16)
                        sp.nop(nofuse=True)
                    sp.wait_ge(v_post, (t + NS) * VP + 3)
                    sp.nop(nofuse=True)
                    sp.dma_start(xr[par][:, :], x[bass.ds(t * P, P), :]).then_inc(xr_in[par], 16)
                dense_strips(sp, dense)
                sp.wait_ge(sc_out[0], 16 + 16 * NS)
                sp.nop(nofuse=True)
                sp.wait_ge(sc_out[1], 16 + 16 * NS)
                sp.nop(nofuse=True)

            pad_experts(sp, 0, 12, pad_out)
            sp.wait_ge(v_plan, PLAN_STEPS)
            sp.nop(nofuse=True)
            sp.wait_ge(pad_out, 16 * 24)
            sp.nop(nofuse=True)
            sp.wait_ge(pad_out_pool, 16 * (E - 24))
            sp.nop(nofuse=True)
            sp.wait_ge(sc_out[0], 16 + 8 * NS)
            sp.nop(nofuse=True)
            sp.wait_ge(sc_out[1], 16 + 8 * NS)
            sp.nop(nofuse=True)

            def load_block(b, r, turn):
                row = sp.value_load(plan_i[0:1, bass.ds(b, 1)], min_val=0, max_val=NULL_ROW)
                sp.wait_ge(v_y, b + 1)
                sp.nop(nofuse=True)
                sp.dma_start(xb[r][:, :], region[bass.ds(row, P), :]).then_inc(xb_in[r], 16)
            blocks_loop(sp, [(load_block, 0)])

        @block.gpsimd
        def _(pool):
            pool.memset(ones_f[:, :], 1.0).then_inc(consts, 1)
            pool.memset(ones_b[:, :], 1.0).then_inc(consts, 1)
            pool.memset(ident[:, :], 0.0).then_inc(consts, 1)
            pool.memset(minus_half[:, :], -0.5).then_inc(consts, 1)
            pool.wait_ge(consts, 4)
            pool.nop(nofuse=True)
            pool.affine_select(out=ident[:, :], in_=ident[:, :], compare_op=ALU.not_equal, fill=1.0, base=0,
                               pattern=[[-1, P]], channel_multiplier=1).then_inc(consts, 1)
            pool.affine_select(out=before[:, :], in_=ones_b[:, :], compare_op=ALU.is_gt, fill=0.0, base=0,
                               pattern=[[1, P]], channel_multiplier=-1).then_inc(consts, 1)
            pool.iota(code_base[:, :, :, :], [[-C, Q], [0, TOP], [-1, KEPT]], base=N, channel_multiplier=0,
                      allow_small_or_imprecise_dtypes=True).then_inc(consts, 1)
            pool.iota(expert_no[:, :], [[1, E]], base=0, channel_multiplier=0,
                      allow_small_or_imprecise_dtypes=True).then_inc(consts, 1)
            for tile, at, step_odd in ((region_base, 0, SPAN - 1), (direction, 1, -2),
                                       (first_block, 0, SPAN - P), (pad_shift, 0, 1 - P)):
                by_pair = SPAN if tile in (region_base, first_block) else 0
                pool.iota(tile[:, :], [[by_pair, E // 2], [step_odd, 2]], base=at, channel_multiplier=0,
                          allow_small_or_imprecise_dtypes=True).then_inc(consts, 1)
            pool.iota(token_no[:, :], [[P, NS]], base=0, channel_multiplier=1,
                      allow_small_or_imprecise_dtypes=True).then_inc(consts, 1)
            pool.iota(part_no[:, :], [[0, 1]], base=0, channel_multiplier=1,
                      allow_small_or_imprecise_dtypes=True).then_inc(consts, 1)
            pool.wait_ge(v_const, 7)
            pool.nop(nofuse=True)
            for i, done in enumerate(sc_out + gat_more):
                part = NULL_ROW + i * (P // 4)
                pool.dma_start(region[part:part + P // 4, :], pad_row[0:P // 4, :]).then_inc(done, 16)
            for par in range(2):
                pool.dma_start(table[N:N + 1, par * (ROW // 2):(par + 1) * (ROW // 2)],
                               pad_row[0:1, 0:ROW // 2]).then_inc(tab_out[par], 16)
            last_row = pool.to_reg(N - 1)
            mean_row = pool.to_reg(N)
            last_region_row = pool.to_reg(NULL_ROW - 1)

            def group(g, par):
                pool.wait_ge(v_var, g + 1)
                pool.nop(nofuse=True)
                pool.tensor_tensor(rs[:, :], ve[:, :], minus_half[:, :], ALU.pow).then_inc(pl_rs, 1)
                pool.wait_ge(v_wh, g * GROUP + GROUP + 2)
                pool.nop(nofuse=True)
                pool.dma_start(table[bass.ds(g * GROUP * P, GROUP * P), :].rearrange("(r p) d -> p r d", p=P),
                               table_rows_sb[par][:, :, :]).then_inc(tab_out[par], 16)
            with pool.Fori(0, LAG // 2) as i:
                for par in range(2):
                    group(i * 2 + par, par)
            pool.wait_ge(v_wh, NS + 2 + 1)
            pool.nop(nofuse=True)
            pool.dma_start(table[N:N + 1, :], mean_sb[:, :]).then_inc(mean_out, 16)
            pool.wait_ge(v_s, LAG)
            pool.nop(nofuse=True)
            pool.wait_ge(tab_out[0], 16 + 8 * LAG)
            pool.nop(nofuse=True)
            pool.wait_ge(tab_out[1], 16 + 8 * LAG)
            pool.nop(nofuse=True)
            pool.wait_ge(mean_out, 16)
            pool.nop(nofuse=True)

            def gather(par, k0, k1, done):
                for k in range(k0, k1):
                    pool.indirect_dma_start(
                        out=G[par][:, k, :], out_offset=None, in_=table[:, :],
                        in_offset=bass.IndirectOffsetOnAxis(ap=idx[par][:, k:k + 1], axis=0),
                        bounds_check=mean_row if k == 0 else last_row, oob_is_err=False).then_inc(done[par], 16)

            def gather_more(u, par):
                pool.wait_ge(gates, u + 1)
                pool.nop(nofuse=True)
                above_all = pool.value_load(gate[0:1, bass.ds(u, 1), 0:1], min_val=0, max_val=1)
                with pool.If(above_all > 0):
                    gather(par, K_ALL, K_MID, gat_more)
                    above_mid = pool.value_load(gate[0:1, bass.ds(u, 1), 1:2], min_val=0, max_val=1)
                    with pool.If(above_mid > 0):
                        gather(par, K_MID, K, gat_more)

            def gather_waits(u, par):
                pool.wait_ge(v_idx, u + 1)
                pool.nop(nofuse=True)
                pool.wait_ge(pe_o, u + 1)
                pool.nop(nofuse=True)

            def inverse_std(w, par):
                pool.wait_ge(v_post, w * VP + CR + 6)
                pool.nop(nofuse=True)
                pool.tensor_tensor(x1[par][:, D + 1:D + 2], ve2[:, :], minus_half[:, 0:1], ALU.pow).then_inc(pl_rs2, 1)

            def scatter(w, par):
                pool.wait_ge(v_post, w * VP + CR + VP)
                pool.nop(nofuse=True)
                pool.indirect_dma_start(
                    out=region[:, :], out_offset=bass.IndirectOffsetOnAxis(ap=posu[par][:, 0:1], axis=0),
                    in_=x1[par][:, :], in_offset=None, bounds_check=last_region_row, oob_is_err=False
                ).then_inc(sc_out[par], 16)

            gather_waits(0, 0)
            gather(0, 0, K_ALL, gat)
            gather_more(0, 0)

            def step(u, par, searching, ahead, post, more):
                if more:
                    gather_waits(u + 1, 1 - par)
                    gather(1 - par, 0, 4, gat)
                if post:
                    scatter(u - 2, par)
                if more:
                    gather(1 - par, 4, K_ALL, gat)
                    gather_more(u + 1, 1 - par)
                if post or u:
                    inverse_std(u - 1, 1 - par)
            rounds(pool, step)
            scatter(NS - 2, 0)
            inverse_std(NS - 1, 1)
            scatter(NS - 1, 1)

            pool.wait_ge(v_flag, 5)
            pool.nop(nofuse=True)
            flag = pool.value_load(flag_i[0:1, 0:1], min_val=0, max_val=4 * P)
            with pool.If(flag > 0):
                def dense(t, par):
                    inverse_std(t + NS, par)
                    scatter(t + NS, par)
                dense_strips(pool, dense)

            pad_experts(pool, 24, E, pad_out_pool)

            def store_block(b, r, turn):
                pool.wait_ge(v_y, b + 1 + RING)
                pool.nop(nofuse=True)
                pool.indirect_dma_start(
                    out=out[:, :], out_offset=bass.IndirectOffsetOnAxis(ap=tok[r % 2][:, 0:1], axis=0),
                    in_=yb[r % 2][:, :], in_offset=None, bounds_check=last_row, oob_is_err=False
                ).then_inc(y_out[r % 2], 16)
            blocks_loop(pool, [(store_block, TAIL)])
            pool.wait_ge(y_out[0], 16 * ((BLOCKS + 1) // 2))
            pool.nop(nofuse=True)
            pool.wait_ge(y_out[1], 16 * (BLOCKS // 2))
            pool.nop(nofuse=True)

        @block.scalar
        def _(act):
            act.sem_inc(a_xT, 4)
            act.sem_inc(a_sg, Q)
            act.sem_inc(a_h, 2)
            act.sem_inc(a_x2, 1)
            act.wait_ge(v_const, 7)

            def transposes(s, r):
                act.wait_ge(pe_xT, s + 1 + 2)
                act.wait_ge(pe_wh, s + 1)
                act.nop(nofuse=True)
                for h in range(DH):
                    act.activation(xT[r % 2][:, h, :], psXn[r % 2][:, h * P:(h + 1) * P], ACT.Copy,
                                   accum_out=xsum[:, h, bass.ds(s, 1)]).then_inc(a_xT, 1)

            def signs(t, par, q):
                act.wait_ge(raw_in[q], t * 16 + 16)
                act.wait_ge(v_find, t * Q + q + 1)
                act.nop(nofuse=True)
                act.activation(sg[par][q][:, :], raw[q], ACT.Sign, bias=minus_half[:, 0:1],
                               saturate=False).then_inc(a_sg, 1)

            with act.Fori(0, LAG // 2) as i:
                for par in range(2):
                    for r in range(GROUP):
                        transposes((i * 2 + par) * GROUP + r, r)
                        if r % 2 == 0:
                            signs(i * 2 + par, par, r // 2)

            def attention_sum(w, par):
                act.wait_ge(pe_o, w + 3)
                act.wait_ge(v_post, w * VP + CR)
                act.activation(hh[:, :], psO[par][:, 0:D], ACT.Copy, scale=rden[par][:, 0:1]).then_inc(a_h, 1)

            def elu_exp(w):
                act.wait_ge(v_post, w * VP + CR + 1)
                act.activation(ex[:, :], um[:, :], ACT.Exp).then_inc(a_ex, 1)

            def transposes2(w):
                act.wait_ge(pe_t2, w + 1)
                act.wait_ge(pe_lg, w + 1)
                act.activation(xT2[:, :, :].rearrange("p h n -> p (h n)"), psT[:, 0:D], ACT.Copy).then_inc(a_x2, 1)

            def softmax_exp(u):
                act.wait_ge(v_sm, u * VS + VS)
                act.activation(pr[:, :], ee[:, :], ACT.Exp, bias=nmx[:, 0:1], accum_out=den[:, 0:1]).then_inc(a_p, 1)

            signs(LAG, 0, 0)

            def step(u, par, searching, ahead, post, more):
                if post:
                    attention_sum(u - 2, par)
                if searching:
                    signs(u + LAG, par, 1)
                if post:
                    elu_exp(u - 2)
                if searching:
                    signs(u + LAG, par, 2)
                    signs(u + LAG, par, 3)
                if post:
                    transposes2(u - 2)
                if ahead:
                    signs(u + LAG + 1, 1 - par, 0)
                softmax_exp(u)
            rounds(act, step)
            for par in range(2):
                attention_sum(NS - 2 + par, par)
                elu_exp(NS - 2 + par)
                transposes2(NS - 2 + par)

            act.wait_ge(v_flag, 5)
            flag = act.value_load(flag_i[0:1, 0:1], min_val=0, max_val=4 * P)
            with act.If(flag > 0):
                def dense(t, par):
                    with act.Fori(0, NS) as b:
                        act.wait_ge(d_v, t * DV_STRIP + NS * DV_A + 2 + b * 2 + 1)
                        act.activation(diag[:, 1, :], scores[:, bass.ds(b * P, P)], ACT.Exp, bias=nmx[:, 0:1],
                                       accum_out=dsum[:, bass.ds(b, 1)]).then_inc(d_a, 1)
                    act.wait_ge(d_v, (t + 1) * DV_STRIP + 1)
                    act.wait_ge(v_post, (t + NS) * VP + CR)
                    act.activation(hh[:, :], dacc[:, :], ACT.Copy, scale=rden[0][:, 0:1]).then_inc(a_h, 1)
                    elu_exp(t + NS)
                    transposes2(t + NS)
                dense_strips(act, dense)

            pad_experts(act, 12, 24, pad_out)

            def copy_xT(b, r, turn):
                act.wait_ge(pe_xb, b + 1)
                act.activation(xTb[r % 2][:, :, :].rearrange("p h n -> p (h n)"), psX[r % 2][:, 0:D],
                               ACT.Copy).then_inc(a_xb, 1)

            def copy_w1(b, r, turn):
                e = act.value_load(plan_i[0:1, bass.ds(b + P, 1)], min_val=0, max_val=E - 1)
                if not isinstance(b, int) or b >= 2:
                    act.wait_ge(a_hT, b - 1)
                act.activation(b1_b[r % 2][:, :], b1_t[:, bass.ds(e, 1)], ACT.Copy)
                act.activation(w1_b[r % 2][:, :, :].rearrange("p h n -> p (h n)"),
                               w1_sb[:, bass.ds(e, 1), :, :].rearrange("p o h n -> p (o h n)"), ACT.Copy).then_inc(a_w1, 1)

            def hidden(b, r, turn):
                act.wait_ge(pe_h, b + 1)
                act.wait_ge(a_w1, b + 1)
                act.activation(hT[r % 2][0:H, :], psH[r % 2][0:H, 0:P], ACT.Relu, bias=b1_b[r % 2][:, :]).then_inc(a_hT, 1)
            act.wait_ge(ffn_in, 16 * 4)
            act.wait_ge(v_plan, PLAN_STEPS)
            blocks_loop(act, [(copy_xT, 1), (hidden, 2), (copy_w1, 0)])

        @block.vector
        def _(v):
            v.sem_inc(v_wh, 2)
            v.sem_inc(v_xn, 2 * GROUP)
            v.sem_inc(v_find, 2 * Q)
            v.sem_inc(v_post, CR)
            v.sem_inc(v_y, RING)
            for r in range(KEPT):
                v.memset(byte_sign[:, :, r], _int32(0x80 << (8 * r))).then_inc(v_const, 1)
            v.memset(most_words[:, :], NONE_WORD).then_inc(v_const, 1)
            v.memset(pad_row[:, 0:D + 2], 0.0)
            v.memset(pad_row[:, D + 2:ROW], NO_TOKEN)
            v.memset(pen[:, :], 0.0)
            v.memset(mean_sb[:, :], 0.0)
            for par in range(2):
                v.memset(G[par][:, :, :], 0.0)
                v.memset(x1[par][:, :], 0.0)
                v.memset(hT[par][:, :], 1.0)
            v.memset(more_sum[0][:, :], 16.0)
            v.memset(zero_col[:, :], 0.0).then_inc(v_const, 1)
            v.wait_ge(consts, 14)
            v.tensor_copy(count[:, :], region_base[:, :]).then_inc(v_const, 1)

            for h in range(DH):
                v.wait_ge(pe_w, h + 1)
                v.tensor_copy(w_t[:, h, :], psT[:, 0:D]).then_inc(v_w, 1)
            for h in range(DH):
                v.tensor_copy(w_aug[:, h, 0:D], w_raw[:, h, :]).then_inc(v_w, 1)
            for h in range(DH):
                v.wait_ge(pe_w, DH + 1)
                v.tensor_copy(w_aug[:, h, D:D + 2], psL[:, 2 * h:2 * h + 2]).then_inc(v_w, 1)
            v.wait_ge(pe_w, DH + 2)
            v.tensor_copy(rw_t[:, :, :], psC[:, 0:DH * E].rearrange("p (h e) -> p h e", h=DH)).then_inc(v_w, 1)

            def search(t, par, q):
                v.wait_ge(a_sg, t * Q + q + 1 + Q)
                v.nop(nofuse=True)
                words = sg[par][q][:, :].bitcast(f32)
                v.max(top_word[:, q, :], words).then_inc(v_top, 1)

            def find(t, par, q):
                words = sg[par][q][:, :].bitcast(f32)
                v.wait_ge(v_top, t * Q + q + 1)
                v.nop(nofuse=True)
                v.max_index(top_pos[:, q, :], top_word[:, q, :], words).then_inc(v_find, 1)

            def decode_words(t):
                v.wait_ge(v_find, t * Q + Q + 2 * Q)
                v.tensor_tensor(bits[:, :, :],
                                top_word[:, :, :].rearrange("p q n -> p (q n)").bitcast(i32).unsqueeze(2).to_broadcast([P, Q * TOP, KEPT]),
                                byte_sign[:, :, :], ALU.bitwise_and).then_inc(v_dec, 1)
                v.scalar_tensor_tensor(out=code[:, :].rearrange("p (n r) -> p n r", r=KEPT),
                                       in0=top_pos[:, :, :].rearrange("p q n -> p (q n)").unsqueeze(2).to_broadcast([P, Q * TOP, KEPT]),
                                       scalar=-float(KEPT),
                                       in1=code_base[:, :, :, :].rearrange("p q n r -> p (q n) r"),
                                       op0=ALU.mult, op1=ALU.add).then_inc(v_dec, 1)
                v.tensor_tensor(most_words[:, :], most_words[:, :], top_word[:, :, TOP - 1], ALU.max).then_inc(v_dec, 1)

            def decode_keys(t):
                at = t * VD
                v.wait_ge(v_dec, at + 3)
                v.scalar_tensor_tensor(out=key[:, :], in0=bits[:, :, :].rearrange("p n r -> p (n r)"), scalar=0.0,
                                       in1=code[:, :], op0=ALU.is_equal, op1=ALU.mult).then_inc(v_dec, 1)

            def decode_first(t):
                at = t * VD
                v.wait_ge(v_dec, at + 4)
                v.nop(nofuse=True)
                v.max(key16[:, 0:TOP], key[:, :]).then_inc(v_dec, 1)

            def decode_rest(t):
                at = t * VD
                v.wait_ge(v_dec, at + 5)
                v.nop(nofuse=True)
                v.match_replace(key2[:, :], key16[:, 0:TOP], key[:, :], 0.0).then_inc(v_dec, 1)

            def decode_second(t):
                at = t * VD
                v.wait_ge(v_dec, at + 6)
                v.nop(nofuse=True)
                v.max(key16[:, TOP:K], key2[:, :]).then_inc(v_dec, 1)

            def decode_keep(t):
                at = t * VD
                v.wait_ge(v_dec, at + 7)
                v.tensor_copy(keys[:, bass.ds(t, 1), :], key16[:, :].unsqueeze(1)).then_inc(v_dec, 1)

            def set_gates(t, bank):
                at = t * 2
                v.wait_ge(v_dec, (t + 1) * VD + VD)
                v.tensor_scalar(many[:, :, :], keys[:, bass.ds(t, 2), K_ALL:K_MID + 1:K_MID - K_ALL], 0.0, None,
                                ALU.is_gt).then_inc(v_gs, 1)
                v.wait_ge(pe_gate, t + 2)
                v.tensor_scalar(more[:, :, :].rearrange("p t k -> p (t k)"), bank[0:1, 0:4], 0.0, None,
                                ALU.is_gt).then_inc(v_gs, 1)
                v.wait_ge(v_gs, at + 2)
                v.tensor_copy(gate[:, bass.ds(t, 2), 0:2], more[:, :, :])
                v.scalar_tensor_tensor(out=more_sum[1][:, :], in0=more[:, :, 0], scalar=16.0 * (K_MID - K_ALL),
                                       in1=more_sum[0][:, :], op0=ALU.mult, op1=ALU.add).then_inc(v_gs, 1)
                v.wait_ge(v_gs, at + 3)
                v.scalar_tensor_tensor(out=more_sum[0][:, :], in0=more[:, :, 1], scalar=16.0 * (K - K_MID),
                                       in1=more_sum[1][:, :], op0=ALU.mult, op1=ALU.add).then_inc(v_gs, 1)
                v.wait_ge(v_gs, at + 4)
                v.tensor_copy(gate[:, bass.ds(t, 2), 2:3].rearrange("p t o -> p (t o)"), more_sum[0][:, :]).then_inc(gates, 2)

            def group_stats(g, par, i, r):
                if r == 0:
                    v.wait_ge(xg_in[par], i * 16 + 16)
                    v.nop(nofuse=True)
                v.bn_stats(st[:, r, :], xg[par][:, r, :]).then_inc(v_st, 1)

            def group_variances(g):
                v.wait_ge(v_st, g * 2 * GROUP + GROUP)
                v.nop(nofuse=True)
                for r in range(GROUP):
                    v.bn_aggr(mv[:, r, :], st[:, r, :]).then_inc(v_st, 1)
                v.wait_ge(v_st, g * 2 * GROUP + 2 * GROUP)
                v.tensor_scalar(ve[:, :], mv[:, :, 1], EPS, None, ALU.add).then_inc(v_var, 1)

            def normalise(g, par, r):
                s = g * GROUP + r
                if r == 0:
                    v.wait_ge(pl_rs, g + 1)
                v.wait_ge(pe_xT, s + 1)
                v.tensor_scalar(xn[r % 2][:, :], xg[par][:, r, :], mv[:, r, 0:1], rs[:, r:r + 1],
                                ALU.subtract, ALU.mult).then_inc(v_xn, 1)

            def table_rows(g, par, i, r):
                v.wait_ge(pe_wh, g * GROUP + r + 1 + 2)
                if r == 0:
                    v.wait_ge(tab_out[par], i * 16 + 16)
                v.tensor_copy(table_rows_sb[par][:, r, 0:D + 2], psW[r % 2][:, 0:D + 2]).then_inc(v_wh, 1)

            def prepare(g, par, i, ahead):
                next_i = i if par == 0 else i + 1
                for r in range(GROUP):
                    normalise(g, par, r)
                    if r >= 2:
                        table_rows(g, par, i, r - 2)
                        if r % 2 == 0:
                            search(g, par, r // 2 - 1)
                        else:
                            find(g, par, r // 2 - 1)
                    if ahead and r >= GROUP // 2:
                        for k in range(2):
                            group_stats(g + 1, 1 - par, next_i, (r - GROUP // 2) * 2 + k)
                if ahead:
                    group_variances(g + 1)
                table_rows(g, par, i, GROUP - 2)
                search(g, par, Q - 1)
                table_rows(g, par, i, GROUP - 1)
                find(g, par, Q - 1)
                v.wait_ge(v_wh, g * GROUP + GROUP + 2)
                v.tensor_copy(s2[:, bass.ds(g * GROUP, GROUP)], table_rows_sb[par][:, :, D])
                v.tensor_copy(s1[:, bass.ds(g * GROUP, GROUP)], table_rows_sb[par][:, :, D + 1]).then_inc(v_s, 1)
                decode_words(g)
                decode_keys(g)
                decode_first(g)
                decode_rest(g)
                decode_second(g)
                decode_keep(g)

            for r in range(GROUP):
                group_stats(0, 0, 0, r)
            group_variances(0)
            if LAG > 2:
                with v.Fori(0, LAG // 2 - 1) as i:
                    for par in range(2):
                        prepare(i * 2 + par, par, i, True)
                    set_gates(i * 2, psC)
            for par in range(2):
                prepare(LAG - 2 + par, par, LAG // 2 - 1, par == 0)
            set_gates(LAG - 2, psC)
            v.wait_ge(a_xT, 2 * NS + 4)
            v.tensor_reduce(xmean[:, :], xsum[:, :, :], AX.X, ALU.add).then_inc(v_w, 1)
            v.wait_ge(v_w, 3 * DH + 2)
            v.tensor_scalar(xmean[:, :], xmean[:, :], 1.0 / N, None, ALU.mult).then_inc(v_w, 1)
            v.wait_ge(pe_w, DH + 3)
            v.tensor_copy(mean_sb[:, 0:D + 1], psW[0][0:1, 0:D + 1]).then_inc(v_wh, 1)
            v.wait_ge(v_s, LAG)

            def indices(u, par):
                v.wait_ge(v_dec, u * VD + VD)
                v.tensor_scalar(idx[par][:, :], keys[:, bass.ds(u, 1), :].rearrange("p o k -> p (o k)"), -1.0, float(N),
                                ALU.mult, ALU.add).then_inc(v_idx, 1)

            def penalties(u):
                v.tensor_scalar(pen[:, 1:K], keys[:, bass.ds(u, 1), 1:K].rearrange("p o k -> p (o k)"), 0.0,
                                MASK_VAL / ALPHA, ALU.is_equal, ALU.mult).then_inc(v_sm, 1)

            def softmax(u, par, i16):
                at = u * VS
                v.wait_ge(gates, u + 1)
                v.nop(nofuse=True)
                more_done = v.value_load(gate[0:1, bass.ds(u, 1), 2:3], min_val=16, max_val=16 + 16 * (K - K_ALL) * NS // 2)
                above_all = v.value_load(gate[0:1, bass.ds(u, 1), 0:1], min_val=0, max_val=1)
                v.wait_ge(v_sm, at + 1)
                v.wait_ge(gat_more[par], more_done)
                v.nop(nofuse=True)
                v.wait_ge(gat[par], i16)
                v.scalar_tensor_tensor(out=sc[:, :], in0=G[par][:, :, D], scalar=s1[:, bass.ds(u, 1)], in1=pen[:, :],
                                       op0=ALU.add, op1=ALU.add).then_inc(v_sm, 1)
                v.wait_ge(v_sm, at + 2)
                v.scalar_tensor_tensor(out=ee[:, :], in0=sc[:, :], scalar=ALPHA, in1=sc[:, :],
                                       op0=ALU.mult, op1=ALU.max).then_inc(v_sm, 1)
                v.wait_ge(v_sm, at + 3)
                v.tensor_reduce(nmx[:, :], ee[:, :], AX.X, ALU.max, negate=True).then_inc(v_sm, 1)
                v.wait_ge(a_p, u + 1)
                v.reciprocal(rden[par][:, :], den[:, :])
                v.wait_ge(pe_o, u + 2)
                v.nop(nofuse=True)

                def diagonals(k0, k1):
                    return v.tensor_tensor(diag[:, k0:k1, :], ident[:, :].unsqueeze(1).to_broadcast([P, k1 - k0, P]),
                                           pr[:, k0:k1].unsqueeze(2).to_broadcast([P, k1 - k0, P]), ALU.mult)
                with v.If(above_all > 0):
                    diagonals(K_ALL, K)
                diagonals(0, K_ALL).then_inc(v_diag, 1)

            def post_min(w):
                v.wait_ge(a_h, w + 3)
                v.tensor_scalar(um[:, :], hh[:, :], 0.0, None, ALU.min).then_inc(v_post, 1)

            def post_elu(w):
                v.wait_ge(a_ex, w + 1)
                v.scalar_tensor_tensor(out=el[:, :], in0=ex[:, :], scalar=-1.0, in1=hh[:, :],
                                       op0=ALU.add, op1=ALU.max).then_inc(v_post, 1)

            def post_x1(w, par, i16):
                v.wait_ge(v_post, w * VP + CR + 2)
                v.wait_ge(xr_in[par], i16)
                v.wait_ge(sc_out[par], i16)
                v.tensor_tensor(x1[par][:, 0:D], el[:, :], xr[par][:, :], ALU.add).then_inc(v_post, 1)

            def post_stats(w, par):
                v.wait_ge(v_post, w * VP + CR + 3)
                v.bn_stats(st2[:, :], x1[par][:, 0:D]).then_inc(v_post, 1)

            def post_mean(w, par):
                v.wait_ge(v_post, w * VP + CR + 4)
                v.nop(nofuse=True)
                v.bn_aggr(x1[par][:, D:D + 2], st2[:, :]).then_inc(v_post, 1)

            def post_variance(w, par, strip):
                v.wait_ge(v_post, w * VP + CR + 5)
                v.tensor_scalar(ve2[:, :], x1[par][:, D + 1:D + 2], EPS, None, ALU.add).then_inc(v_post, 1)
                v.tensor_copy(x1[par][:, D + 2:D + 3], token_no[:, bass.ds(strip, 1)]).then_inc(v_post, 1)

            def post_norm(w, par):
                v.wait_ge(pl_rs2, w + 1)
                v.tensor_scalar(xn2[:, :], x1[par][:, 0:D], x1[par][:, D:D + 1], x1[par][:, D + 1:D + 2],
                                ALU.subtract, ALU.mult).then_inc(v_post, 1)

            def post_logits(w):
                v.wait_ge(pe_lg, w + 2)
                v.tensor_copy(lg[:, :], psL[:, 0:E]).then_inc(v_post, 1)

            def post_best(w):
                v.wait_ge(v_post, w * VP + CR + 9)
                v.nop(nofuse=True)
                v.max(lmax[:, :], lg[:, :]).then_inc(v_post, 1)

            def post_argmax(w):
                v.wait_ge(v_post, w * VP + CR + 10)
                v.nop(nofuse=True)
                v.max_index(lidx[:, :], lmax[:, :], lg[:, :]).then_inc(v_post, 1)

            def post_expert(w):
                v.wait_ge(v_post, w * VP + CR + 11)
                v.tensor_copy(ef[:, :], lidx[:, 0:1]).then_inc(v_post, 1)

            def post_one_hot(w):
                v.wait_ge(v_post, w * VP + CR + 12)
                v.scalar_tensor_tensor(out=oh[:, :], in0=expert_no[:, :], scalar=ef[:, 0:1], in1=direction[:, :],
                                       op0=ALU.is_equal, op1=ALU.mult).then_inc(v_post, 1)

            def post_position(w, par):
                at = w * VP + CR
                v.wait_ge(pe_cum, w + 1)
                v.tensor_tensor(c2[:, :], psC[:, 0:E], count[:, :], ALU.add).then_inc(v_post, 1)
                v.tensor_tensor(count[:, :], psC[:, E:2 * E], count[:, :], ALU.add).then_inc(v_post, 1)
                v.wait_ge(v_post, at + 15)
                v.tensor_tensor_reduce(out=c3[:, :], in0=c2[:, :], in1=oh[:, :], scale=1.0, scalar=0.0,
                                       op0=ALU.mult, op1=ALU.add, accum_out=posf[:, :]).then_inc(v_post, 1)
                v.wait_ge(v_post, at + 16)
                v.scalar_tensor_tensor(out=posu[par][:, :], in0=posf[:, :], scalar=-1.0, in1=posf[:, :],
                                       op0=ALU.mult, op1=ALU.max).then_inc(v_post, 1)

            indices(0, 0)

            def post_all(w, par, i16, strip):
                post_min(w)
                post_elu(w)
                post_x1(w, par, i16)
                post_stats(w, par)
                post_mean(w, par)
                post_variance(w, par, strip)
                post_norm(w, par)
                post_logits(w)
                post_best(w)
                post_argmax(w)
                post_expert(w)
                post_one_hot(w)
                post_position(w, par)

            def half_up(u, par):
                return (u - par) * 8 + 16

            def step(u, par, searching, ahead, post, more):
                w, t = u - 2, u + LAG
                if more:
                    indices(u + 1, 1 - par)
                penalties(u)
                if post:
                    post_min(w)
                if searching:
                    search(t, par, 0)
                if post:
                    post_elu(w)
                if searching:
                    find(t, par, 0)
                if post:
                    post_x1(w, par, half_up(w, par))
                if searching:
                    search(t, par, 1)
                if post:
                    post_stats(w, par)
                if searching:
                    find(t, par, 1)
                if post:
                    post_mean(w, par)
                if searching:
                    search(t, par, 2)
                if post:
                    post_variance(w, par, w)
                if searching:
                    find(t, par, 2)
                    search(t, par, 3)
                if post:
                    post_norm(w, par)
                if searching:
                    find(t, par, 3)
                    decode_words(t)
                    decode_keys(t)
                if post:
                    post_logits(w)
                if searching:
                    decode_first(t)
                if post:
                    post_best(w)
                if searching:
                    decode_rest(t)
                if post:
                    post_argmax(w)
                if searching:
                    decode_second(t)
                if post:
                    post_expert(w)
                if searching:
                    decode_keep(t)
                if post:
                    post_one_hot(w)
                if searching and par:
                    set_gates(t - 1, psP)
                if post:
                    post_position(w, par)
                softmax(u, par, half_up(u, par) * K_ALL)
            rounds(v, step)
            for par in range(2):
                w = NS - 2 + par
                post_all(w, par, half_up(w, par), w)

            v.tensor_reduce(mx[:, :], keys[:, :, K - 1], AX.X, ALU.max).then_inc(v_flag, 1)
            v.tensor_reduce(nmx[:, :], most_words[:, :], AX.X, ALU.max).then_inc(v_flag, 1)
            v.wait_ge(v_flag, 2)
            v.tensor_scalar(flagc[:, 0:1], mx[:, :], 0.0, None, ALU.is_gt).then_inc(v_flag, 1)
            v.tensor_scalar(flagc[:, 1:2], nmx[:, :], NONE_WORD, None, ALU.is_gt).then_inc(v_flag, 1)
            v.wait_ge(pe_flag, 1)
            v.tensor_copy(flag_i[0:1, 0:1], psL[0:1, 0:1]).then_inc(v_flag, 1)
            v.wait_ge(v_flag, 5)
            flag = v.value_load(flag_i[0:1, 0:1], min_val=0, max_val=4 * P)
            with v.If(flag > 0):
                v.wait_ge(v_post, NS * VP + CR)
                v.tensor_copy(count[:, :], region_base[:, :])
                v.engine_nop().then_inc(d_v, 1)

                def dense(t, par):
                    A = t * DV_STRIP + 1
                    with v.Fori(0, NS) as b:
                        at = A + b * DV_A
                        v.tensor_scalar(diag[:, 0, :], ident[:, :], s2[:, bass.ds(b, 1)], None, ALU.mult).then_inc(d_v, 1)
                        v.wait_ge(d_in, (t * NS + b) * 16 + 16)
                        v.tensor_scalar(diag[:, 2, :], adj_block[:, :], 0.0, None, ALU.is_gt).then_inc(d_v, 1)
                        v.wait_ge(d_v, at + 2)
                        v.wait_ge(d_pe, t * 3 * NS + b + 1)
                        v.tensor_scalar(diag[:, 3, :], psC[:, 0:P], s1[:, bass.ds(t, 1)], None, ALU.add).then_inc(d_v, 1)
                        v.tensor_scalar(diag[:, 4, :], diag[:, 2, :], -1.0, -MASK_VAL, ALU.add, ALU.mult).then_inc(d_v, 1)
                        v.wait_ge(d_v, at + 4)
                        v.scalar_tensor_tensor(out=diag[:, 5, :], in0=diag[:, 3, :], scalar=ALPHA, in1=diag[:, 3, :],
                                               op0=ALU.mult, op1=ALU.max).then_inc(d_v, 1)
                        v.wait_ge(d_v, at + 5)
                        v.tensor_tensor(diag[:, 6, :], diag[:, 5, :], diag[:, 2, :], ALU.mult).then_inc(d_v, 1)
                        v.wait_ge(d_v, at + 6)
                        v.tensor_tensor(scores[:, bass.ds(b * P, P)], diag[:, 6, :], diag[:, 4, :], ALU.add).then_inc(d_v, 1)
                        v.wait_ge(d_v, at + 7)
                    at = A + NS * DV_A
                    v.tensor_reduce(mx[:, :], scores[:, :], AX.X, ALU.max).then_inc(d_v, 1)
                    v.wait_ge(d_v, at + 1)
                    v.tensor_scalar(nmx[:, :], mx[:, :], -1.0, None, ALU.mult)
                    v.memset(dacc[:, :], 0.0).then_inc(d_v, 1)
                    with v.Fori(0, NS) as b:
                        v.wait_ge(d_pe, t * 3 * NS + NS + b * 2 + 1)
                        v.tensor_copy(diag[:, 7, :], psT[:, 0:P]).then_inc(d_v, 1)
                        v.wait_ge(d_pe, t * 3 * NS + NS + b * 2 + 2)
                        v.tensor_tensor(dacc[:, :], dacc[:, :], psO[0][:, 0:D], ALU.add).then_inc(d_v, 1)
                    v.wait_ge(d_v, at + 2 + 2 * NS)
                    v.tensor_reduce(den[:, :], dsum[:, :], AX.X, ALU.add)
                    v.drain()
                    v.reciprocal(rden[0][:, :], den[:, :]).then_inc(d_v, 1)
                    post_all(t + NS, par, half_up(t, par) + 8 * NS, t)
                dense_strips(v, dense)

            n = 0

            def planned(ins):
                nonlocal n
                n += 1
                ins.then_inc(v_plan, 1)
                return n

            v.wait_ge(v_plan, planned(v.tensor_tensor(cum[0][:, :], count[:, :], pad_shift[:, :], ALU.add)))
            v.wait_ge(v_plan, planned(v.tensor_copy(pad_i[:, :], cum[0][0:1, :])))
            assert n == PLAN_PADS
            v.wait_ge(v_plan, planned(v.tensor_tensor(nbf[:, :], count[:, :], region_base[:, :], ALU.subtract)))
            v.wait_ge(v_plan, planned(v.tensor_tensor(nbf[:, :], nbf[:, :], direction[:, :], ALU.mult)))
            v.wait_ge(v_plan, planned(v.tensor_scalar(nbi[:, :], nbf[:, :], float(P - 1), None, ALU.add)))
            v.wait_ge(v_plan, planned(v.tensor_scalar(nbj[:, :], nbi[:, :], 7, None, ALU.arith_shift_right)))
            v.wait_ge(v_plan, planned(v.tensor_copy(nbf[:, :], nbj[:, :])))
            v.wait_ge(v_plan, planned(v.tensor_copy(cum[0][:, :], nbj[:, :])))
            src = 0
            for shift in (1, 2, 4, 8, 16):
                v.wait_ge(v_plan, planned(v.tensor_copy(cum[1 - src][:, 0:shift], cum[src][:, 0:shift])))
                v.wait_ge(v_plan, planned(v.tensor_tensor(cum[1 - src][:, shift:E], cum[src][:, shift:E], cum[src][:, 0:E - shift],
                                        ALU.add)))
                src = 1 - src
            v.wait_ge(v_plan, planned(v.tensor_scalar(le[:, :], cum[src][:, :], part_no[:, 0:1], None, ALU.is_le)))
            v.wait_ge(v_plan, planned(v.tensor_reduce(plan[:, 0:1], le[:, :], AX.X, ALU.add)))

            def pick(col, row, of):
                v.wait_ge(v_plan, planned(v.tensor_tensor_reduce(out=le2[:, :], in0=row[:, :], in1=of[:, :], scale=1.0, scalar=0.0,
                                               op0=ALU.mult, op1=ALU.add, accum_out=plan[:, col:col + 1])))
            pick(1, le, nbf)
            v.wait_ge(v_plan, planned(v.tensor_scalar(plan[:, 2:3], plan[:, 1:2], part_no[:, 0:1], -float(P), ALU.subtract, ALU.mult)))
            v.wait_ge(v_plan, planned(v.tensor_scalar(le[:, :], expert_no[:, :], plan[:, 0:1], None, ALU.is_equal)))
            pick(3, le, direction)
            pick(4, le, first_block)
            v.wait_ge(v_plan, planned(v.tensor_scalar(plan[:, 5:6], plan[:, 0:1], float(E), float(NULL_ROW), ALU.is_ge, ALU.mult)))
            v.wait_ge(v_plan, planned(v.tensor_tensor(plan[:, 2:3], plan[:, 2:3], plan[:, 3:4], ALU.mult)))
            v.wait_ge(v_plan, planned(v.tensor_tensor(plan[:, 4:5], plan[:, 4:5], plan[:, 5:6], ALU.add)))
            v.wait_ge(v_plan, planned(v.tensor_tensor(plan[:, 6:7], plan[:, 2:3], plan[:, 4:5], ALU.add)))
            assert n == PLAN_ROWS
            v.wait_ge(pe_plan, 1)
            v.wait_ge(v_plan, planned(v.tensor_copy(plan_i[:, 0:P], psC[0:1, 0:P])))
            v.wait_ge(v_plan, planned(v.tensor_scalar(plan_i[:, P:2 * P], psC[0:1, P:2 * P], float(E - 1), None, ALU.min)))
            assert n == PLAN_STEPS

            def block_norm(b, r, turn):
                v.wait_ge(xb_in[r], turn * 16 + 16)
                if not isinstance(b, int) or b >= 2:
                    v.wait_ge(pe_xb, b - 1)
                v.tensor_scalar(xnb[r % 2][:, :], xb[r][:, 0:D], xb[r][:, D:D + 1], xb[r][:, D + 1:D + 2],
                                ALU.subtract, ALU.mult).then_inc(v_xb, 1)

            def block_rows(b, r, turn):
                v.wait_ge(pe_y, b + 1)
                if not isinstance(b, int) or b > 1:
                    v.wait_ge(y_out[r % 2], (b - r % 2) * 8)
                v.tensor_copy(tok[r % 2][:, :], xb[r][:, D + 2:D + 3])
                v.scalar_tensor_tensor(out=yb[r % 2][:, :], in0=psO[r % 2][:, 0:D], scalar=0.0, in1=xb[r][:, 0:D],
                                       op0=ALU.max, op1=ALU.add).then_inc(v_y, 1)
            def copy_w2(b, r, turn):
                e = v.value_load(plan_i[0:1, bass.ds(b + P, 1)], min_val=0, max_val=E - 1)
                v.tensor_copy(w2_b[r % 2][:, :], w2_sb[:, bass.ds(e, 1), :].rearrange("p o n -> p (o n)")).then_inc(v_w2, 1)
            v.wait_ge(ffn_in, 16 * 4)
            blocks_loop(v, [(copy_w2, 2), (block_norm, 0), (block_rows, 3)])

        @block.tensor
        def _(pe):
            pe.sem_inc(pe_xT, 2)
            pe.sem_inc(pe_wh, 2)
            pe.sem_inc(pe_o, 2)
            pe.sem_inc(pe_lg, 1)
            pe.wait_ge(const_in, 16 * 5)
            pe.wait_ge(consts, 14)
            pe.nop(nofuse=True)
            for fh in range(DH):
                if fh:
                    pe.wait_ge(v_w, fh)
                    pe.nop(nofuse=True)
                for kh in range(DH):
                    mm = pe.transpose(psT[:, kh * P:(kh + 1) * P], w_raw[:, kh, fh * P:(fh + 1) * P], ident[:, :])
                mm.then_inc(pe_w, 1)
            pe.wait_ge(v_w, DH)
            pe.nop(nofuse=True)
            for kh in range(DH):
                for fh in range(DH):
                    mm = pe.matmul(psL[:, 2 * kh:2 * kh + 2], w_t[:, fh, kh * P:(kh + 1) * P], a_sb[:, fh, :],
                                   start=(fh == 0), stop=(fh == DH - 1))
            mm.then_inc(pe_w, 1)
            for h in range(DH):
                mm = pe.transpose(psC[:, h * E:(h + 1) * E], rw_sb[:, h * P:(h + 1) * P], ident[0:E, 0:E])
            mm.then_inc(pe_w, 1)
            pe.wait_ge(v_w, 3 * DH)

            def transposes(s, r):
                pe.wait_ge(v_xn, s + 1 + 2 * GROUP)
                pe.wait_ge(a_xT, 2 * s + 2)
                pe.nop(nofuse=True)
                for h in range(DH):
                    mm = pe.transpose(psXn[r % 2][:, h * P:(h + 1) * P], xn[r % 2][:, h * P:(h + 1) * P], ident[:, :])
                mm.then_inc(pe_xT, 1)

            def table_rows(s, r):
                pe.wait_ge(a_xT, 2 * s + 6)
                pe.wait_ge(v_wh, s + 1)
                pe.nop(nofuse=True)
                for h in range(DH):
                    mm = pe.matmul(psW[r % 2][:, 0:D + 2], xT[r % 2][:, h, :], w_aug[:, h, :],
                                   start=(h == 0), stop=(h == DH - 1))
                mm.then_inc(pe_wh, 1)

            def gate_rows(t, bank):
                pe.wait_ge(v_gs, t * 2 + 1)
                pe.matmul(bank[0:1, 0:4], ones_b[:, 0:1], many[:, :, :].rearrange("p t k -> p (t k)"),
                          start=True, stop=True).then_inc(pe_gate, 2)

            with pe.Fori(0, LAG // 2) as i:
                for par in range(2):
                    s = (i * 2 + par) * GROUP
                    for r in range(GROUP):
                        transposes(s + r, r)
                        if r:
                            table_rows(s + r - 1, r - 1)
                    table_rows(s + GROUP - 1, GROUP - 1)
                gate_rows(i * 2, psC)
            pe.wait_ge(v_w, 3 * DH + 3)
            pe.wait_ge(v_wh, NS + 2)
            pe.nop(nofuse=True)
            for h in range(DH):
                mm = pe.matmul(psW[0][0:1, 0:D + 2], xmean[:, h:h + 1], w_aug[:, h, :],
                               start=(h == 0), stop=(h == DH - 1))
            mm.then_inc(pe_w, 1)

            def weighted_sum(u, par):
                pe.wait_ge(v_diag, u + 1)
                pe.wait_ge(a_h, u + 1)
                pe.nop(nofuse=True)

                def products(k0, k1):
                    for k in range(k0, k1):
                        mm = pe.matmul(psO[par][:, 0:D], diag[:, k, :], G[par][:, k, 0:D],
                                       start=(k == 0), stop=(k == K_ALL - 1))
                    return mm
                above_all = pe.value_load(gate[0:1, bass.ds(u, 1), 0:1], min_val=0, max_val=1)
                products(0, 1)
                with pe.If(above_all > 0):
                    products(K_ALL, K_MID)
                    above_mid = pe.value_load(gate[0:1, bass.ds(u, 1), 1:2], min_val=0, max_val=1)
                    with pe.If(above_mid > 0):
                        products(K_MID, K)
                products(1, K_ALL).then_inc(pe_o, 1)

            def post_transposes(w):
                pe.wait_ge(v_post, w * VP + CR + 8)
                pe.wait_ge(a_x2, w + 1)
                pe.nop(nofuse=True)
                for h in range(DH):
                    mm = pe.transpose(psT[:, h * P:(h + 1) * P], xn2[:, h * P:(h + 1) * P], ident[:, :])
                mm.then_inc(pe_t2, 1)

            def logits(w):
                pe.wait_ge(a_x2, w + 2)
                pe.nop(nofuse=True)
                for h in range(DH):
                    pe.matmul(psL[:, 0:E], xT2[:, h, :], rw_t[:, h, :], start=(h == 0), stop=False)
                pe.matmul(psL[:, 0:E], ones_f[0:1, :], rb_sb[:, :], start=False, stop=True).then_inc(pe_lg, 1)

            def ranks(w):
                pe.wait_ge(v_post, w * VP + CR + 13)
                pe.matmul(psC[:, 0:E], before[:, :], oh[:, :], start=True, stop=True)
                pe.matmul(psC[:, E:2 * E], ones_b[:, :], oh[:, :], start=True, stop=True).then_inc(pe_cum, 1)

            pe.wait_ge(v_w, 3 * DH + 1)

            def step(u, par, searching, ahead, post, more):
                if post:
                    post_transposes(u - 2)
                    logits(u - 2)
                if searching and par:
                    gate_rows(u - 1 + LAG, psP)
                if post:
                    ranks(u - 2)
                weighted_sum(u, par)
            rounds(pe, step)
            for par in range(2):
                post_transposes(NS - 2 + par)
                logits(NS - 2 + par)
                ranks(NS - 2 + par)

            pe.wait_ge(v_flag, 4)
            pe.matmul(psL[0:1, 0:1], flagc[:, 0:1], ones_f[:, 0:1], start=True, stop=False)
            pe.matmul(psL[0:1, 0:1], flagc[:, 1:2], ones_f[:, 0:1], start=False, stop=True).then_inc(pe_flag, 1)
            pe.wait_ge(v_flag, 5)
            flag = pe.value_load(flag_i[0:1, 0:1], min_val=0, max_val=4 * P)
            with pe.If(flag > 0):
                def dense(t, par):
                    with pe.Fori(0, NS) as b:
                        pe.wait_ge(d_v, t * DV_STRIP + 1 + b * DV_A + 1)
                        pe.matmul(psC[:, 0:P], ones_f[:, :], diag[:, 0, :], start=True, stop=True).then_inc(d_pe, 1)
                    with pe.Fori(0, NS) as b:
                        pe.wait_ge(d_a, t * NS + b + 1)
                        pe.transpose(psT[:, 0:P], diag[:, 1, :], ident[:, :]).then_inc(d_pe, 1)
                        pe.wait_ge(d_v, t * DV_STRIP + 1 + NS * DV_A + 2 + 2 * b + 1)
                        pe.wait_ge(d_wh, (t * NS + b) * 16 + 16)
                        pe.matmul(psO[0][:, 0:D], diag[:, 7, :], G[0][:, 0, 0:D], start=True, stop=True).then_inc(d_pe, 1)
                    post_transposes(t + NS)
                    logits(t + NS)
                    ranks(t + NS)
                dense_strips(pe, dense)

            pe.wait_ge(v_plan, PLAN_ROWS)
            pe.nop(nofuse=True)
            for j, col in ((0, 6), (1, 0)):
                mm = pe.matmul(psC[0:1, j * P:(j + 1) * P], plan[:, col:col + 1], ident[:, :], start=True, stop=True)
            mm.then_inc(pe_plan, 1)
            def block_transposes(b, r, turn):
                pe.wait_ge(v_xb, b + 1)
                for h in range(DH):
                    mm = pe.transpose(psX[r % 2][:, h * P:(h + 1) * P], xnb[r % 2][:, h * P:(h + 1) * P], ident[:, :])
                mm.then_inc(pe_xb, 1)

            def block_hidden(b, r, turn):
                pe.wait_ge(a_xb, b + 1)
                for h in range(DH):
                    mm = pe.matmul(psH[r % 2][0:H, 0:P], w1_b[r % 2][:, h, :], xTb[r % 2][:, h, :],
                                   start=(h == 0), stop=(h == DH - 1))
                mm.then_inc(pe_h, 1)

            def block_output(b, r, turn):
                pe.wait_ge(a_hT, b + 1)
                if isinstance(b, int) and b + 2 >= BLOCKS:
                    pe.wait_ge(v_w2, b + 1)
                    pe.nop(nofuse=True)
                pe.matmul(psO[r % 2][:, 0:D], hT[r % 2][:, :], w2_b[r % 2][:, :],
                          start=True, stop=True).then_inc(pe_y, 1)
            blocks_loop(pe, [(block_transposes, 1), (block_hidden, 2), (block_output, 3)])


def _int32(bits):
    return bits - (1 << 32) if bits >> 31 else bits


def _word_of_signs(bits):
    import numpy as np
    return abs(float(np.array([bits], np.uint32).view(np.float32)[0]))


_INS = ["x", "adj", "L0_gnn_W", "L0_gnn_a", "L0_ffn_router_w", "L0_ffn_router_b",
        "L0_ffn_W1", "L0_ffn_b1", "L0_ffn_W2", "L0_ffn_b2"]


def kernel(**inputs):
    import numpy as np
    import concourse.bacc as bacc
    from concourse.bass_utils import run_bass_kernel_spmd as run

    nc = bacc.Bacc("TRN2", target_bir_lowering=False, num_devices=1)
    arrays, args = {}, []
    for name in _INS:
        a = np.ascontiguousarray(inputs[name])
        arrays[f"in_{name}"] = a
        args.append(nc.dram_tensor(f"in_{name}", a.shape, mybir.dt.from_np(a.dtype), kind="ExternalInput").ap())
    N = arrays["in_x"].shape[0]
    args.append(nc.dram_tensor("out_x", (N, D), mybir.dt.float32, kind="ExternalOutput").ap())
    args.append(nc.dram_tensor("wh_table", (N + 1, ROW), mybir.dt.float32, kind="Internal").ap())
    args.append(nc.dram_tensor("regions", (E // 2 * (N + 2 * P) + P, ROW), mybir.dt.float32, kind="Internal").ap())
    gat_moe(nc, *args)
    return run(nc, [arrays], core_ids=[0]).results[0]["out_x"]
```

```python
import concourse.bass as bass
from concourse import mybir
from collections import namedtuple
from contextlib import ExitStack

P = 128
D = 256
DH = D // P
E = 32
H = 64
ROW = 260
Q = 4
TOP = 8
K = 16
K_ALL = 10
K_MID = 12
RING = 6
KEPT = 4
GROUP = 8
EPS = 1e-5
ALPHA = 0.2
MASK_VAL = -9000000000000000.0
NO_TOKEN = 1.0e6

Does = namedtuple("Does", "ahead search attend fetch load post place")


def gat_moe(nc, x, adj, gW, ga, rw, rb, W1, b1, W2, b2, out, table, region):
    f32, i32, u32 = mybir.dt.float32, mybir.dt.int32, mybir.dt.uint32
    bf16, f8 = mybir.dt.bfloat16, mybir.dt.float8e4
    ALU, ACT, AX = mybir.AluOpType, mybir.ActivationFunctionType, mybir.AxisListType

    N = x.shape[0]
    NS = N // P
    LAG = NS // GROUP
    C = N // Q
    WORDS = C // KEPT
    CAND = Q * TOP * KEPT
    SPAN = N + 2 * P
    BLOCKS = NS + E - 1
    NULL_ROW = E // 2 * SPAN
    assert RING % 2 == 0 and BLOCKS // RING <= E and LAG % 2 == 0 and NS % (2 * GROUP) == 0 and NS >= LAG + 4 and 3 * RING <= BLOCKS <= P

    ctx = ExitStack()
    with ctx:
        def sb(name, shape, dt=f32):
            return ctx.enter_context(nc.sbuf_tensor(name, shape, dt))

        def ps(name, shape, dt=f32):
            return ctx.enter_context(nc.psum_tensor(name, shape, dt))

        def sem(name):
            return ctx.enter_context(nc.semaphore(name))

        ident = sb("ident", [P, P])
        ones_f = sb("ones_f", [P, P])
        ones_b = sb("ones_b", [P, P], bf16)
        before = sb("before", [P, P], bf16)
        byte_sign = sb("byte_sign", [P, Q * TOP, KEPT], i32)
        code_base = sb("code_base", [P, Q, TOP, KEPT])
        expert_no = sb("expert_no", [P, E])
        region_base = sb("region_base", [P, E])
        direction = sb("direction", [P, E])
        first_block = sb("first_block", [P, E])
        pad_shift = sb("pad_shift", [P, E])
        token_no = sb("token_no", [P, NS])
        minus_half = sb("minus_half", [P, GROUP])
        part_no = sb("part_no", [P, 1])
        pad_row = sb("pad_row", [P, ROW])

        w_aug = sb("w_aug", [P, DH, D + 2])
        w_raw = sb("w_raw", [P, DH, D])
        w_t = sb("w_t", [P, DH, D])
        a_sb = sb("a_sb", [P, DH, 2])
        rw_sb = sb("rw_sb", [E, D])
        rw_t = sb("rw_t", [P, DH, E])
        rb_sb = sb("rb_sb", [1, E])
        w1_sb = sb("w1_sb", [P, E, DH, H])
        b1_t = sb("b1_t", [H, E])
        w2_sb = sb("w2_sb", [H + 1, E, D])

        w1_flat = w1_sb[:, :, :, :].rearrange("p e h n -> p (e h n)")
        xg = [w1_flat[:, i * GROUP * D:(i + 1) * GROUP * D].rearrange("p (r d) -> p r d", r=GROUP) for i in range(2)]
        st = sb("st", [P, GROUP, 6])
        mv = sb("mv", [P, GROUP, 2])
        ve = sb("ve", [P, GROUP])
        rs = sb("rs", [P, GROUP])
        xn = [sb(f"xn{i}", [P, D]) for i in range(2)]
        xT = [sb(f"xT{i}", [P, DH, P]) for i in range(2)]
        xsum = sb("xsum", [P, DH, NS])
        xmean = sb("xmean", [P, DH])
        mean_sb = sb("mean_sb", [1, ROW])
        s1 = sb("s1", [P, NS])
        s2 = sb("s2", [P, NS])

        raw_all = sb("raw_all", [P, Q * C], i32)
        raw = [raw_all[:, q * C:(q + 1) * C] for q in range(Q)]
        sg = [[sb(f"sg{i}{q}", [P, C], f8) for q in range(Q)] for i in range(2)]
        top_word = sb("top_word", [P, Q, TOP])
        top_pos = sb("top_pos", [P, Q, TOP], u32)
        bits = sb("bits", [P, Q * TOP, KEPT], i32)
        code = sb("code", [P, CAND])
        key = sb("key", [P, CAND])
        key2 = sb("key2", [P, CAND])
        key16 = sb("key16", [P, K])
        keys = sb("keys", [P, NS, K])
        many = sb("many", [P, 2, 2], bf16)
        more = sb("more", [1, 2, 2])
        more_sum = [sb(f"more_sum{i}", [1, 2]) for i in range(2)]
        gate = sb("gate", [1, NS, 4], i32)
        most_words = sb("most_words", [P, Q])

        idx = [sb(f"idx{i}", [P, K], u32) for i in range(2)]
        G = [sb(f"G{i}", [P, K, ROW]) for i in range(2)]
        sc = sb("sc", [P, K])
        pen = sb("pen", [P, K])
        ee = sb("ee", [P, K])
        mx = sb("mx", [P, 1])
        nmx = sb("nmx", [P, 1])
        pr = sb("pr", [P, K])
        den = sb("den", [P, 1])
        rden = [sb(f"rden{i}", [P, 1]) for i in range(2)]
        diag = sb("diag", [P, K, P])

        table_rows_sb = [G[0][:, i * GROUP:(i + 1) * GROUP, :] for i in range(2)]

        xr = [sb(f"xr{i}", [P, D]) for i in range(2)]
        hh = sb("hh", [P, D])
        um = sb("um", [P, D])
        ex = sb("ex", [P, D])
        el = sb("el", [P, D])
        st2 = sb("st2", [P, 6])
        ve2 = sb("ve2", [P, 1])
        x1 = [sb(f"x1{i}", [P, ROW]) for i in range(2)]
        xn2 = sb("xn2", [P, D])
        xT2 = sb("xT2", [P, DH, P])
        lg = sb("lg", [P, E])
        lmax = sb("lmax", [P, TOP])
        lidx = sb("lidx", [P, TOP], u32)
        ef = sb("ef", [P, 1])
        oh = sb("oh", [P, E], bf16)
        count = sb("count", [P, E])
        c2 = sb("c2", [P, E])
        c3 = sb("c3", [P, E])
        posf = sb("posf", [P, 1])
        posu = [sb(f"posu{i}", [P, 1], u32) for i in range(2)]

        nbi = sb("nbi", [P, E], i32)
        nbj = sb("nbj", [P, E], i32)
        nbf = sb("nbf", [P, E])
        cum = [sb(f"cum{i}", [P, E]) for i in range(2)]
        le = sb("le", [P, E])
        le2 = sb("le2", [P, E])
        plan = sb("plan", [P, 8])
        plan_i = sb("plan_i", [1, 2 * P], i32)
        pad_i = sb("pad_i", [1, E], i32)
        steps_f = sb("steps_f", [1, 2])
        turn_of = sb("turn_of", [1, E])
        steps_i = sb("steps_i", [1, 4], i32)

        scores = raw_all[:, :].bitcast(f32)
        adj_block = sb("adj_block", [P, P], i32)
        dsum = sb("dsum", [P, NS])
        dacc = sb("dacc", [P, D])
        flagc = sb("flagc", [P, 2])
        flag_i = sb("flag_i", [1, 2], i32)

        xb = [sb(f"xb{i}", [P, ROW]) for i in range(RING)]
        xnb = [sb(f"xnb{i}", [P, D]) for i in range(2)]
        xTb = [sb(f"xTb{i}", [P, DH, P]) for i in range(2)]
        w1_b = [sb(f"w1_b{i}", [P, DH, H]) for i in range(2)]
        b1_b = [sb(f"b1_b{i}", [H, 1]) for i in range(2)]
        w2_b = [sb(f"w2_b{i}", [H + 1, D]) for i in range(2)]
        hT = [sb(f"hT{i}", [H + 1, P]) for i in range(2)]
        yb = [sb(f"yb{i}", [P, D]) for i in range(2)]
        tok = [sb(f"tok{i}", [P, 1], u32) for i in range(2)]

        psP = ps("psP", [P, 512])
        psW = [ps(f"psW{i}", [P, 512]) for i in range(2)]
        psO = [ps(f"psO{i}", [P, 512]) for i in range(2)]
        psT = ps("psT", [P, 512])
        psL = ps("psL", [P, 512])
        psC = ps("psC", [P, 512])
        psXn = [psP, psO[0]]
        psX = [psP, psW[0]]
        psH = [psL, psW[1]]

        const_in = sem("const_in")
        ffn_in = sem("ffn_in")
        consts = sem("consts")
        v_const = sem("v_const")
        pe_w = sem("pe_w")
        v_w = sem("v_w")
        xg_in = [sem(f"xg_in{i}") for i in range(2)]
        v_st = sem("v_st")
        v_var = sem("v_var")
        pl_rs = sem("pl_rs")
        v_xn = sem("v_xn")
        pe_xT = sem("pe_xT")
        a_xT = sem("a_xT")
        pe_wh = sem("pe_wh")
        v_wh = sem("v_wh")
        v_s = sem("v_s")
        tab_out = [sem(f"tab_out{i}") for i in range(2)]
        mean_out = sem("mean_out")

        raw_in = [sem(f"raw_in{q}") for q in range(Q)]
        a_sg = sem("a_sg")
        v_top = sem("v_top")
        v_find = sem("v_find")
        v_dec = sem("v_dec")
        v_idx = sem("v_idx")
        v_gs = sem("v_gs")
        pe_gate = sem("pe_gate")
        gates = sem("gates")
        gat = [sem(f"gat{i}") for i in range(2)]
        gat_more = [sem(f"gat_more{i}") for i in range(2)]
        v_sm = sem("v_sm")
        a_p = sem("a_p")
        v_diag = sem("v_diag")
        pe_o = sem("pe_o")
        a_h = sem("a_h")
        v_post = sem("v_post")
        v_place = sem("v_place")
        a_ex = sem("a_ex")
        pl_rs2 = sem("pl_rs2")
        pe_t2 = sem("pe_t2")
        a_x2 = sem("a_x2")
        pe_lg = sem("pe_lg")
        pe_cum = sem("pe_cum")
        xr_in = [sem(f"xr_in{i}") for i in range(2)]
        sc_out = [sem(f"sc_out{i}") for i in range(2)]

        v_flag = sem("v_flag")
        pe_flag = sem("pe_flag")
        d_in = sem("d_in")
        d_wh = sem("d_wh")
        d_v = sem("d_v")
        d_pe = sem("d_pe")
        d_a = sem("d_a")

        v_plan = sem("v_plan")
        pe_plan = sem("pe_plan")
        pad_out = sem("pad_out")
        pad_out_pool = sem("pad_out_pool")
        xb_in = [sem(f"xb_in{i}") for i in range(RING)]
        v_xb = sem("v_xb")
        pe_xb = sem("pe_xb")
        a_xb = sem("a_xb")
        v_w2 = sem("v_w2")
        a_w1 = sem("a_w1")
        pe_h = sem("pe_h")
        a_hT = sem("a_hT")
        pe_y = sem("pe_y")
        v_y = sem("v_y")
        y_out = [sem(f"y_out{i}") for i in range(2)]

        VP = 8
        VE = 9
        VD = 8
        VS = 4
        NONE_WORD = -float(_word_of_signs(0xB8B8B8B8))

        def groups(eng, step):
            def pair(i):
                for par in range(2):
                    step(i * 2 + par, par, i, i * 2 + par > 0, i * 2 + par + 1 < LAG)
            pair(0)
            if LAG > 4:
                with eng.Fori(1, LAG // 2 - 1) as i:
                    for par in range(2):
                        step(i * 2 + par, par, i, True, True)
            if LAG > 2:
                pair(LAG // 2 - 1)

        def does(u):
            return Does(ahead=u + LAG + 1 < NS, search=u + LAG < NS, attend=u < NS, fetch=u + 1 < NS, load=1 <= u < NS + 1,
                        post=2 <= u < NS + 2, place=3 <= u < NS + 3)

        def rounds(eng, step):
            def peeled(u0, u1):
                for u in range(u0, u1):
                    step(u, u % 2, does(u))

            def loop(u0, u1):
                if u1 > u0:
                    with eng.Fori(u0 // 2, u1 // 2) as i:
                        for par in range(2):
                            step(i * 2 + par, par, does(u0))
            peeled(0, 4)
            loop(4, NS - LAG - 2)
            peeled(max(4, NS - LAG - 2), NS - LAG)
            loop(NS - LAG, NS - 2)
            peeled(NS - 2, NS + 3)

        def dense_strips(eng, step):
            with eng.Fori(0, NS // 2) as i:
                for par in range(2):
                    step(i * 2 + par, par)

        DV_A = 7
        DV_STRIP = NS * DV_A + 2 + NS * 2 + 1
        PLAN_PADS = 2
        PLAN_ROWS = PLAN_PADS + 27
        PLAN_STEPS = PLAN_ROWS + 8
        TURNS = BLOCKS // RING
        TAIL = 3

        def blocks_loop(eng, stages):
            def step(i, r, turn):
                for stage, lag in stages:
                    if not isinstance(i, int) or 0 <= i - lag < BLOCKS:
                        stage(i - lag, (r - lag) % RING, turn if lag <= r else turn - 1)
            eng.wait_ge(v_plan, PLAN_STEPS)
            eng.nop(nofuse=True)
            steps = eng.value_load(steps_i[0:1, 0:1], min_val=1, max_val=BLOCKS + TAIL)
            for r in range(RING):
                step(r, r, 0)
            with eng.Fori(1, TURNS) as turn:
                with eng.If(steps > turn * RING):
                    for r in range(RING):
                        step(turn * RING + r, r, turn)
            with eng.If(steps > TURNS * RING):
                for i in range(TURNS * RING, BLOCKS + TAIL):
                    step(i, i % RING, i // RING)
            return steps

        block = ctx.enter_context(nc.Block())

        def pad_experts(eng, first, end, done):
            eng.wait_ge(v_plan, PLAN_PADS)
            eng.nop(nofuse=True)
            with eng.Fori(first // 2, end // 2) as pair:
                rows = [eng.value_load(pad_i[0:1, bass.ds(pair * 2 + k, 1)], min_val=0, max_val=NULL_ROW) for k in range(2)]
                for row in rows:
                    eng.dma_start(region[bass.ds(row, P), :], pad_row[:, :]).then_inc(done, 16)

        @block.sync
        def _(sp):
            sp.dma_start(w_raw[:, :, :], gW.rearrange("(h p) n -> p h n", p=P)).then_inc(const_in, 16)

            def load_group(g, par, i):
                sp.wait_ge(v_xn, g * GROUP + GROUP)
                sp.nop(nofuse=True)
                sp.dma_start(xg[par][:, :, :],
                             x[bass.ds(g * GROUP * P, GROUP * P), :].rearrange("(r p) d -> p r d", p=P)
                             ).then_inc(xg_in[par], 16)

            def load_strip(t):
                for q in range(Q):
                    sp.wait_ge(a_sg, t * Q + q + 1)
                    sp.nop(nofuse=True)
                    sp.dma_start(raw[q], adj[bass.ds(t * P, P), q * C:(q + 1) * C]).then_inc(raw_in[q], 16)

            def load_x(v, par):
                sp.wait_ge(v_post, v * VP + 3)
                sp.nop(nofuse=True)
                sp.dma_start(xr[par][:, :], x[bass.ds(v * P, P), :]).then_inc(xr_in[par], 16)

            def group(g, par, i, behind, ahead):
                load_group(g, par, i)
                load_strip(g)
            groups(sp, group)
            load_strip(LAG)

            def load_weights(u):
                sp.wait_ge(v_post, (u - 1) * VP + 3)
                sp.nop(nofuse=True)
                half = E // 2
                if u < NS:
                    e = (u - NS + 2) * half
                    sp.dma_start(w2_sb[0:H, e:e + half, :], W2[e:e + half].rearrange("e k n -> k e n")).then_inc(ffn_in, 16)
                if u == NS - 1:
                    sp.dma_start(w2_sb[H:H + 1, :, :], b2.rearrange("(o e) n -> o e n", o=1)).then_inc(ffn_in, 16)
                    with nc.allow_non_contiguous_dma(reason="a small matrix, transposed"):
                        sp.dma_start(b1_t[:, :], b1.rearrange("e n -> n e")).then_inc(ffn_in, 16)
                sp.wait_ge(v_xn, NS + 2 * GROUP)
                sp.nop(nofuse=True)
                quarter = E // 4
                for part in {NS: (0,), NS + 1: (1,), NS + 2: (2, 3)}.get(u, ()):
                    e = part * quarter
                    sp.dma_start(w1_sb[:, e:e + quarter, :, :].rearrange("p e h n -> p (e h) n"),
                                 W1[e:e + quarter].rearrange("e (h p) n -> p (e h) n", p=P)).then_inc(ffn_in, 16)

            def step(u, par, do):
                if do.ahead:
                    load_strip(u + LAG + 1)
                if do.load:
                    load_x(u - 1, 1 - par)
                if isinstance(u, int) and u >= NS - 2:
                    load_weights(u)
            rounds(sp, step)

            sp.wait_ge(v_flag, 5)
            sp.nop(nofuse=True)
            flag = sp.value_load(flag_i[0:1, 0:1], min_val=0, max_val=4 * P)
            with sp.If(flag > 0):
                def dense(t, par):
                    with sp.Fori(0, NS) as b:
                        sp.wait_ge(d_v, t * DV_STRIP + b * DV_A + 1)
                        sp.nop(nofuse=True)
                        sp.dma_start(adj_block[:, :], adj[bass.ds(t * P, P), bass.ds(b * P, P)]).then_inc(d_in, 16)
                        sp.wait_ge(d_in, (t * NS + b) * 16 + 16)
                        sp.nop(nofuse=True)
                    with sp.Fori(0, NS) as b:
                        sp.wait_ge(d_v, t * DV_STRIP + NS * DV_A + 2 + b * 2 + 1)
                        sp.nop(nofuse=True)
                        sp.dma_start(G[0][:, 0, :], table[bass.ds(b * P, P), :]).then_inc(d_wh, 16)
                        sp.wait_ge(d_wh, (t * NS + b) * 16 + 16)
                        sp.nop(nofuse=True)
                    sp.wait_ge(v_post, (t + NS) * VP + 3)
                    sp.nop(nofuse=True)
                    sp.dma_start(xr[par][:, :], x[bass.ds(t * P, P), :]).then_inc(xr_in[par], 16)
                dense_strips(sp, dense)
                sp.wait_ge(sc_out[0], 16 + 16 * NS)
                sp.nop(nofuse=True)
                sp.wait_ge(sc_out[1], 16 + 16 * NS)
                sp.nop(nofuse=True)

            pad_experts(sp, 0, 10, pad_out)
            sp.wait_ge(v_plan, PLAN_STEPS)
            sp.nop(nofuse=True)
            sp.wait_ge(pad_out, 16 * 20)
            sp.nop(nofuse=True)
            sp.wait_ge(pad_out_pool, 16 * (E - 20))
            sp.nop(nofuse=True)
            sp.wait_ge(sc_out[0], 16 + 8 * NS)
            sp.nop(nofuse=True)
            sp.wait_ge(sc_out[1], 16 + 8 * NS)
            sp.nop(nofuse=True)

            def load_block(b, r, turn):
                row = sp.value_load(plan_i[0:1, bass.ds(b, 1)], min_val=0, max_val=NULL_ROW)
                sp.wait_ge(v_y, b + 1)
                sp.nop(nofuse=True)
                sp.dma_start(xb[r][:, :], region[bass.ds(row, P), :]).then_inc(xb_in[r], 16)
            blocks_loop(sp, [(load_block, 0)])

        @block.gpsimd
        def _(pool):
            pool.memset(ones_f[:, :], 1.0).then_inc(consts, 1)
            pool.memset(ones_b[:, :], 1.0).then_inc(consts, 1)
            pool.memset(ident[:, :], 0.0).then_inc(consts, 1)
            pool.memset(minus_half[:, :], -0.5).then_inc(consts, 1)
            pool.wait_ge(consts, 4)
            pool.nop(nofuse=True)
            pool.affine_select(out=ident[:, :], in_=ident[:, :], compare_op=ALU.not_equal, fill=1.0, base=0,
                               pattern=[[-1, P]], channel_multiplier=1).then_inc(consts, 1)
            pool.affine_select(out=before[:, :], in_=ones_b[:, :], compare_op=ALU.is_gt, fill=0.0, base=0,
                               pattern=[[1, P]], channel_multiplier=-1).then_inc(consts, 1)
            pool.iota(code_base[:, :, :, :], [[-C, Q], [0, TOP], [-1, KEPT]], base=N, channel_multiplier=0,
                      allow_small_or_imprecise_dtypes=True).then_inc(consts, 1)
            pool.iota(expert_no[:, :], [[1, E]], base=0, channel_multiplier=0,
                      allow_small_or_imprecise_dtypes=True).then_inc(consts, 1)
            for tile, at, step_odd in ((region_base, 0, SPAN - 1), (direction, 1, -2),
                                       (first_block, 0, SPAN - P), (pad_shift, 0, 1 - P)):
                by_pair = SPAN if tile in (region_base, first_block) else 0
                pool.iota(tile[:, :], [[by_pair, E // 2], [step_odd, 2]], base=at, channel_multiplier=0,
                          allow_small_or_imprecise_dtypes=True).then_inc(consts, 1)
            pool.iota(token_no[:, :], [[P, NS]], base=0, channel_multiplier=1,
                      allow_small_or_imprecise_dtypes=True).then_inc(consts, 1)
            pool.iota(part_no[:, :], [[0, 1]], base=0, channel_multiplier=1,
                      allow_small_or_imprecise_dtypes=True).then_inc(consts, 1)
            pool.wait_ge(v_const, 6)
            pool.nop(nofuse=True)
            for par in range(2):
                pool.dma_start(table[N:N + 1, par * (ROW // 2):(par + 1) * (ROW // 2)],
                               pad_row[0:1, 0:ROW // 2]).then_inc(tab_out[par], 16)

            def inverse_stds(g):
                pool.wait_ge(v_var, g + 1)
                pool.nop(nofuse=True)
                pool.tensor_tensor(rs[:, :], ve[:, :], minus_half[:, :], ALU.pow).then_inc(pl_rs, 1)

            inverse_stds(0)
            for i, done in enumerate(sc_out + gat_more):
                part = NULL_ROW + i * (P // 4)
                pool.dma_start(region[part:part + P // 4, :], pad_row[0:P // 4, :]).then_inc(done, 16)
            pool.memset(G[1][:, :, :], 0.0).then_inc(consts, 1)
            last_row = pool.to_reg(N - 1)
            mean_row = pool.to_reg(N)
            last_region_row = pool.to_reg(NULL_ROW - 1)

            def group(g, par, i, behind, ahead):
                if ahead:
                    inverse_stds(g + 1)
                pool.wait_ge(v_wh, g * GROUP + GROUP + 2)
                pool.nop(nofuse=True)
                pool.dma_start(table[bass.ds(g * GROUP * P, GROUP * P), :].rearrange("(r p) d -> p r d", p=P),
                               table_rows_sb[par][:, :, :]).then_inc(tab_out[par], 16)
            groups(pool, group)
            pool.wait_ge(v_wh, NS + 2 + 1)
            pool.nop(nofuse=True)
            pool.dma_start(table[N:N + 1, :], mean_sb[:, :]).then_inc(mean_out, 16)
            pool.wait_ge(consts, 15)
            pool.nop(nofuse=True)
            pool.wait_ge(v_s, LAG)
            pool.nop(nofuse=True)
            pool.wait_ge(tab_out[0], 16 + 8 * LAG)
            pool.nop(nofuse=True)
            pool.wait_ge(tab_out[1], 16 + 8 * LAG)
            pool.nop(nofuse=True)
            pool.wait_ge(mean_out, 16)
            pool.nop(nofuse=True)

            def gather(par, k0, k1, done):
                for k in range(k0, k1):
                    pool.indirect_dma_start(
                        out=G[par][:, k, :], out_offset=None, in_=table[:, :],
                        in_offset=bass.IndirectOffsetOnAxis(ap=idx[par][:, k:k + 1], axis=0),
                        bounds_check=mean_row if k == 0 else last_row, oob_is_err=False).then_inc(done[par], 16)

            def gather_more(u, par):
                pool.wait_ge(gates, u + 1)
                pool.nop(nofuse=True)
                above_all = pool.value_load(gate[0:1, bass.ds(u, 1), 0:1], min_val=0, max_val=1)
                with pool.If(above_all > 0):
                    gather(par, K_ALL, K_MID, gat_more)
                    above_mid = pool.value_load(gate[0:1, bass.ds(u, 1), 1:2], min_val=0, max_val=1)
                    with pool.If(above_mid > 0):
                        gather(par, K_MID, K, gat_more)

            def gather_waits(u, par):
                pool.wait_ge(v_idx, u + 1)
                pool.nop(nofuse=True)
                pool.wait_ge(pe_o, u + 1)
                pool.nop(nofuse=True)

            def inverse_std(w, par):
                pool.wait_ge(v_post, w * VP + 2 * VP + 6)
                pool.nop(nofuse=True)
                pool.tensor_tensor(x1[par][:, D + 1:D + 2], ve2[:, :], minus_half[:, 0:1], ALU.pow).then_inc(pl_rs2, 1)

            def scatter(w, par):
                pool.wait_ge(v_place, w * VE + VE + VE)
                pool.nop(nofuse=True)
                pool.indirect_dma_start(
                    out=region[:, :], out_offset=bass.IndirectOffsetOnAxis(ap=posu[par][:, 0:1], axis=0),
                    in_=x1[par][:, :], in_offset=None, bounds_check=last_region_row, oob_is_err=False
                ).then_inc(sc_out[par], 16)

            gather_waits(0, 0)
            gather(0, 0, K_ALL, gat)
            gather_more(0, 0)

            def step(u, par, do):
                if do.post and not do.search:
                    inverse_std(u - 2, par)
                if do.fetch:
                    gather_waits(u + 1, 1 - par)
                    gather(1 - par, 0, 2, gat)
                if do.post and do.search:
                    inverse_std(u - 2, par)
                if do.fetch:
                    gather(1 - par, 2, 5, gat)
                if do.place:
                    scatter(u - 3, 1 - par)
                if do.fetch:
                    gather(1 - par, 5, K_ALL, gat)
                    gather_more(u + 1, 1 - par)
            rounds(pool, step)

            pool.wait_ge(v_flag, 5)
            pool.nop(nofuse=True)
            flag = pool.value_load(flag_i[0:1, 0:1], min_val=0, max_val=4 * P)
            with pool.If(flag > 0):
                def dense(t, par):
                    inverse_std(t + NS, par)
                    scatter(t + NS, par)
                dense_strips(pool, dense)

            pad_experts(pool, 20, E, pad_out_pool)

            def store_block(b, r, turn):
                pool.wait_ge(v_y, b + 1 + RING)
                pool.nop(nofuse=True)
                pool.indirect_dma_start(
                    out=out[:, :], out_offset=bass.IndirectOffsetOnAxis(ap=tok[r % 2][:, 0:1], axis=0),
                    in_=yb[r % 2][:, :], in_offset=None, bounds_check=last_row, oob_is_err=False
                ).then_inc(y_out[r % 2], 16)
            steps = blocks_loop(pool, [(store_block, TAIL)])
            with pool.If(steps > TURNS * RING):
                pool.wait_ge(y_out[0], 16 * ((BLOCKS + 1) // 2))
                pool.nop(nofuse=True)
                pool.wait_ge(y_out[1], 16 * (BLOCKS // 2))
                pool.nop(nofuse=True)
            with pool.If(steps < TURNS * RING + 1):
                for par in range(2):
                    rows_out = pool.value_load(steps_i[0:1, 1 + par:2 + par], min_val=16, max_val=16 * BLOCKS)
                    pool.wait_ge(y_out[par], rows_out)
                    pool.nop(nofuse=True)

        @block.scalar
        def _(act):
            with nc.allow_non_contiguous_dma(reason="two small vectors"):
                act.dma_start(a_sb[:, :, 0:1], ga[D:2 * D, :].rearrange("(h p) o -> p h o", p=P)).then_inc(const_in, 16)
                act.dma_start(a_sb[:, :, 1:2], ga[0:D, :].rearrange("(h p) o -> p h o", p=P)).then_inc(const_in, 16)
            act.dma_start(rw_sb[:, :], rw[:, :]).then_inc(const_in, 16)
            act.dma_start(rb_sb[:, :], rb.rearrange("(o n) -> o n", o=1)).then_inc(const_in, 16)
            act.sem_inc(a_xT, 4)
            act.sem_inc(a_sg, Q)
            act.sem_inc(a_h, 2)
            act.sem_inc(a_x2, 1)
            act.wait_ge(v_const, 7)

            def transposes(s, r):
                act.wait_ge(pe_xT, s + 1 + 2)
                act.wait_ge(pe_wh, s + 1)
                act.nop(nofuse=True)
                for h in range(DH):
                    act.activation(xT[r % 2][:, h, :], psXn[r % 2][:, h * P:(h + 1) * P], ACT.Copy,
                                   accum_out=xsum[:, h, bass.ds(s, 1)]).then_inc(a_xT, 1)

            def signs(t, par, q):
                act.wait_ge(raw_in[q], t * 16 + 16)
                act.wait_ge(v_find, t * Q + q + 1)
                act.nop(nofuse=True)
                act.activation(sg[par][q][:, :], raw[q], ACT.Sign, bias=minus_half[:, 0:1],
                               saturate=False).then_inc(a_sg, 1)

            def group(g, par, i, behind, ahead):
                for r in range(GROUP):
                    transposes(g * GROUP + r, r)
                    if r % 2 == 0:
                        signs(g, par, r // 2)
            groups(act, group)

            def attention_sum(w, par):
                act.wait_ge(pe_o, w + 3)
                act.wait_ge(v_post, w * VP + 2 * VP)
                act.activation(hh[:, :], psO[par][:, 0:D], ACT.Copy, scale=rden[par][:, 0:1]).then_inc(a_h, 1)

            def elu_exp(w):
                act.wait_ge(v_post, w * VP + 2 * VP + 1)
                act.activation(ex[:, :], um[:, :], ACT.Exp).then_inc(a_ex, 1)

            def transposes2(w):
                act.wait_ge(pe_t2, w + 1)
                act.wait_ge(pe_lg, w + 1)
                act.activation(xT2[:, :, :].rearrange("p h n -> p (h n)"), psT[:, 0:D], ACT.Copy).then_inc(a_x2, 1)

            def softmax_exp(u):
                act.wait_ge(v_sm, u * VS + VS)
                act.activation(pr[:, :], ee[:, :], ACT.Exp, bias=nmx[:, 0:1], accum_out=den[:, 0:1]).then_inc(a_p, 1)

            for q in range(Q):
                signs(LAG, 0, q)

            def step(u, par, do):
                if do.ahead:
                    signs(u + LAG + 1, 1 - par, 0)
                if do.post:
                    attention_sum(u - 2, par)
                if do.ahead:
                    signs(u + LAG + 1, 1 - par, 1)
                if do.post:
                    elu_exp(u - 2)
                if do.ahead:
                    signs(u + LAG + 1, 1 - par, 2)
                    signs(u + LAG + 1, 1 - par, 3)
                if do.post:
                    transposes2(u - 2)
                if do.attend:
                    softmax_exp(u)
            rounds(act, step)

            act.wait_ge(v_flag, 5)
            flag = act.value_load(flag_i[0:1, 0:1], min_val=0, max_val=4 * P)
            with act.If(flag > 0):
                def dense(t, par):
                    with act.Fori(0, NS) as b:
                        act.wait_ge(d_v, t * DV_STRIP + NS * DV_A + 2 + b * 2 + 1)
                        act.activation(diag[:, 1, :], scores[:, bass.ds(b * P, P)], ACT.Exp, bias=nmx[:, 0:1],
                                       accum_out=dsum[:, bass.ds(b, 1)]).then_inc(d_a, 1)
                    act.wait_ge(d_v, (t + 1) * DV_STRIP + 1)
                    act.wait_ge(v_post, (t + NS) * VP + 2 * VP)
                    act.activation(hh[:, :], dacc[:, :], ACT.Copy, scale=rden[0][:, 0:1]).then_inc(a_h, 1)
                    elu_exp(t + NS)
                    transposes2(t + NS)
                dense_strips(act, dense)

            pad_experts(act, 10, 20, pad_out)

            def copy_xT(b, r, turn):
                act.wait_ge(pe_xb, b + 1)
                act.activation(xTb[r % 2][:, :, :].rearrange("p h n -> p (h n)"), psX[r % 2][:, 0:D],
                               ACT.Copy).then_inc(a_xb, 1)

            def copy_w1(b, r, turn):
                e = act.value_load(plan_i[0:1, bass.ds(b + P, 1)], min_val=0, max_val=E - 1)
                if not isinstance(b, int) or b >= 2:
                    act.wait_ge(a_hT, b - 1)
                act.activation(b1_b[r % 2][:, :], b1_t[:, bass.ds(e, 1)], ACT.Copy)
                act.activation(w1_b[r % 2][:, :, :].rearrange("p h n -> p (h n)"),
                               w1_sb[:, bass.ds(e, 1), :, :].rearrange("p o h n -> p (o h n)"), ACT.Copy).then_inc(a_w1, 1)

            def hidden(b, r, turn):
                act.wait_ge(pe_h, b + 1)
                act.wait_ge(a_w1, b + 1)
                act.activation(hT[r % 2][0:H, :], psH[r % 2][0:H, 0:P], ACT.Relu, bias=b1_b[r % 2][:, :]).then_inc(a_hT, 1)
            act.wait_ge(ffn_in, 16 * 8)
            act.wait_ge(v_plan, PLAN_STEPS)
            blocks_loop(act, [(copy_xT, 1), (hidden, 2), (copy_w1, 0)])

        @block.vector
        def _(v):
            v.sem_inc(v_wh, 2)
            v.sem_inc(v_xn, 2 * GROUP)
            v.sem_inc(v_find, 2 * Q)
            v.sem_inc(v_post, 2 * VP)
            v.sem_inc(v_place, VE)
            v.sem_inc(v_y, RING)
            for r in range(KEPT):
                v.memset(byte_sign[:, :, r], _int32(0x80 << (8 * r))).then_inc(v_const, 1)
            v.memset(most_words[:, :], NONE_WORD).then_inc(v_const, 1)
            v.memset(pad_row[:, 0:D + 2], 0.0)
            v.memset(pad_row[:, D + 2:ROW], NO_TOKEN)
            v.memset(pen[:, :], 0.0)
            v.memset(mean_sb[:, :], 0.0)
            for par in range(2):
                v.memset(x1[par][:, :], 0.0)
                v.memset(hT[par][:, :], 1.0)
            v.memset(more_sum[0][:, :], 16.0).then_inc(v_const, 1)
            v.wait_ge(consts, 14)
            v.tensor_copy(count[:, :], region_base[:, :]).then_inc(v_const, 1)

            for h in range(DH):
                v.wait_ge(pe_w, h + 1)
                v.tensor_copy(w_t[:, h, :], psT[:, 0:D]).then_inc(v_w, 1)
            for h in range(DH):
                v.tensor_copy(w_aug[:, h, 0:D], w_raw[:, h, :]).then_inc(v_w, 1)
            for h in range(DH):
                v.wait_ge(pe_w, DH + 1)
                v.tensor_copy(w_aug[:, h, D:D + 2], psL[:, 2 * h:2 * h + 2]).then_inc(v_w, 1)
            v.wait_ge(pe_w, DH + 2)
            v.tensor_copy(rw_t[:, :, :], psC[:, 0:DH * E].rearrange("p (h e) -> p h e", h=DH)).then_inc(v_w, 1)

            def search(t, par, q):
                v.wait_ge(a_sg, t * Q + q + 1 + Q)
                v.nop(nofuse=True)
                words = sg[par][q][:, :].bitcast(f32)
                v.max(top_word[:, q, :], words).then_inc(v_top, 1)

            def find(t, par, q):
                words = sg[par][q][:, :].bitcast(f32)
                v.wait_ge(v_top, t * Q + q + 1)
                v.nop(nofuse=True)
                v.max_index(top_pos[:, q, :], top_word[:, q, :], words).then_inc(v_find, 1)

            def decode_words(t):
                v.wait_ge(v_find, t * Q + Q + 2 * Q)
                v.tensor_tensor(bits[:, :, :],
                                top_word[:, :, :].rearrange("p q n -> p (q n)").bitcast(i32).unsqueeze(2).to_broadcast([P, Q * TOP, KEPT]),
                                byte_sign[:, :, :], ALU.bitwise_and).then_inc(v_dec, 1)
                v.scalar_tensor_tensor(out=code[:, :].rearrange("p (n r) -> p n r", r=KEPT),
                                       in0=top_pos[:, :, :].rearrange("p q n -> p (q n)").unsqueeze(2).to_broadcast([P, Q * TOP, KEPT]),
                                       scalar=-float(KEPT),
                                       in1=code_base[:, :, :, :].rearrange("p q n r -> p (q n) r"),
                                       op0=ALU.mult, op1=ALU.add).then_inc(v_dec, 1)
                v.tensor_tensor(most_words[:, :], most_words[:, :], top_word[:, :, TOP - 1], ALU.max).then_inc(v_dec, 1)

            def decode_keys(t):
                at = t * VD
                v.wait_ge(v_dec, at + 3)
                v.scalar_tensor_tensor(out=key[:, :], in0=bits[:, :, :].rearrange("p n r -> p (n r)"), scalar=0.0,
                                       in1=code[:, :], op0=ALU.is_equal, op1=ALU.mult).then_inc(v_dec, 1)

            def decode_first(t):
                at = t * VD
                v.wait_ge(v_dec, at + 4)
                v.nop(nofuse=True)
                v.max(key16[:, 0:TOP], key[:, :]).then_inc(v_dec, 1)

            def decode_rest(t):
                at = t * VD
                v.wait_ge(v_dec, at + 5)
                v.nop(nofuse=True)
                v.match_replace(key2[:, :], key16[:, 0:TOP], key[:, :], 0.0).then_inc(v_dec, 1)

            def decode_second(t):
                at = t * VD
                v.wait_ge(v_dec, at + 6)
                v.nop(nofuse=True)
                v.max(key16[:, TOP:K], key2[:, :]).then_inc(v_dec, 1)

            def decode_keep(t):
                at = t * VD
                v.wait_ge(v_dec, at + 7)
                v.tensor_copy(keys[:, bass.ds(t, 1), :], key16[:, :].unsqueeze(1)).then_inc(v_dec, 1)

            def gate_flags(t):
                v.wait_ge(v_dec, (t + 1) * VD + VD)
                v.tensor_scalar(many[:, :, :], keys[:, bass.ds(t, 2), K_ALL:K_MID + 1:K_MID - K_ALL], 0.0, None,
                                ALU.is_gt).then_inc(v_gs, 1)

            def set_gates(t, bank):
                at = t * 2
                v.wait_ge(pe_gate, t + 2)
                v.tensor_scalar(more[:, :, :].rearrange("p t k -> p (t k)"), bank[0:1, 0:4], 0.0, None,
                                ALU.is_gt).then_inc(v_gs, 1)
                v.wait_ge(v_gs, at + 2)
                v.tensor_copy(gate[:, bass.ds(t, 2), 0:2], more[:, :, :])
                v.scalar_tensor_tensor(out=more_sum[1][:, :], in0=more[:, :, 0], scalar=16.0 * (K_MID - K_ALL),
                                       in1=more_sum[0][:, :], op0=ALU.mult, op1=ALU.add).then_inc(v_gs, 1)
                v.wait_ge(v_gs, at + 3)
                v.scalar_tensor_tensor(out=more_sum[0][:, :], in0=more[:, :, 1], scalar=16.0 * (K - K_MID),
                                       in1=more_sum[1][:, :], op0=ALU.mult, op1=ALU.add).then_inc(v_gs, 1)
                v.wait_ge(v_gs, at + 4)
                v.tensor_copy(gate[:, bass.ds(t, 2), 2:3].rearrange("p t o -> p (t o)"), more_sum[0][:, :]).then_inc(gates, 2)

            def group_stats(g, par, i, r):
                if r == 0:
                    v.wait_ge(xg_in[par], i * 16 + 16)
                    v.nop(nofuse=True)
                v.bn_stats(st[:, r, :], xg[par][:, r, :]).then_inc(v_st, 1)

            def group_variances(g):
                v.wait_ge(v_st, g * 2 * GROUP + GROUP)
                v.nop(nofuse=True)
                for r in range(GROUP):
                    v.bn_aggr(mv[:, r, :], st[:, r, :]).then_inc(v_st, 1)
                v.wait_ge(v_st, g * 2 * GROUP + 2 * GROUP)
                v.tensor_scalar(ve[:, :], mv[:, :, 1], EPS, None, ALU.add).then_inc(v_var, 1)

            def normalise(g, par, r):
                s = g * GROUP + r
                if r == 0:
                    v.wait_ge(pl_rs, g + 1)
                v.wait_ge(pe_xT, s + 1)
                v.tensor_scalar(xn[r % 2][:, :], xg[par][:, r, :], mv[:, r, 0:1], rs[:, r:r + 1],
                                ALU.subtract, ALU.mult).then_inc(v_xn, 1)

            def table_rows(g, par, i, r):
                v.wait_ge(pe_wh, g * GROUP + r + 1 + 2)
                if r == 0:
                    v.wait_ge(tab_out[par], i * 16 + 16)
                v.tensor_copy(table_rows_sb[par][:, r, 0:D + 2], psW[r % 2][:, 0:D + 2]).then_inc(v_wh, 1)

            def prepare(g, par, i, behind, ahead):
                next_i = i if par == 0 else i + 1
                for r in range(GROUP):
                    normalise(g, par, r)
                    if behind and r == 0:
                        decode_words(g - 1)
                        decode_keys(g - 1)
                    if behind and r == 1:
                        decode_first(g - 1)
                    if behind and r == 2:
                        decode_rest(g - 1)
                    if behind and r == 3:
                        decode_second(g - 1)
                    if behind and r == 4:
                        decode_keep(g - 1)
                    if behind and par == 0 and r == 5:
                        gate_flags(g - 2)
                    if behind and par == 0 and r == 7:
                        set_gates(g - 2, psC)
                    if r >= 2:
                        table_rows(g, par, i, r - 2)
                        if r % 2 == 0:
                            search(g, par, r // 2 - 1)
                        else:
                            find(g, par, r // 2 - 1)
                    if ahead and r >= GROUP // 2:
                        for k in range(2):
                            group_stats(g + 1, 1 - par, next_i, (r - GROUP // 2) * 2 + k)
                if ahead:
                    group_variances(g + 1)
                table_rows(g, par, i, GROUP - 2)
                search(g, par, Q - 1)
                table_rows(g, par, i, GROUP - 1)
                find(g, par, Q - 1)
                v.wait_ge(v_wh, g * GROUP + GROUP + 2)
                v.tensor_copy(s2[:, bass.ds(g * GROUP, GROUP)], table_rows_sb[par][:, :, D])
                v.tensor_copy(s1[:, bass.ds(g * GROUP, GROUP)], table_rows_sb[par][:, :, D + 1]).then_inc(v_s, 1)
            for r in range(GROUP):
                group_stats(0, 0, 0, r)
            group_variances(0)
            v.memset(G[0][:, :, :], 0.0)
            groups(v, prepare)
            decode_words(LAG - 1)
            decode_keys(LAG - 1)
            v.wait_ge(a_xT, 2 * NS + 4)
            v.tensor_reduce(xmean[:, :], xsum[:, :, :], AX.X, ALU.add).then_inc(v_w, 1)
            v.wait_ge(v_w, 3 * DH + 2)
            v.tensor_scalar(xmean[:, :], xmean[:, :], 1.0 / N, None, ALU.mult).then_inc(v_w, 1)
            decode_first(LAG - 1)
            decode_rest(LAG - 1)
            decode_second(LAG - 1)
            v.wait_ge(pe_w, DH + 3)
            v.tensor_copy(mean_sb[:, 0:D + 1], psW[0][0:1, 0:D + 1]).then_inc(v_wh, 1)
            v.wait_ge(v_s, LAG)
            decode_keep(LAG - 1)
            gate_flags(LAG - 2)
            set_gates(LAG - 2, psC)

            def indices(u, par):
                v.wait_ge(v_dec, u * VD + VD)
                v.tensor_scalar(idx[par][:, :], keys[:, bass.ds(u, 1), :].rearrange("p o k -> p (o k)"), -1.0, float(N),
                                ALU.mult, ALU.add).then_inc(v_idx, 1)

            def penalties(u):
                v.tensor_scalar(pen[:, 1:K], keys[:, bass.ds(u, 1), 1:K].rearrange("p o k -> p (o k)"), 0.0,
                                MASK_VAL / ALPHA, ALU.is_equal, ALU.mult).then_inc(v_sm, 1)

            def load_gates(u):
                v.wait_ge(gates, u + 1)
                v.nop(nofuse=True)
                more_done = v.value_load(gate[0:1, bass.ds(u, 1), 2:3], min_val=16, max_val=16 + 16 * (K - K_ALL) * NS // 2)
                above_all = v.value_load(gate[0:1, bass.ds(u, 1), 0:1], min_val=0, max_val=1)
                return more_done, above_all

            def softmax(u, par, i16, more_done, above_all):
                at = u * VS
                v.wait_ge(v_sm, at + 1)
                v.wait_ge(gat_more[par], more_done)
                v.nop(nofuse=True)
                v.wait_ge(gat[par], i16)
                v.scalar_tensor_tensor(out=sc[:, :], in0=G[par][:, :, D], scalar=s1[:, bass.ds(u, 1)], in1=pen[:, :],
                                       op0=ALU.add, op1=ALU.add).then_inc(v_sm, 1)
                v.wait_ge(v_sm, at + 2)
                v.scalar_tensor_tensor(out=ee[:, :], in0=sc[:, :], scalar=ALPHA, in1=sc[:, :],
                                       op0=ALU.mult, op1=ALU.max).then_inc(v_sm, 1)
                v.wait_ge(v_sm, at + 3)
                v.tensor_reduce(nmx[:, :], ee[:, :], AX.X, ALU.max, negate=True).then_inc(v_sm, 1)
                v.wait_ge(a_p, u + 1)
                v.reciprocal(rden[par][:, :], den[:, :])
                v.wait_ge(pe_o, u + 2)
                v.nop(nofuse=True)

                def diagonals(k0, k1):
                    return v.tensor_tensor(diag[:, k0:k1, :], ident[:, :].unsqueeze(1).to_broadcast([P, k1 - k0, P]),
                                           pr[:, k0:k1].unsqueeze(2).to_broadcast([P, k1 - k0, P]), ALU.mult)
                with v.If(above_all > 0):
                    diagonals(K_ALL, K)
                diagonals(0, K_ALL).then_inc(v_diag, 1)

            def post_min(w):
                v.wait_ge(a_h, w + 3)
                v.tensor_scalar(um[:, :], hh[:, :], 0.0, None, ALU.min).then_inc(v_post, 1)

            def post_elu(w):
                v.wait_ge(a_ex, w + 1)
                v.scalar_tensor_tensor(out=el[:, :], in0=ex[:, :], scalar=-1.0, in1=hh[:, :],
                                       op0=ALU.add, op1=ALU.max).then_inc(v_post, 1)

            def post_x1(w, par, i16):
                v.wait_ge(v_post, w * VP + 2 * VP + 2)
                v.wait_ge(xr_in[par], i16)
                v.wait_ge(sc_out[par], i16)
                v.tensor_tensor(x1[par][:, 0:D], el[:, :], xr[par][:, :], ALU.add).then_inc(v_post, 1)

            def post_stats(w, par):
                v.wait_ge(v_post, w * VP + 2 * VP + 3)
                v.bn_stats(st2[:, :], x1[par][:, 0:D]).then_inc(v_post, 1)

            def post_mean(w, par):
                v.wait_ge(v_post, w * VP + 2 * VP + 4)
                v.nop(nofuse=True)
                v.bn_aggr(x1[par][:, D:D + 2], st2[:, :]).then_inc(v_post, 1)

            def post_variance(w, par, strip):
                v.wait_ge(v_post, w * VP + 2 * VP + 5)
                v.tensor_scalar(ve2[:, :], x1[par][:, D + 1:D + 2], EPS, None, ALU.add).then_inc(v_post, 1)
                v.tensor_copy(x1[par][:, D + 2:D + 3], token_no[:, bass.ds(strip, 1)]).then_inc(v_post, 1)

            def post_norm(w, par):
                v.wait_ge(pl_rs2, w + 1)
                v.tensor_scalar(xn2[:, :], x1[par][:, 0:D], x1[par][:, D:D + 1], x1[par][:, D + 1:D + 2],
                                ALU.subtract, ALU.mult).then_inc(v_post, 1)

            def place_logits(w):
                v.wait_ge(pe_lg, w + 2)
                v.tensor_copy(lg[:, :], psL[:, 0:E]).then_inc(v_place, 1)

            def place_best(w):
                v.wait_ge(v_place, w * VE + VE + 1)
                v.nop(nofuse=True)
                v.max(lmax[:, :], lg[:, :]).then_inc(v_place, 1)

            def place_argmax(w):
                v.wait_ge(v_place, w * VE + VE + 2)
                v.nop(nofuse=True)
                v.max_index(lidx[:, :], lmax[:, :], lg[:, :]).then_inc(v_place, 1)

            def place_expert(w):
                v.wait_ge(v_place, w * VE + VE + 3)
                v.tensor_copy(ef[:, :], lidx[:, 0:1]).then_inc(v_place, 1)

            def place_one_hot(w):
                v.wait_ge(v_place, w * VE + VE + 4)
                v.scalar_tensor_tensor(out=oh[:, :], in0=expert_no[:, :], scalar=ef[:, 0:1], in1=direction[:, :],
                                       op0=ALU.is_equal, op1=ALU.mult).then_inc(v_place, 1)

            def place_ranks(w):
                v.wait_ge(pe_cum, w + 1)
                v.tensor_tensor(c2[:, :], psC[:, 0:E], count[:, :], ALU.add).then_inc(v_place, 1)
                v.tensor_tensor(count[:, :], psC[:, E:2 * E], count[:, :], ALU.add).then_inc(v_place, 1)

            def place_pick(w):
                v.wait_ge(v_place, w * VE + VE + 7)
                v.tensor_tensor_reduce(out=c3[:, :], in0=c2[:, :], in1=oh[:, :], scale=1.0, scalar=0.0,
                                       op0=ALU.mult, op1=ALU.add, accum_out=posf[:, :]).then_inc(v_place, 1)

            def place_position(w, par):
                v.wait_ge(v_place, w * VE + VE + 8)
                v.scalar_tensor_tensor(out=posu[par][:, :], in0=posf[:, :], scalar=-1.0, in1=posf[:, :],
                                       op0=ALU.mult, op1=ALU.max).then_inc(v_place, 1)

            indices(0, 0)

            def post_all(w, par, i16, strip):
                post_min(w)
                post_elu(w)
                post_x1(w, par, i16)
                post_stats(w, par)
                post_mean(w, par)
                post_variance(w, par, strip)
                post_norm(w, par)
                place_logits(w)
                place_best(w)
                place_argmax(w)
                place_expert(w)
                place_one_hot(w)
                place_ranks(w)
                place_pick(w)
                place_position(w, par)

            def half_up(u, par):
                return (u - par) * 8 + 16

            def step(u, par, do):
                t, w, y = u + LAG, u - 2, u - 3
                if do.fetch:
                    indices(u + 1, 1 - par)
                if do.attend:
                    penalties(u)
                if do.place:
                    place_logits(y)
                    place_best(y)
                if do.search:
                    search(t, par, 0)
                if do.place:
                    place_argmax(y)
                if do.search:
                    find(t, par, 0)
                if do.place:
                    place_expert(y)
                if do.search:
                    search(t, par, 1)
                if do.place:
                    place_one_hot(y)
                if do.search:
                    find(t, par, 1)
                if do.attend:
                    more_done, above_all = load_gates(u)
                if do.post:
                    post_min(w)
                if do.search:
                    search(t, par, 2)
                if do.post:
                    post_elu(w)
                if do.search:
                    find(t, par, 2)
                if do.post:
                    post_x1(w, par, half_up(w, par))
                if do.search:
                    search(t, par, 3)
                if do.post:
                    post_stats(w, par)
                if do.search:
                    find(t, par, 3)
                if do.post:
                    post_mean(w, par)
                if do.search:
                    decode_words(t)
                if do.post:
                    post_variance(w, par, w)
                if do.search:
                    decode_keys(t)
                if do.place:
                    place_ranks(y)
                if do.search:
                    decode_first(t)
                if do.place:
                    place_pick(y)
                if do.search:
                    decode_rest(t)
                if do.place:
                    place_position(y, 1 - par)
                if do.search:
                    decode_second(t)
                    decode_keep(t)
                if do.search and par:
                    gate_flags(t - 1)
                if do.post:
                    post_norm(w, par)
                if do.search and par:
                    set_gates(t - 1, psP)
                if do.attend:
                    softmax(u, par, half_up(u, par) * K_ALL, more_done, above_all)
            rounds(v, step)

            v.tensor_reduce(mx[:, :], keys[:, :, K - 1], AX.X, ALU.max).then_inc(v_flag, 1)
            v.tensor_reduce(nmx[:, :], most_words[:, :], AX.X, ALU.max).then_inc(v_flag, 1)
            v.wait_ge(v_flag, 2)
            v.tensor_scalar(flagc[:, 0:1], mx[:, :], 0.0, None, ALU.is_gt).then_inc(v_flag, 1)
            v.tensor_scalar(flagc[:, 1:2], nmx[:, :], NONE_WORD, None, ALU.is_gt).then_inc(v_flag, 1)
            v.wait_ge(pe_flag, 1)
            v.tensor_copy(flag_i[0:1, 0:1], psL[0:1, 0:1]).then_inc(v_flag, 1)
            v.wait_ge(v_flag, 5)
            flag = v.value_load(flag_i[0:1, 0:1], min_val=0, max_val=4 * P)
            with v.If(flag > 0):
                v.wait_ge(v_place, NS * VE + VE)
                v.tensor_copy(count[:, :], region_base[:, :])
                v.engine_nop().then_inc(d_v, 1)

                def dense(t, par):
                    A = t * DV_STRIP + 1
                    with v.Fori(0, NS) as b:
                        at = A + b * DV_A
                        v.tensor_scalar(diag[:, 0, :], ident[:, :], s2[:, bass.ds(b, 1)], None, ALU.mult).then_inc(d_v, 1)
                        v.wait_ge(d_in, (t * NS + b) * 16 + 16)
                        v.tensor_scalar(diag[:, 2, :], adj_block[:, :], 0.0, None, ALU.is_gt).then_inc(d_v, 1)
                        v.wait_ge(d_v, at + 2)
                        v.wait_ge(d_pe, t * 3 * NS + b + 1)
                        v.tensor_scalar(diag[:, 3, :], psC[:, 0:P], s1[:, bass.ds(t, 1)], None, ALU.add).then_inc(d_v, 1)
                        v.tensor_scalar(diag[:, 4, :], diag[:, 2, :], -1.0, -MASK_VAL, ALU.add, ALU.mult).then_inc(d_v, 1)
                        v.wait_ge(d_v, at + 4)
                        v.scalar_tensor_tensor(out=diag[:, 5, :], in0=diag[:, 3, :], scalar=ALPHA, in1=diag[:, 3, :],
                                               op0=ALU.mult, op1=ALU.max).then_inc(d_v, 1)
                        v.wait_ge(d_v, at + 5)
                        v.tensor_tensor(diag[:, 6, :], diag[:, 5, :], diag[:, 2, :], ALU.mult).then_inc(d_v, 1)
                        v.wait_ge(d_v, at + 6)
                        v.tensor_tensor(scores[:, bass.ds(b * P, P)], diag[:, 6, :], diag[:, 4, :], ALU.add).then_inc(d_v, 1)
                        v.wait_ge(d_v, at + 7)
                    at = A + NS * DV_A
                    v.tensor_reduce(mx[:, :], scores[:, :], AX.X, ALU.max).then_inc(d_v, 1)
                    v.wait_ge(d_v, at + 1)
                    v.tensor_scalar(nmx[:, :], mx[:, :], -1.0, None, ALU.mult)
                    v.memset(dacc[:, :], 0.0).then_inc(d_v, 1)
                    with v.Fori(0, NS) as b:
                        v.wait_ge(d_pe, t * 3 * NS + NS + b * 2 + 1)
                        v.tensor_copy(diag[:, 7, :], psT[:, 0:P]).then_inc(d_v, 1)
                        v.wait_ge(d_pe, t * 3 * NS + NS + b * 2 + 2)
                        v.tensor_tensor(dacc[:, :], dacc[:, :], psO[0][:, 0:D], ALU.add).then_inc(d_v, 1)
                    v.wait_ge(d_v, at + 2 + 2 * NS)
                    v.tensor_reduce(den[:, :], dsum[:, :], AX.X, ALU.add)
                    v.drain()
                    v.reciprocal(rden[0][:, :], den[:, :]).then_inc(d_v, 1)
                    post_all(t + NS, par, half_up(t, par) + 8 * NS, t)
                dense_strips(v, dense)

            n = 0

            def planned(ins):
                nonlocal n
                n += 1
                ins.then_inc(v_plan, 1)
                return n

            v.wait_ge(v_plan, planned(v.tensor_tensor(cum[0][:, :], count[:, :], pad_shift[:, :], ALU.add)))
            v.wait_ge(v_plan, planned(v.tensor_copy(pad_i[:, :], cum[0][0:1, :])))
            assert n == PLAN_PADS
            v.wait_ge(v_plan, planned(v.tensor_tensor(nbf[:, :], count[:, :], region_base[:, :], ALU.subtract)))
            v.wait_ge(v_plan, planned(v.tensor_tensor(nbf[:, :], nbf[:, :], direction[:, :], ALU.mult)))
            v.wait_ge(v_plan, planned(v.tensor_scalar(nbi[:, :], nbf[:, :], float(P - 1), None, ALU.add)))
            v.wait_ge(v_plan, planned(v.tensor_scalar(nbj[:, :], nbi[:, :], 7, None, ALU.arith_shift_right)))
            v.wait_ge(v_plan, planned(v.tensor_copy(nbf[:, :], nbj[:, :])))
            v.wait_ge(v_plan, planned(v.tensor_copy(cum[0][:, :], nbj[:, :])))
            src = 0
            for shift in (1, 2, 4, 8, 16):
                v.wait_ge(v_plan, planned(v.tensor_copy(cum[1 - src][:, 0:shift], cum[src][:, 0:shift])))
                v.wait_ge(v_plan, planned(v.tensor_tensor(cum[1 - src][:, shift:E], cum[src][:, shift:E], cum[src][:, 0:E - shift],
                                        ALU.add)))
                src = 1 - src
            v.wait_ge(v_plan, planned(v.tensor_scalar(le[:, :], cum[src][:, :], part_no[:, 0:1], None, ALU.is_le)))
            v.wait_ge(v_plan, planned(v.tensor_reduce(plan[:, 0:1], le[:, :], AX.X, ALU.add)))

            def pick(col, row, of):
                v.wait_ge(v_plan, planned(v.tensor_tensor_reduce(out=le2[:, :], in0=row[:, :], in1=of[:, :], scale=1.0, scalar=0.0,
                                               op0=ALU.mult, op1=ALU.add, accum_out=plan[:, col:col + 1])))
            pick(1, le, nbf)
            v.wait_ge(v_plan, planned(v.tensor_scalar(plan[:, 2:3], plan[:, 1:2], part_no[:, 0:1], -float(P), ALU.subtract, ALU.mult)))
            v.wait_ge(v_plan, planned(v.tensor_scalar(le[:, :], expert_no[:, :], plan[:, 0:1], None, ALU.is_equal)))
            pick(3, le, direction)
            pick(4, le, first_block)
            v.wait_ge(v_plan, planned(v.tensor_scalar(plan[:, 5:6], plan[:, 0:1], float(E), float(NULL_ROW), ALU.is_ge, ALU.mult)))
            v.wait_ge(v_plan, planned(v.tensor_tensor(plan[:, 2:3], plan[:, 2:3], plan[:, 3:4], ALU.mult)))
            v.wait_ge(v_plan, planned(v.tensor_tensor(plan[:, 4:5], plan[:, 4:5], plan[:, 5:6], ALU.add)))
            v.wait_ge(v_plan, planned(v.tensor_tensor(plan[:, 6:7], plan[:, 2:3], plan[:, 4:5], ALU.add)))
            assert n == PLAN_ROWS
            v.wait_ge(v_plan, planned(v.tensor_scalar(steps_f[:, 0:1], cum[src][0:1, E - 1:E], float(TAIL), None, ALU.add)))
            v.wait_ge(v_plan, planned(v.tensor_scalar(turn_of[:, :], expert_no[0:1, :], float(RING), steps_f[:, 0:1],
                                                      ALU.mult, ALU.is_lt)))
            v.wait_ge(v_plan, planned(v.tensor_reduce(steps_f[:, 1:2], turn_of[:, 0:TURNS], AX.X, ALU.add)))
            v.wait_ge(v_plan, planned(v.tensor_copy(steps_i[:, 0:1], steps_f[:, 0:1])))
            for par in range(2):
                stored = (RING - TAIL + 1 - par) // 2
                v.wait_ge(v_plan, planned(v.tensor_scalar(steps_i[:, 1 + par:2 + par], steps_f[:, 1:2], 16.0 * RING / 2,
                                                          16.0 * (stored - RING // 2), ALU.mult, ALU.add)))
            v.wait_ge(pe_plan, 1)
            v.wait_ge(v_plan, planned(v.tensor_copy(plan_i[:, 0:P], psC[0:1, 0:P])))
            v.wait_ge(v_plan, planned(v.tensor_scalar(plan_i[:, P:2 * P], psC[0:1, P:2 * P], float(E - 1), None, ALU.min)))
            assert n == PLAN_STEPS

            def block_norm(b, r, turn):
                v.wait_ge(xb_in[r], turn * 16 + 16)
                if not isinstance(b, int) or b >= 2:
                    v.wait_ge(pe_xb, b - 1)
                v.tensor_scalar(xnb[r % 2][:, :], xb[r][:, 0:D], xb[r][:, D:D + 1], xb[r][:, D + 1:D + 2],
                                ALU.subtract, ALU.mult).then_inc(v_xb, 1)

            def block_rows(b, r, turn):
                v.wait_ge(pe_y, b + 1)
                if not isinstance(b, int) or b > 1:
                    v.wait_ge(y_out[r % 2], (b - r % 2) * 8)
                v.tensor_copy(tok[r % 2][:, :], xb[r][:, D + 2:D + 3])
                v.scalar_tensor_tensor(out=yb[r % 2][:, :], in0=psO[r % 2][:, 0:D], scalar=0.0, in1=xb[r][:, 0:D],
                                       op0=ALU.max, op1=ALU.add).then_inc(v_y, 1)
            def copy_w2(b, r, turn):
                e = v.value_load(plan_i[0:1, bass.ds(b + P, 1)], min_val=0, max_val=E - 1)
                v.tensor_copy(w2_b[r % 2][:, :], w2_sb[:, bass.ds(e, 1), :].rearrange("p o n -> p (o n)")).then_inc(v_w2, 1)
            v.wait_ge(ffn_in, 16 * 8)
            blocks_loop(v, [(copy_w2, 2), (block_norm, 0), (block_rows, 3)])

        @block.tensor
        def _(pe):
            pe.sem_inc(pe_xT, 2)
            pe.sem_inc(pe_wh, 2)
            pe.sem_inc(pe_o, 2)
            pe.sem_inc(pe_lg, 1)
            pe.wait_ge(const_in, 16 * 5)
            pe.wait_ge(consts, 14)
            pe.nop(nofuse=True)
            for fh in range(DH):
                if fh:
                    pe.wait_ge(v_w, fh)
                    pe.nop(nofuse=True)
                for kh in range(DH):
                    mm = pe.transpose(psT[:, kh * P:(kh + 1) * P], w_raw[:, kh, fh * P:(fh + 1) * P], ident[:, :])
                mm.then_inc(pe_w, 1)
            pe.wait_ge(v_w, DH)
            pe.nop(nofuse=True)
            for kh in range(DH):
                for fh in range(DH):
                    mm = pe.matmul(psL[:, 2 * kh:2 * kh + 2], w_t[:, fh, kh * P:(kh + 1) * P], a_sb[:, fh, :],
                                   start=(fh == 0), stop=(fh == DH - 1))
            mm.then_inc(pe_w, 1)
            for h in range(DH):
                mm = pe.transpose(psC[:, h * E:(h + 1) * E], rw_sb[:, h * P:(h + 1) * P], ident[0:E, 0:E])
            mm.then_inc(pe_w, 1)
            pe.wait_ge(v_w, 3 * DH)

            def transposes(s, r):
                pe.wait_ge(v_xn, s + 1 + 2 * GROUP)
                pe.wait_ge(a_xT, 2 * s + 2)
                pe.nop(nofuse=True)
                for h in range(DH):
                    mm = pe.transpose(psXn[r % 2][:, h * P:(h + 1) * P], xn[r % 2][:, h * P:(h + 1) * P], ident[:, :])
                mm.then_inc(pe_xT, 1)

            def table_rows(s, r):
                pe.wait_ge(a_xT, 2 * s + 6)
                pe.wait_ge(v_wh, s + 1)
                pe.nop(nofuse=True)
                for h in range(DH):
                    mm = pe.matmul(psW[r % 2][:, 0:D + 2], xT[r % 2][:, h, :], w_aug[:, h, :],
                                   start=(h == 0), stop=(h == DH - 1))
                mm.then_inc(pe_wh, 1)

            def gate_rows(t, bank):
                pe.wait_ge(v_gs, t * 2 + 1)
                pe.matmul(bank[0:1, 0:4], ones_b[:, 0:1], many[:, :, :].rearrange("p t k -> p (t k)"),
                          start=True, stop=True).then_inc(pe_gate, 2)

            def group(g, par, i, behind, ahead):
                for r in range(GROUP):
                    transposes(g * GROUP + r, r)
                    if behind and par == 0 and r == 6:
                        gate_rows(g - 2, psC)
                    if r:
                        table_rows(g * GROUP + r - 1, r - 1)
                table_rows(g * GROUP + GROUP - 1, GROUP - 1)
            groups(pe, group)
            pe.wait_ge(v_w, 3 * DH + 3)
            pe.wait_ge(v_wh, NS + 2)
            pe.nop(nofuse=True)
            for h in range(DH):
                mm = pe.matmul(psW[0][0:1, 0:D + 2], xmean[:, h:h + 1], w_aug[:, h, :],
                               start=(h == 0), stop=(h == DH - 1))
            mm.then_inc(pe_w, 1)
            gate_rows(LAG - 2, psC)

            def weighted_sum(u, par):
                pe.wait_ge(gates, u + 1)
                pe.nop(nofuse=True)
                above_all = pe.value_load(gate[0:1, bass.ds(u, 1), 0:1], min_val=0, max_val=1)
                pe.wait_ge(v_diag, u + 1)
                pe.wait_ge(a_h, u + 1)
                pe.nop(nofuse=True)

                def products(k0, k1):
                    for k in range(k0, k1):
                        mm = pe.matmul(psO[par][:, 0:D], diag[:, k, :], G[par][:, k, 0:D],
                                       start=(k == 0), stop=(k == K_ALL - 1))
                    return mm
                products(0, 1)
                with pe.If(above_all > 0):
                    products(K_ALL, K_MID)
                    above_mid = pe.value_load(gate[0:1, bass.ds(u, 1), 1:2], min_val=0, max_val=1)
                    with pe.If(above_mid > 0):
                        products(K_MID, K)
                products(1, K_ALL).then_inc(pe_o, 1)

            def post_transposes(w):
                pe.wait_ge(v_post, w * VP + 2 * VP + 8)
                pe.wait_ge(a_x2, w + 1)
                pe.nop(nofuse=True)
                for h in range(DH):
                    mm = pe.transpose(psT[:, h * P:(h + 1) * P], xn2[:, h * P:(h + 1) * P], ident[:, :])
                mm.then_inc(pe_t2, 1)

            def logits(w):
                pe.wait_ge(v_place, w * VE + 1)
                pe.wait_ge(a_x2, w + 2)
                pe.nop(nofuse=True)
                for h in range(DH):
                    pe.matmul(psL[:, 0:E], xT2[:, h, :], rw_t[:, h, :], start=(h == 0), stop=False)
                pe.matmul(psL[:, 0:E], ones_f[0:1, :], rb_sb[:, :], start=False, stop=True).then_inc(pe_lg, 1)

            def ranks(w):
                pe.wait_ge(v_place, w * VE + VE + 5)
                pe.matmul(psC[:, 0:E], before[:, :], oh[:, :], start=True, stop=True)
                pe.matmul(psC[:, E:2 * E], ones_b[:, :], oh[:, :], start=True, stop=True).then_inc(pe_cum, 1)

            pe.wait_ge(v_w, 3 * DH + 1)

            def step(u, par, do):
                if do.place:
                    ranks(u - 3)
                if do.search and par:
                    gate_rows(u - 1 + LAG, psP)
                if do.post:
                    post_transposes(u - 2)
                    logits(u - 2)
                if do.attend:
                    weighted_sum(u, par)
            rounds(pe, step)

            pe.wait_ge(v_flag, 4)
            pe.matmul(psL[0:1, 0:1], flagc[:, 0:1], ones_f[:, 0:1], start=True, stop=False)
            pe.matmul(psL[0:1, 0:1], flagc[:, 1:2], ones_f[:, 0:1], start=False, stop=True).then_inc(pe_flag, 1)
            pe.wait_ge(v_flag, 5)
            flag = pe.value_load(flag_i[0:1, 0:1], min_val=0, max_val=4 * P)
            with pe.If(flag > 0):
                def dense(t, par):
                    with pe.Fori(0, NS) as b:
                        pe.wait_ge(d_v, t * DV_STRIP + 1 + b * DV_A + 1)
                        pe.matmul(psC[:, 0:P], ones_f[:, :], diag[:, 0, :], start=True, stop=True).then_inc(d_pe, 1)
                    with pe.Fori(0, NS) as b:
                        pe.wait_ge(d_a, t * NS + b + 1)
                        pe.transpose(psT[:, 0:P], diag[:, 1, :], ident[:, :]).then_inc(d_pe, 1)
                        pe.wait_ge(d_v, t * DV_STRIP + 1 + NS * DV_A + 2 + 2 * b + 1)
                        pe.wait_ge(d_wh, (t * NS + b) * 16 + 16)
                        pe.matmul(psO[0][:, 0:D], diag[:, 7, :], G[0][:, 0, 0:D], start=True, stop=True).then_inc(d_pe, 1)
                    post_transposes(t + NS)
                    logits(t + NS)
                    ranks(t + NS)
                dense_strips(pe, dense)

            pe.wait_ge(v_plan, PLAN_ROWS)
            pe.nop(nofuse=True)
            for j, col in ((0, 6), (1, 0)):
                mm = pe.matmul(psC[0:1, j * P:(j + 1) * P], plan[:, col:col + 1], ident[:, :], start=True, stop=True)
            mm.then_inc(pe_plan, 1)
            def block_transposes(b, r, turn):
                pe.wait_ge(v_xb, b + 1)
                for h in range(DH):
                    mm = pe.transpose(psX[r % 2][:, h * P:(h + 1) * P], xnb[r % 2][:, h * P:(h + 1) * P], ident[:, :])
                mm.then_inc(pe_xb, 1)

            def block_hidden(b, r, turn):
                pe.wait_ge(a_xb, b + 1)
                for h in range(DH):
                    mm = pe.matmul(psH[r % 2][0:H, 0:P], w1_b[r % 2][:, h, :], xTb[r % 2][:, h, :],
                                   start=(h == 0), stop=(h == DH - 1))
                mm.then_inc(pe_h, 1)

            def block_output(b, r, turn):
                pe.wait_ge(a_hT, b + 1)
                if isinstance(b, int) and b + 2 >= BLOCKS:
                    pe.wait_ge(v_w2, b + 1)
                    pe.nop(nofuse=True)
                pe.matmul(psO[r % 2][:, 0:D], hT[r % 2][:, :], w2_b[r % 2][:, :],
                          start=True, stop=True).then_inc(pe_y, 1)
            blocks_loop(pe, [(block_transposes, 1), (block_hidden, 2), (block_output, 3)])


def _int32(bits):
    return bits - (1 << 32) if bits >> 31 else bits


def _word_of_signs(bits):
    import numpy as np
    return abs(float(np.array([bits], np.uint32).view(np.float32)[0]))


_INS = ["x", "adj", "L0_gnn_W", "L0_gnn_a", "L0_ffn_router_w", "L0_ffn_router_b",
        "L0_ffn_W1", "L0_ffn_b1", "L0_ffn_W2", "L0_ffn_b2"]


def kernel(**inputs):
    import numpy as np
    import concourse.bacc as bacc
    from concourse.bass_utils import run_bass_kernel_spmd as run

    nc = bacc.Bacc("TRN2", target_bir_lowering=False, num_devices=1)
    arrays, args = {}, []
    for name in _INS:
        a = np.ascontiguousarray(inputs[name])
        arrays[f"in_{name}"] = a
        args.append(nc.dram_tensor(f"in_{name}", a.shape, mybir.dt.from_np(a.dtype), kind="ExternalInput").ap())
    N = arrays["in_x"].shape[0]
    args.append(nc.dram_tensor("out_x", (N, D), mybir.dt.float32, kind="ExternalOutput").ap())
    args.append(nc.dram_tensor("wh_table", (N + 1, ROW), mybir.dt.float32, kind="Internal").ap())
    args.append(nc.dram_tensor("regions", (E // 2 * (N + 2 * P) + P, ROW), mybir.dt.float32, kind="Internal").ap())
    gat_moe(nc, *args)
    return run(nc, [arrays], core_ids=[0]).results[0]["out_x"]
```
